# Optimizing a Trainium2 kernel written in Bass

```python
import numpy as np
import jax
import jax.numpy as jnp

def _softmax(x, axis=-1):
    return jax.nn.softmax(x, axis=axis)

def _gelu(x):
    return jax.nn.gelu(x, approximate=True)

def _silu(x):
    return jax.nn.silu(x)

def _sigmoid(x):
    return jax.nn.sigmoid(x)

def _layernorm(x, axis=-1, eps=1e-05):
    m = jnp.mean(x, axis=axis, keepdims=True)
    v = jnp.var(x, axis=axis, keepdims=True)
    return (x - m) / jnp.sqrt(v + eps)

def _scatter_add(tgt, idx, src, axis=0):
    return tgt.at[idx].add(src)

def _segment_sum(src, seg, n):
    return jax.ops.segment_sum(src, seg, n)
kernel_name = 'mk_seq_postln_d4_jaxref_r8_151537'

def setup_inputs(seed: int=0):
    np.random.seed(seed)
    _w = jnp.asarray

    def _L0_attn_setup():
        import jax, jax.numpy as jnp
        import numpy as np
        DIM = 128
        HEADS = 16
        HDIM = DIM // HEADS
        CHUNK = 64
        RES_SCALE = float(1.0 / np.sqrt(2.0))
        EPS_FP32 = float(np.finfo(np.float32).eps)

        def _rms(x, eps):
            return x * jax.lax.rsqrt(jnp.mean(x * x, axis=-1, keepdims=True) + eps)

        def _mixer(x, in_proj_w, out_proj_w):
            B, S, D = x.shape
            proj = x @ in_proj_w.T
            q, k, v, a, g = jnp.split(proj, 5, axis=-1)
            rs = lambda t: t.reshape(B, S, HEADS, HDIM)
            q, k, v, a, g = map(rs, (q, k, v, a, g))
            q = _rms(q, EPS_FP32)
            k = jnp.tanh(k)
            a = jnp.clip(jax.nn.sigmoid(a + 2.0), 0.6, 0.9995)
            u = k * v
            nC = S // CHUNK
            a_c = jnp.moveaxis(a.reshape(B, nC, CHUNK, HEADS, HDIM), 1, 0)
            u_c = jnp.moveaxis(u.reshape(B, nC, CHUNK, HEADS, HDIM), 1, 0)

            def step(state, inp):
                ac, uc = inp
                prefix = jnp.cumprod(ac, axis=1)
                acc = jnp.cumsum(uc / jnp.maximum(prefix, 1e-06), axis=1)
                states = prefix * (state[:, None] + acc)
                return (states[:, -1], states)
            state0 = jnp.zeros((B, HEADS, HDIM), jnp.float32)
            _, states = jax.lax.scan(step, state0, (a_c, u_c))
            memory = jnp.moveaxis(states, 0, 1).reshape(B, S, HEADS, HDIM)
            gate = jax.nn.sigmoid(g)
            y = gate * (q * memory) + (1.0 - gate) * v
            return y.reshape(B, S, D) @ out_proj_w.T
        key = jax.random.key(seed)
        ks = jax.random.split(key, 5)
        s = 0.02
        return {'x': jax.random.normal(ks[0], (2, 512, DIM), jnp.float32), 'norm1_w': jnp.ones((DIM,), jnp.float32), 'norm2_w': jnp.ones((DIM,), jnp.float32), 'in_proj_w': jax.random.normal(ks[1], (5 * DIM, DIM), jnp.float32) * s, 'out_proj_w': jax.random.normal(ks[2], (DIM, DIM), jnp.float32) * s, 'fc_w': jax.random.normal(ks[3], (512, DIM), jnp.float32) * s, 'proj_w': jax.random.normal(ks[4], (DIM, 512), jnp.float32) * s}
    _L0_attn_in = _L0_attn_setup()

    def _L0_ffn_setup():
        import jax, jax.numpy as jnp
        import numpy as np
        EPS = 1e-08

        def _ternary_linear(x, w):
            alpha = jnp.mean(jnp.abs(w))
            w_t = jnp.sign(w) * (jnp.abs(w) > 0.5 * alpha).astype(w.dtype)
            w_q = w + jax.lax.stop_gradient(w_t - w)
            d = x.shape[-1]
            rms = jnp.sqrt(jnp.sum(x * x, axis=-1, keepdims=True)) / jnp.sqrt(jnp.asarray(d, x.dtype))
            x_norm = x / (rms + EPS)
            return jnp.einsum('bsd,fd->bsf', x_norm, w_q)
        key = jax.random.key(seed)
        k1, k2, k3 = jax.random.split(key, 3)
        d_model, d_ff = (128, 512)
        B, S = (4, 512)
        x = jax.random.normal(k1, (B, S, d_model), dtype=jnp.float32)
        w_up = jax.random.normal(k2, (d_ff, d_model), dtype=jnp.float32) * 0.02
        w_down = jax.random.normal(k3, (d_model, d_ff), dtype=jnp.float32) * 0.02
        return {'x': x, 'w_up': w_up, 'w_down': w_down}
    _L0_ffn_in = _L0_ffn_setup()

    def _L1_attn_setup():
        import jax, jax.numpy as jnp
        import numpy as np
        D_MODEL = 128
        NUM_HEADS = 16
        DK = D_MODEL // NUM_HEADS
        key = jax.random.key(seed)
        kx, kq, kk, kv, ko = jax.random.split(key, 5)
        B, S = (4, 256)
        bound = float(np.sqrt(6.0 / (D_MODEL + D_MODEL)))
        uni = lambda k: jax.random.uniform(k, (D_MODEL, D_MODEL), jnp.float32, -bound, bound)
        return {'x': jax.random.normal(kx, (B, S, D_MODEL), jnp.float32), 'q_heads': uni(kq), 'k_heads': uni(kk), 'v_heads': uni(kv), 'output_proj': uni(ko)}
    _L1_attn_in = _L1_attn_setup()

    def _L1_ffn_setup():
        import math
        import jax, jax.numpy as jnp
        import numpy as np
        H = 128
        F = 512
        E = 8
        TOP_K = 2
        CAP_FACTOR = 1.25
        MIN_CAP = 4
        SHARED_SCALE = 0.1

        def _top2_gating(logits, capacity):
            N, nE = logits.shape
            gates = jax.nn.softmax(logits, axis=-1)
            idx1 = jnp.argmax(gates, axis=-1)
            mask1 = jax.nn.one_hot(idx1, nE, dtype=gates.dtype)
            idx2 = jnp.argmax(gates * (1.0 - mask1), axis=-1)
            mask2 = jax.nn.one_hot(idx2, nE, dtype=gates.dtype)
            pos1 = jnp.cumsum(mask1, axis=0) - mask1
            mask1 = mask1 * (pos1 < capacity)
            pos2 = jnp.cumsum(mask2, axis=0) - mask2 + jnp.sum(mask1, axis=0, keepdims=True)
            mask2 = mask2 * (pos2 < capacity)
            g1 = jnp.sum(gates * mask1, axis=-1)
            g2 = jnp.sum(gates * mask2, axis=-1)
            denom = jnp.maximum(g1 + g2, jnp.finfo(gates.dtype).eps)
            g1, g2 = (g1 / denom, g2 / denom)
            loc1 = jnp.sum(pos1 * mask1, axis=-1).astype(jnp.int32)
            loc2 = jnp.sum(pos2 * mask2, axis=-1).astype(jnp.int32)
            oh1 = jax.nn.one_hot(loc1, capacity, dtype=gates.dtype)
            oh2 = jax.nn.one_hot(loc2, capacity, dtype=gates.dtype)
            combine = (g1[:, None] * mask1)[:, :, None] * oh1[:, None, :] + (g2[:, None] * mask2)[:, :, None] * oh2[:, None, :]
            dispatch = (combine > 0).astype(gates.dtype)
            return (combine, dispatch)
        key = jax.random.key(seed)
        ks = jax.random.split(key, 10)
        s_h = 1.0 / math.sqrt(H)
        s_f = 1.0 / math.sqrt(F)
        return {'hidden_states': jax.random.normal(ks[0], (2, 256, H), jnp.float32), 'router_w': jax.random.uniform(ks[1], (H, E), jnp.float32, -s_h, s_h), 'w1': jax.random.uniform(ks[2], (E, H, F), jnp.float32, -s_h, s_h), 'b1': jax.random.uniform(ks[3], (E, F), jnp.float32, -s_h, s_h), 'w2': jax.random.uniform(ks[4], (E, F, H), jnp.float32, -s_f, s_f), 'b2': jax.random.uniform(ks[5], (E, H), jnp.float32, -s_f, s_f), 'sw1': jax.random.uniform(ks[6], (H, F), jnp.float32, -s_h, s_h), 'sb1': jax.random.uniform(ks[7], (F,), jnp.float32, -s_h, s_h), 'sw2': jax.random.uniform(ks[8], (F, H), jnp.float32, -s_f, s_f), 'sb2': jax.random.uniform(ks[9], (H,), jnp.float32, -s_f, s_f)}
    _L1_ffn_in = _L1_ffn_setup()

    def _L2_attn_setup():
        import jax, jax.numpy as jnp
        import numpy as np
        import math
        NUM_HEADS = 16

        def get_slopes(n):

            def pow2(n):
                start = 2 ** (-2 ** (-(math.log2(n) - 3)))
                return [start * start ** i for i in range(n)]
            if math.log2(n).is_integer():
                return pow2(n)
            c = 2 ** math.floor(math.log2(n))
            return pow2(c) + get_slopes(2 * c)[0::2][:n - c]
        key = jax.random.key(seed)
        ks = jax.random.split(key, 5)
        B, T, C = (2, 256, 128)
        return {'x': jax.random.normal(ks[0], (B, T, C), dtype=jnp.float32), 'W_qkv': jax.random.normal(ks[1], (C, 3 * C), dtype=jnp.float32) * 0.02, 'b_qkv': jax.random.normal(ks[2], (3 * C,), dtype=jnp.float32) * 0.02, 'W_proj': jax.random.normal(ks[3], (C, C), dtype=jnp.float32) * 0.02, 'b_proj': jax.random.normal(ks[4], (C,), dtype=jnp.float32) * 0.02}
    _L2_attn_in = _L2_attn_setup()

    def _L2_ffn_setup():
        import jax, jax.numpy as jnp
        import numpy as np
        D_MODEL = 128
        M = 64
        INNER = 16
        key = jax.random.key(seed)
        ks = jax.random.split(key, 9)

        def init(k, shape, fan_in):
            bound = 1.0 / np.sqrt(fan_in)
            return jax.random.uniform(k, shape, jnp.float32, -bound, bound)
        x = jax.random.normal(ks[0], (16, 512, D_MODEL), dtype=jnp.float32)
        Win = init(ks[1], (D_MODEL, M), D_MODEL)
        bin_ = init(ks[2], (M,), D_MODEL)
        W1 = init(ks[3], (M, INNER), 1)
        b1 = init(ks[4], (M, INNER), 1)
        W2 = init(ks[5], (M, INNER), INNER)
        b2 = init(ks[6], (M,), INNER)
        Wout = init(ks[7], (M, D_MODEL), M)
        bout = init(ks[8], (D_MODEL,), M)
        return {'x': x, 'Win': Win, 'bin_': bin_, 'W1': W1, 'b1': b1, 'W2': W2, 'b2': b2, 'Wout': Wout, 'bout': bout}
    _L2_ffn_in = _L2_ffn_setup()

    def _L3_attn_setup():
        import jax, jax.numpy as jnp
        import numpy as np
        DIM, HEADS = (128, 16)
        B, N = (2, 256)
        key = jax.random.key(seed)
        ks = jax.random.split(key, 8)
        d = DIM // HEADS
        return {'x': jax.random.normal(ks[0], (B, N, DIM), dtype=jnp.float32), 'w_qkv': jax.random.normal(ks[1], (DIM, 3 * DIM), dtype=jnp.float32) * DIM ** (-0.5), 'w_out': jax.random.normal(ks[2], (DIM, DIM), dtype=jnp.float32) * DIM ** (-0.5), 'b_out': jnp.zeros((DIM,), dtype=jnp.float32), 'void_q': jax.random.normal(ks[3], (1, HEADS, 1, d), dtype=jnp.float32), 'void_k': jax.random.normal(ks[4], (1, HEADS, 1, d), dtype=jnp.float32), 'void_v': jax.random.normal(ks[5], (1, HEADS, 1, d), dtype=jnp.float32), 'attention_trace': jax.random.uniform(ks[6], (HEADS, 1, 1), dtype=jnp.float32), 'temperature_factor': jax.random.normal(ks[7], (HEADS, 1, 1), dtype=jnp.float32)}
    _L3_attn_in = _L3_attn_setup()

    def _L3_ffn_setup():
        import jax, jax.numpy as jnp
        import numpy as np
        D_MODEL = 128
        D_FF = 256
        N_EXPERTS = 8
        TOP_K = 2
        CLAMP = 10000.0
        ROUTER_EPS = 1e-08
        LN_EPS = 1e-05

        def _layernorm(x, g, b):
            mu = jnp.mean(x, axis=-1, keepdims=True)
            var = jnp.mean(jnp.square(x - mu), axis=-1, keepdims=True)
            return (x - mu) * jax.lax.rsqrt(var + LN_EPS) * g + b
        key = jax.random.key(seed)
        k1, k2, k3, k4 = jax.random.split(key, 4)
        B, S = (8, 128)
        x = jax.random.normal(k1, (B, S, D_MODEL), dtype=jnp.float32)
        ln_gamma = jnp.ones((D_MODEL,), jnp.float32)
        ln_beta = jnp.zeros((D_MODEL,), jnp.float32)
        bound = 0.02 * float(np.sqrt(3.0))
        router_w = jax.random.uniform(k2, (N_EXPERTS, D_MODEL), jnp.float32, -bound, bound)
        gate_up_w = jax.random.normal(k3, (N_EXPERTS, 2 * D_FF, D_MODEL), jnp.float32) * (1.0 / np.sqrt(D_MODEL))
        down_w = jax.random.normal(k4, (N_EXPERTS, D_MODEL, D_FF), jnp.float32) * (1.0 / np.sqrt(D_FF))
        return {'x': x, 'ln_gamma': ln_gamma, 'ln_beta': ln_beta, 'router_w': router_w, 'gate_up_w': gate_up_w, 'down_w': down_w}
    _L3_ffn_in = _L3_ffn_setup()
    _d = {'L0_attn_x': _L0_attn_in['x'], 'L0_attn_norm1_w': _L0_attn_in['norm1_w'], 'L0_attn_norm2_w': _L0_attn_in['norm2_w'], 'L0_attn_in_proj_w': _L0_attn_in['in_proj_w'], 'L0_attn_out_proj_w': _L0_attn_in['out_proj_w'], 'L0_attn_fc_w': _L0_attn_in['fc_w'], 'L0_attn_proj_w': _L0_attn_in['proj_w'], 'L0_ffn_w_up': _L0_ffn_in['w_up'], 'L0_ffn_w_down': _L0_ffn_in['w_down'], 'L1_attn_q_heads': _L1_attn_in['q_heads'], 'L1_attn_k_heads': _L1_attn_in['k_heads'], 'L1_attn_v_heads': _L1_attn_in['v_heads'], 'L1_attn_output_proj': _L1_attn_in['output_proj'], 'L1_ffn_router_w': _L1_ffn_in['router_w'], 'L1_ffn_w1': _L1_ffn_in['w1'], 'L1_ffn_b1': _L1_ffn_in['b1'], 'L1_ffn_w2': _L1_ffn_in['w2'], 'L1_ffn_b2': _L1_ffn_in['b2'], 'L1_ffn_sw1': _L1_ffn_in['sw1'], 'L1_ffn_sb1': _L1_ffn_in['sb1'], 'L1_ffn_sw2': _L1_ffn_in['sw2'], 'L1_ffn_sb2': _L1_ffn_in['sb2'], 'L2_attn_W_qkv': _L2_attn_in['W_qkv'], 'L2_attn_b_qkv': _L2_attn_in['b_qkv'], 'L2_attn_W_proj': _L2_attn_in['W_proj'], 'L2_attn_b_proj': _L2_attn_in['b_proj'], 'L2_ffn_Win': _L2_ffn_in['Win'], 'L2_ffn_bin_': _L2_ffn_in['bin_'], 'L2_ffn_W1': _L2_ffn_in['W1'], 'L2_ffn_b1': _L2_ffn_in['b1'], 'L2_ffn_W2': _L2_ffn_in['W2'], 'L2_ffn_b2': _L2_ffn_in['b2'], 'L2_ffn_Wout': _L2_ffn_in['Wout'], 'L2_ffn_bout': _L2_ffn_in['bout'], 'L3_attn_w_qkv': _L3_attn_in['w_qkv'], 'L3_attn_w_out': _L3_attn_in['w_out'], 'L3_attn_b_out': _L3_attn_in['b_out'], 'L3_attn_void_q': _L3_attn_in['void_q'], 'L3_attn_void_k': _L3_attn_in['void_k'], 'L3_attn_void_v': _L3_attn_in['void_v'], 'L3_attn_attention_trace': _L3_attn_in['attention_trace'], 'L3_attn_temperature_factor': _L3_attn_in['temperature_factor'], 'L3_ffn_ln_gamma': _L3_ffn_in['ln_gamma'], 'L3_ffn_ln_beta': _L3_ffn_in['ln_beta'], 'L3_ffn_router_w': _L3_ffn_in['router_w'], 'L3_ffn_gate_up_w': _L3_ffn_in['gate_up_w'], 'L3_ffn_down_w': _L3_ffn_in['down_w']}
    _x0 = _d['L0_attn_x']
    _d['L0_attn_x'] = jax.random.normal(jax.random.fold_in(jax.random.key(seed), 1), (4, 512, 128), dtype=_x0.dtype)
    del _x0
    return _d

def reference(L0_attn_x, L0_attn_norm1_w, L0_attn_norm2_w, L0_attn_in_proj_w, L0_attn_out_proj_w, L0_attn_fc_w, L0_attn_proj_w, L0_ffn_w_up, L0_ffn_w_down, L1_attn_q_heads, L1_attn_k_heads, L1_attn_v_heads, L1_attn_output_proj, L1_ffn_router_w, L1_ffn_w1, L1_ffn_b1, L1_ffn_w2, L1_ffn_b2, L1_ffn_sw1, L1_ffn_sb1, L1_ffn_sw2, L1_ffn_sb2, L2_attn_W_qkv, L2_attn_b_qkv, L2_attn_W_proj, L2_attn_b_proj, L2_ffn_Win, L2_ffn_bin_, L2_ffn_W1, L2_ffn_b1, L2_ffn_W2, L2_ffn_b2, L2_ffn_Wout, L2_ffn_bout, L3_attn_w_qkv, L3_attn_w_out, L3_attn_b_out, L3_attn_void_q, L3_attn_void_k, L3_attn_void_v, L3_attn_attention_trace, L3_attn_temperature_factor, L3_ffn_ln_gamma, L3_ffn_ln_beta, L3_ffn_router_w, L3_ffn_gate_up_w, L3_ffn_down_w):

    def _L0_attn_ref(x, norm1_w, norm2_w, in_proj_w, out_proj_w, fc_w, proj_w):
        import jax, jax.numpy as jnp
        import numpy as np
        DIM = 128
        HEADS = 16
        HDIM = DIM // HEADS
        CHUNK = 64
        RES_SCALE = float(1.0 / np.sqrt(2.0))
        EPS_FP32 = float(np.finfo(np.float32).eps)

        def _rms(x, eps):
            return x * jax.lax.rsqrt(jnp.mean(x * x, axis=-1, keepdims=True) + eps)

        def _mixer(x, in_proj_w, out_proj_w):
            B, S, D = x.shape
            proj = x @ in_proj_w.T
            q, k, v, a, g = jnp.split(proj, 5, axis=-1)
            rs = lambda t: t.reshape(B, S, HEADS, HDIM)
            q, k, v, a, g = map(rs, (q, k, v, a, g))
            q = _rms(q, EPS_FP32)
            k = jnp.tanh(k)
            a = jnp.clip(jax.nn.sigmoid(a + 2.0), 0.6, 0.9995)
            u = k * v
            nC = S // CHUNK
            a_c = jnp.moveaxis(a.reshape(B, nC, CHUNK, HEADS, HDIM), 1, 0)
            u_c = jnp.moveaxis(u.reshape(B, nC, CHUNK, HEADS, HDIM), 1, 0)

            def step(state, inp):
                ac, uc = inp
                prefix = jnp.cumprod(ac, axis=1)
                acc = jnp.cumsum(uc / jnp.maximum(prefix, 1e-06), axis=1)
                states = prefix * (state[:, None] + acc)
                return (states[:, -1], states)
            state0 = jnp.zeros((B, HEADS, HDIM), jnp.float32)
            _, states = jax.lax.scan(step, state0, (a_c, u_c))
            memory = jnp.moveaxis(states, 0, 1).reshape(B, S, HEADS, HDIM)
            gate = jax.nn.sigmoid(g)
            y = gate * (q * memory) + (1.0 - gate) * v
            return y.reshape(B, S, D) @ out_proj_w.T
        h1 = norm1_w * _rms(x, 1e-06)
        x = x + RES_SCALE * _mixer(h1, in_proj_w, out_proj_w)
        h2 = norm2_w * _rms(x, 1e-06)
        mlp = jax.nn.silu(h2 @ fc_w.T) @ proj_w.T
        return x + RES_SCALE * mlp

    def _L0_ffn_ref(x, w_up, w_down):
        import jax, jax.numpy as jnp
        import numpy as np
        EPS = 1e-08

        def _ternary_linear(x, w):
            alpha = jnp.mean(jnp.abs(w))
            w_t = jnp.sign(w) * (jnp.abs(w) > 0.5 * alpha).astype(w.dtype)
            w_q = w + jax.lax.stop_gradient(w_t - w)
            d = x.shape[-1]
            rms = jnp.sqrt(jnp.sum(x * x, axis=-1, keepdims=True)) / jnp.sqrt(jnp.asarray(d, x.dtype))
            x_norm = x / (rms + EPS)
            return jnp.einsum('bsd,fd->bsf', x_norm, w_q)
        h = jax.nn.gelu(_ternary_linear(x, w_up), approximate=False)
        return _ternary_linear(h, w_down)

    def _L1_attn_ref(x, q_heads, k_heads, v_heads, output_proj):
        import jax, jax.numpy as jnp
        import numpy as np
        D_MODEL = 128
        NUM_HEADS = 16
        DK = D_MODEL // NUM_HEADS
        B, S, _ = x.shape

        def proj(W):
            return (x @ W.T).reshape(B, S, NUM_HEADS, DK).transpose(0, 2, 1, 3)
        q, k, v = (proj(q_heads), proj(k_heads), proj(v_heads))
        scale = 1.0 / jnp.sqrt(jnp.asarray(DK, x.dtype))
        scores = jnp.einsum('bhqd,bhkd->bhqk', q, k) * scale
        causal = jnp.triu(jnp.ones((S, S), bool), k=1)
        scores = jnp.where(causal, jnp.asarray(-jnp.inf, scores.dtype), scores)
        attn = jax.nn.softmax(scores, axis=-1)
        out = jnp.einsum('bhqk,bhkd->bhqd', attn, v)
        out = out.transpose(0, 2, 1, 3).reshape(B, S, D_MODEL)
        return out @ output_proj.T

    def _L1_ffn_ref(hidden_states, router_w, w1, b1, w2, b2, sw1, sb1, sw2, sb2):
        import math
        import jax, jax.numpy as jnp
        import numpy as np
        H = 128
        F = 512
        E = 8
        TOP_K = 2
        CAP_FACTOR = 1.25
        MIN_CAP = 4
        SHARED_SCALE = 0.1

        def _top2_gating(logits, capacity):
            N, nE = logits.shape
            gates = jax.nn.softmax(logits, axis=-1)
            idx1 = jnp.argmax(gates, axis=-1)
            mask1 = jax.nn.one_hot(idx1, nE, dtype=gates.dtype)
            idx2 = jnp.argmax(gates * (1.0 - mask1), axis=-1)
            mask2 = jax.nn.one_hot(idx2, nE, dtype=gates.dtype)
            pos1 = jnp.cumsum(mask1, axis=0) - mask1
            mask1 = mask1 * (pos1 < capacity)
            pos2 = jnp.cumsum(mask2, axis=0) - mask2 + jnp.sum(mask1, axis=0, keepdims=True)
            mask2 = mask2 * (pos2 < capacity)
            g1 = jnp.sum(gates * mask1, axis=-1)
            g2 = jnp.sum(gates * mask2, axis=-1)
            denom = jnp.maximum(g1 + g2, jnp.finfo(gates.dtype).eps)
            g1, g2 = (g1 / denom, g2 / denom)
            loc1 = jnp.sum(pos1 * mask1, axis=-1).astype(jnp.int32)
            loc2 = jnp.sum(pos2 * mask2, axis=-1).astype(jnp.int32)
            oh1 = jax.nn.one_hot(loc1, capacity, dtype=gates.dtype)
            oh2 = jax.nn.one_hot(loc2, capacity, dtype=gates.dtype)
            combine = (g1[:, None] * mask1)[:, :, None] * oh1[:, None, :] + (g2[:, None] * mask2)[:, :, None] * oh2[:, None, :]
            dispatch = (combine > 0).astype(gates.dtype)
            return (combine, dispatch)
        B, S, h = hidden_states.shape
        x = hidden_states.reshape(-1, h)
        N = x.shape[0]
        capacity = min(max(MIN_CAP, math.ceil(TOP_K * CAP_FACTOR * N / E)), N)
        logits = x @ router_w
        combine, dispatch = _top2_gating(logits, capacity)
        expert_in = jnp.einsum('nec,nh->ech', dispatch, x)
        hmid = jax.nn.silu(jnp.einsum('ech,ehf->ecf', expert_in, w1) + b1[:, None, :])
        expert_out = jnp.einsum('ecf,efh->ech', hmid, w2) + b2[:, None, :]
        y = jnp.einsum('nec,ech->nh', combine, expert_out)
        shared = jax.nn.silu(x @ sw1 + sb1) @ sw2 + sb2
        out = y + SHARED_SCALE * shared
        return out.reshape(B, S, h)

    def _L2_attn_ref(x, W_qkv, b_qkv, W_proj, b_proj):
        import jax, jax.numpy as jnp
        import numpy as np
        import math
        NUM_HEADS = 16

        def get_slopes(n):

            def pow2(n):
                start = 2 ** (-2 ** (-(math.log2(n) - 3)))
                return [start * start ** i for i in range(n)]
            if math.log2(n).is_integer():
                return pow2(n)
            c = 2 ** math.floor(math.log2(n))
            return pow2(c) + get_slopes(2 * c)[0::2][:n - c]
        B, T, C = x.shape
        H = NUM_HEADS
        D = C // H
        qkv = x @ W_qkv + b_qkv
        q, k, v = jnp.split(qkv, 3, axis=-1)
        q = q.reshape(B, T, H, D).transpose(0, 2, 1, 3)
        k = k.reshape(B, T, H, D).transpose(0, 2, 1, 3)
        v = v.reshape(B, T, H, D).transpose(0, 2, 1, 3)
        slopes = jnp.asarray(get_slopes(H), dtype=jnp.float32)
        idx = jnp.arange(T)
        alibi = jnp.minimum(idx[None, :] - idx[:, None], 0).astype(jnp.float32)
        bias = slopes[:, None, None] * alibi
        scale = 1.0 / math.sqrt(D)
        scores = jnp.einsum('bhtd,bhsd->bhts', q, k) * scale + bias[None]
        w = jax.nn.softmax(scores, axis=-1)
        y = jnp.einsum('bhts,bhsd->bhtd', w, v)
        y = y.transpose(0, 2, 1, 3).reshape(B, T, C)
        return y @ W_proj + b_proj

    def _L2_ffn_ref(x, Win, bin_, W1, b1, W2, b2, Wout, bout):
        import jax, jax.numpy as jnp
        import numpy as np
        D_MODEL = 128
        M = 64
        INNER = 16
        s = jnp.einsum('btd,dm->btm', x, Win) + bin_
        h = jax.nn.relu(s[..., None] * W1 + b1)
        g = jnp.einsum('btmh,mh->btm', h, W2) + b2
        out = jnp.einsum('btm,md->btd', g, Wout) + bout
        return out

    def _L3_attn_ref(x, w_qkv, w_out, b_out, void_q, void_k, void_v, attention_trace, temperature_factor):
        import jax, jax.numpy as jnp
        import numpy as np
        DIM, HEADS = (128, 16)
        B, N = (2, 256)
        b, n, dim = x.shape
        h = void_q.shape[1]
        d = dim // h
        qkv = x @ w_qkv
        q, k, v = jnp.split(qkv, 3, axis=-1)

        def to_heads(t):
            return t.reshape(b, n, h, d).transpose(0, 2, 1, 3)
        q, k, v = (to_heads(q), to_heads(k), to_heads(v))
        q = jnp.concatenate([q, jnp.broadcast_to(void_q, (b, h, 1, d))], axis=2)
        k = jnp.concatenate([k, jnp.broadcast_to(void_k, (b, h, 1, d))], axis=2)
        v = jnp.concatenate([v, jnp.broadcast_to(void_v, (b, h, 1, d))], axis=2)
        dots = jnp.einsum('bhid,bhjd->bhij', q, k) * dim ** (-0.5)
        dots = dots.at[:, :, n, n].add(10.0)
        temperature = jnp.maximum(1.0 + jnp.abs(attention_trace) * temperature_factor, 1.0)
        attn = jax.nn.softmax(dots / temperature, axis=-1)
        out = jnp.einsum('bhij,bhjd->bhid', attn, v)[:, :, :n, :]
        out = out.transpose(0, 2, 1, 3).reshape(b, n, dim)
        return out @ w_out + b_out

    def _L3_ffn_ref(x, ln_gamma, ln_beta, router_w, gate_up_w, down_w):
        import jax, jax.numpy as jnp
        import numpy as np
        D_MODEL = 128
        D_FF = 256
        N_EXPERTS = 8
        TOP_K = 2
        CLAMP = 10000.0
        ROUTER_EPS = 1e-08
        LN_EPS = 1e-05

        def _layernorm(x, g, b):
            mu = jnp.mean(x, axis=-1, keepdims=True)
            var = jnp.mean(jnp.square(x - mu), axis=-1, keepdims=True)
            return (x - mu) * jax.lax.rsqrt(var + LN_EPS) * g + b
        B, S, D = x.shape
        xn = _layernorm(x, ln_gamma, ln_beta)
        xf = xn.reshape(-1, D)
        N = xf.shape[0]
        logits = jnp.clip(xf @ router_w.T, -CLAMP, CLAMP)
        m = jnp.max(logits, axis=-1, keepdims=True)
        e = jnp.exp(logits - m)
        probs = e / (jnp.sum(e, axis=-1, keepdims=True) + ROUTER_EPS)
        probs = jnp.clip(probs, ROUTER_EPS, 1.0)
        topk_p, topk_i = jax.lax.top_k(probs, TOP_K)
        dense_gate = jnp.zeros((N, N_EXPERTS), probs.dtype).at[jnp.arange(N)[:, None], topk_i].add(topk_p)
        out = jnp.zeros_like(xf)
        for eid in range(N_EXPERTS):
            xe = xf * dense_gate[:, eid:eid + 1]
            gu = xe @ gate_up_w[eid].T
            gate, up = jnp.split(gu, 2, axis=-1)
            hidden = jax.nn.silu(gate) * up
            out = out + hidden @ down_w[eid].T
        return x + out.reshape(B, S, D)
    x = L0_attn_x
    x = _layernorm(x + _L0_attn_ref(x, L0_attn_norm1_w, L0_attn_norm2_w, L0_attn_in_proj_w, L0_attn_out_proj_w, L0_attn_fc_w, L0_attn_proj_w), axis=-1)
    x = _layernorm(x + _L0_ffn_ref(x, L0_ffn_w_up, L0_ffn_w_down), axis=-1)
    x = _layernorm(x + _L1_attn_ref(x, L1_attn_q_heads, L1_attn_k_heads, L1_attn_v_heads, L1_attn_output_proj), axis=-1)
    x = _layernorm(x + _L1_ffn_ref(x, L1_ffn_router_w, L1_ffn_w1, L1_ffn_b1, L1_ffn_w2, L1_ffn_b2, L1_ffn_sw1, L1_ffn_sb1, L1_ffn_sw2, L1_ffn_sb2), axis=-1)
    x = _layernorm(x + _L2_attn_ref(x, L2_attn_W_qkv, L2_attn_b_qkv, L2_attn_W_proj, L2_attn_b_proj), axis=-1)
    x = _layernorm(x + _L2_ffn_ref(x, L2_ffn_Win, L2_ffn_bin_, L2_ffn_W1, L2_ffn_b1, L2_ffn_W2, L2_ffn_b2, L2_ffn_Wout, L2_ffn_bout), axis=-1)
    x = _layernorm(x + _L3_attn_ref(x, L3_attn_w_qkv, L3_attn_w_out, L3_attn_b_out, L3_attn_void_q, L3_attn_void_k, L3_attn_void_v, L3_attn_attention_trace, L3_attn_temperature_factor), axis=-1)
    x = _layernorm(x + _L3_ffn_ref(x, L3_ffn_ln_gamma, L3_ffn_ln_beta, L3_ffn_router_w, L3_ffn_gate_up_w, L3_ffn_down_w), axis=-1)
    return x

_drawn_inputs = setup_inputs


def setup_inputs(seed=0):
    import zlib

    import numpy as np

    out = dict(_drawn_inputs(seed))
    spreads = {'L0_attn_norm1_w': (1.0, 0.6),
     'L0_attn_norm2_w': (1.0, 0.6),
     'L3_attn_b_out': (0.0, 0.1),
     'L3_ffn_ln_gamma': (1.0, 0.6),
     'L3_ffn_ln_beta': (0.0, 0.8)}
    factors = {'L0_attn_in_proj_w': 3.608,
     'L0_attn_out_proj_w': 4.034,
     'L1_ffn_b1': 4.408,
     'L1_ffn_b2': 3.108,
     'L1_ffn_sw1': 3.554,
     'L1_ffn_sb1': 8.0,
     'L1_ffn_sw2': 3.3,
     'L1_ffn_sb2': 8.0,
     'L2_attn_b_qkv': 8.0,
     'L2_attn_b_proj': 2.707,
     'L2_ffn_bin_': 8.0,
     'L3_attn_void_k': 8.0,
     'L3_attn_void_v': 8.0,
     'L3_attn_attention_trace': 8.0,
     'L3_attn_temperature_factor': 8.0,
     'L3_ffn_router_w': 5.42,
     'L3_ffn_gate_up_w': 5.738,
     'L3_ffn_down_w': 5.613}
    for name, (base, spread) in spreads.items():
        noise = np.random.default_rng([zlib.crc32(name.encode()), seed]).standard_normal(out[name].shape)
        drawn = base * np.exp(spread * noise) if base else spread * noise
        out[name] = jnp.asarray(drawn.astype(out[name].dtype))
    for name, factor in factors.items():
        out[name] = (out[name] * factor).astype(out[name].dtype)
    return out
```

```python
from contextlib import ExitStack, contextmanager

import numpy as np

import concourse.bass as bass
from concourse import mybir

F32 = mybir.dt.float32
BF16 = mybir.dt.bfloat16
ALU = mybir.AluOpType
ACT = mybir.ActivationFunctionType
AX = mybir.AxisListType
ds = bass.ds

P = 128
D = 128
B, S = 4, 512
NT = B * S // P
CT = S // P
H, HD = 16, 8
G, R = 4, 4
E = 8
SCAN = 64
CAP = 640
RES = float(1.0 / np.sqrt(2.0))
EPS32 = float(np.finfo(np.float32).eps)
NEG = -1.0e30
NCOMBO = 72
NLIN = 9


class Track:

    def __init__(self, name, engine, sem, step=1):
        self.name, self.engine, self.sem, self.step = name, engine, sem, step
        self.count = step
        self.gate = None

    def done(self, instruction):
        instruction.then_inc(self.sem, self.step)
        self.count += self.step
        return Token(self, self.count, tuple(LOOPS))

    def here(self):
        return Token(self, self.count, tuple(LOOPS))

    def after(self, *tokens):
        for t in tokens:
            if t is not None:
                self.engine.wait_ge(t.track.sem, t.value())
        return self.engine

    def plain(self, *tokens):
        self.after(*tokens)
        self.engine.sem_inc(self.gate, 1)
        return self.engine


LOOPS = []


class Token:
    def __init__(self, track, count, loops):
        self.track, self.count, self.loops = track, count, loops

    def value(self):
        v = self.count
        for loop in self.loops:
            per = loop.per.get(self.track.name, 0)
            if loop in LOOPS:
                if per:
                    v = loop.i * per + v
            else:
                v = v + (loop.n - 1) * per
        return v


PER = {
 'mixer': {'vector': 35, 'scalar': 13, 'tensor': 14, 'gpsimd': 6},
 'ternary': {'vector': 22, 'scalar': 6, 'tensor': 7, 'gpsimd': 8},
 'a1_prep': {'vector': 7, 'scalar': 4, 'tensor': 4, 'spill': 128},
 'a1': {'vector': 84,
        'scalar': 36,
        'tensor': 120,
        'gpsimd': 16,
        'operand0': 64,
        'operand1': 64,
        'operand2': 64,
        'operand3': 64,
        'mrow0': 32,
        'mrow1': 32,
        'mrow2': 32,
        'mrow3': 32},
 'a1_out': {'vector': 17, 'scalar': 1, 'tensor': 2, 'gpsimd': 2},
 'route1': {'vector': 1, 'scalar': 2, 'tensor': 2},
 'experts1': {'vector': 47, 'scalar': 40, 'tensor': 48, 'gpsimd': 2},
 'a2_prep': {'vector': 7, 'scalar': 4, 'tensor': 4, 'spill': 128},
 'a2': {'vector': 84,
        'scalar': 68,
        'tensor': 120,
        'gpsimd': 16,
        'operand0': 64,
        'operand1': 64,
        'operand2': 64,
        'operand3': 64,
        'mrow0': 32,
        'mrow1': 32,
        'mrow2': 32,
        'mrow3': 32},
 'a2_out': {'vector': 18, 'scalar': 1, 'tensor': 2, 'gpsimd': 2},
 'channels': {'vector': 14, 'scalar': 10, 'tensor': 10, 'gpsimd': 2},
 'a3_prep': {'vector': 7, 'scalar': 4, 'tensor': 4, 'spill': 128},
 'a3': {'vector': 92,
        'scalar': 40,
        'tensor': 132,
        'gpsimd': 16,
        'operand0': 64,
        'operand1': 64,
        'operand2': 64,
        'operand3': 64,
        'mrow0': 32,
        'mrow1': 32,
        'mrow2': 32,
        'mrow3': 32},
 'a3_out': {'vector': 18, 'scalar': 1, 'tensor': 2, 'gpsimd': 2},
 'route3': {'vector': 13, 'scalar': 1, 'tensor': 2, 'gpsimd': 2},
 'experts3': {'vector': 50, 'scalar': 19, 'tensor': 50, 'gpsimd': 4}}


class Loop:
    def __init__(self, nc, tracks, n, name):
        self.nc, self.tracks, self.n, self.name, self.per = nc, tracks, n, name, PER.get(name, {})

    @contextmanager
    def run(self):
        with self.nc.Fori(0, self.n) as i:
            self.i = i
            self.start = {t.name: t.count for t in self.tracks}
            LOOPS.append(self)
            yield self
            LOOPS.pop()
        got = {t.name: t.count - self.start[t.name] for t in self.tracks if t.count != self.start[t.name]}
        assert got == self.per, f"{self.name}: a turn counts {got}"
        for t in self.tracks:
            t.count += (self.n - 1) * self.per.get(t.name, 0)


def build_program(nc, args, out):
    ctx = ExitStack()
    with ctx:
        def sb(name, shape, dt=F32):
            return ctx.enter_context(nc.sbuf_tensor(name, shape, dt))

        def sem(name):
            return ctx.enter_context(nc.semaphore(name))

        V = Track("vector", nc.vector, sem("vector"))
        A = Track("scalar", nc.scalar, sem("scalar"))
        PE = Track("tensor", nc.tensor, sem("tensor"))
        PO = Track("gpsimd", nc.gpsimd, sem("gpsimd"))

        PE.gate, A.gate = sem("tensor_gate"), sem("scalar_gate")
        V.gate, PO.gate = sem("vector_gate"), sem("gpsimd_gate")
        sync_gate = sem("sync_gate")
        dma_tracks = []

        def dma(name, engine=None):
            t = Track(name, engine or nc.sync, sem("dma_" + name), 16)
            t.gate = sync_gate
            dma_tracks.append(t)
            return t

        LD0 = [dma(f"load{i}") for i in range(9)]
        CONST = dma("const")
        SPILL = dma("spill")
        ROWS = dma("rows")
        CAST = dma("cast", nc.gpsimd)
        OUT = dma("out")
        tracks = [V, A, PE, PO] + dma_tracks
        CAST.count = 0
        for t in tracks:
            if t is not CAST:
                t.engine.sem_inc(t.sem, t.step)

        def loop(n, name):
            return Loop(nc, tracks, n, name).run()

        X = sb("X", [P, NT, D])
        xn = sb("xn", [P, CT, D])
        xT = sb("xT", [P, S])
        sq = sb("sq", [P, CT, D])
        x1 = sb("x1", [P, CT, D])
        tot = sb("tot", [P, CT, D])
        ss = sb("ss", [P, CT])
        va = sb("va", [P, CT])
        rs = sb("rs", [P, CT])
        bn6 = sb("bn6", [P, CT, 6])
        mv = sb("mv", [P, CT, 2])
        hT = sb("hT", [P, 4, S])
        zone = sb("zone", [P, 12288])

        def in_zone(at, shape, dt=F32, parts=P):
            n = int(np.prod(shape)) * (2 if dt == BF16 else 4) // 4
            v = zone[0:parts, at:at + n]
            if dt == BF16:
                v = v.bitcast(BF16)
            names = " ".join("abcd"[:len(shape)])
            return v.rearrange(f"p ({names}) -> p {names}", **{"abcd"[i]: shape[i] for i in range(len(shape))})

        PS = ctx.enter_context(nc.psum_tensor("PS", [P, 8, 512], F32))

        def bank(i):
            return PS[:, i, :]

        def chunk(i):
            return PS[:, i, :].rearrange("p (j d) -> p j d", j=CT)

        def flat(t):
            return t.rearrange("p a b -> p (a b)")

        consts = {}
        for name in ("ident", "causal_kq", "causal_qk", "alibi_kq", "alibi_qk", "headmean", "tri"):
            consts[name] = sb("c_" + name, [P, P])
            nc.sync.dma_start(consts[name][:], args["c_" + name]).then_inc(CONST.sem, 16)
            CONST.count += 16
        rank = sb("rank", [P, E])
        slopes = sb("slopes", [P, H])
        qscale2 = sb("qscale2", [P, 1])
        for t, n in ((rank, "c_rank"), (slopes, "c_slopes"), (qscale2, "c_qscale2")):
            nc.sync.dma_start(t[:], args[n]).then_inc(CONST.sem, 16)
            CONST.count += 16
        const_in = CONST.here()
        ident = consts["ident"]

        def load(track, name, shape, src):
            t = sb(name, shape)
            track.done(nc.sync.dma_start(t[:], src))
            return t

        L = LD0
        for b in range(B):
            x_in = L[8].done(nc.sync.dma_start(X[:, b * CT:(b + 1) * CT, :], args["x"][b].rearrange("(j p) d -> p j d", p=P)))
        w_in = load(L[0], "w_in", [P, 5 * D], args["L0_attn_in_proj_w"])
        w_out0 = load(L[0], "w_out0", [P, D], args["L0_attn_out_proj_w"])
        w_fc = load(L[0], "w_fc", [P, 512], args["L0_attn_fc_w"])
        w_pr = load(L[0], "w_pr", [P, 4, D], args["L0_attn_proj_w"].rearrange("(f p) d -> p f d", p=P))
        n1 = load(L[0], "n1", [P, 1], args["L0_attn_norm1_w"])
        n2 = load(L[0], "n2", [P, 1], args["L0_attn_norm2_w"])
        w_up = load(L[1], "w_up", [P, 512], args["L0_ffn_w_up"])
        w_dn = load(L[1], "w_dn", [P, 4, D], args["L0_ffn_w_down"].rearrange("(f p) d -> p f d", p=P))
        wq1, wk1, wv1, wo1 = [load(L[2], n, [P, D], args[a]) for n, a in (
            ("wq1", "L1_attn_q_heads"), ("wk1", "L1_attn_k_heads"), ("wv1", "L1_attn_v_heads"), ("wo1", "L1_attn_output_proj"))]

        ones = sb("ones", [P, P])
        onesb = sb("onesb", [P, P], BF16)
        half = sb("half", [P, NT])
        mhalf = sb("mhalf", [P, NT])
        m_one = sb("m_one", [P, NT])
        PO.done(nc.gpsimd.memset(ones[:], 1.0))
        PO.done(nc.gpsimd.memset(onesb[:], 1.0))
        PO.done(nc.gpsimd.memset(half[:], 0.5))
        PO.done(nc.gpsimd.memset(m_one[:], -1.0))
        pool_ready = PO.done(nc.gpsimd.memset(mhalf[:], -0.5))
        bf = {}
        V.after(const_in)
        for name in ("ident", "causal_kq", "causal_qk", "alibi_kq", "alibi_qk", "tri"):
            bf[name] = sb("b_" + name, [P, P], BF16)
            bf_ready = V.done(nc.vector.tensor_copy(bf[name][:], consts[name][:]))
        bcol = {}
        for name, val in (("two", 2.0), ("eps32", EPS32)):
            bcol[name] = sb("bc_" + name, [P, 1])
            bcol_ready = PO.done(nc.gpsimd.memset(bcol[name][:], val))
        PE.after(const_in, pool_ready, bf_ready)
        A.after(bcol_ready, const_in)
        PO.after(pool_ready)
        V.after(bcol_ready)

        st = {}

        def at_start():
            now = {"V": V.here(), "A": A.here(), "PE": PE.here(), "PO": PO.here()}
            V.after(now["A"], now["PE"], now["PO"])
            A.after(now["V"], now["PE"], now["PO"])
            PE.after(now["V"], now["A"], now["PO"])
            PO.after(now["V"], now["A"], now["PE"])

        def rstd(ready, src, n, eps):
            t = PO.done(PO.plain(ready).tensor_scalar(va[:], src, 1.0 / n, eps, ALU.mult, ALU.add))
            return PO.done(PO.after(t).tensor_tensor(rs[:], va[:], mhalf[:, 0:CT], ALU.pow))

        def sum_squares(src, *ready):
            t = V.done(V.after(*ready).tensor_tensor(sq[:], src, src, ALU.mult))
            return V.done(V.after(t).tensor_reduce(ss[:], sq[:], AX.X, ALU.add))

        def scaled(dst, src, col, *ready):
            return V.done(V.after(*ready).tensor_tensor(
                dst, src, col.unsqueeze(2).broadcast_to([P, CT, D]), ALU.mult))

        def rms_norm(src, eps, *ready):
            t = sum_squares(src, *ready)
            t = rstd(t, ss[:], D, eps)
            return scaled(xn[:], src, rs[:], t)

        def transposed(ready, dst=None, scale=None, bias=None, free=()):
            for j in range(CT):
                t = PE.after(*((ready,) + tuple(free) if j == 0 else ())).transpose(
                    PS[:, 0, j * P:(j + 1) * P], xn[:, j, :], ident[:])
            t = PE.done(t)
            if scale is None:
                u = A.done(A.after(t).copy(xT[:], bank(0)))
            else:
                u = A.done(A.after(t).activation(xT[:], bank(0), ACT.Identity, scale=scale, bias=bias))
            return u

        def layer_norm(src, dst, *ready):
            for j in range(CT):
                t = V.done(V.after(*(ready if j == 0 else ())).bn_stats(bn6[:, j, :], src[:, j, :]))
            V.plain(t)
            for j in range(CT):
                t = V.done(nc.vector.bn_aggr(mv[:, j, :], bn6[:, j, :]))
            t = PO.done(PO.plain(t).tensor_scalar(va[:], mv[:, :, 1], 1.0, 1e-5, ALU.mult, ALU.add))
            t = PO.done(PO.after(t).tensor_tensor(rs[:], va[:], mhalf[:, 0:CT], ALU.pow))
            V.after(t)
            for j in range(CT):
                t = V.done(nc.vector.tensor_scalar(dst[:, j, :], src[:, j, :], mv[:, j, 0:1], rs[:, j:j + 1],
                                                   ALU.subtract, ALU.mult))
            return t

        def token_major(ready, lhs, rhs, nf, bk=7):
            PE.after(*ready)
            for j in range(CT):
                for f in range(nf):
                    mm = nc.tensor.matmul(PS[:, bk, j * D:(j + 1) * D], lhs(f, j), rhs(f),
                                          start=(f == 0), stop=(f == nf - 1))
            return PE.done(mm)

        V.after(L[0].here())
        t1 = V.done(nc.vector.tensor_scalar(w_in[:], w_in[:], n1[:, 0:1], None, ALU.mult))
        t2 = V.done(nc.vector.tensor_scalar(w_fc[:], w_fc[:], n2[:, 0:1], None, ALU.mult))
        sb0 = {n: in_zone(512 * i, [S]) for i, n in enumerate((
            "vS", "kS", "aS", "gS", "qsq", "lnm", "rq", "aC", "aM", "aR", "pre", "uu", "mem", "yy", "tq"))}
        t3 = PO.done(nc.gpsimd.memset(sb0["aR"][:], 0.0))
        PE.after(t1, t2, L[0].here())
        V.after(x_in, t3)
        with loop(B, "mixer") as lp:
            at_start()
            Xc = X[:, ds(lp.i * CT, CT), :]
            t = rms_norm(Xc, 1e-6)
            t = transposed(t)
            PE.after(t)
            for n in range(5):
                t = PE.done(nc.tensor.matmul(bank(1 + n), w_in[:, n * D:(n + 1) * D], xT[:], start=True, stop=True))
            q, k, v, a, g = (bank(1 + n) for n in range(5))
            A.after(t)
            vS, kS, aS, gS = (sb0[n] for n in ("vS", "kS", "aS", "gS"))
            t_k = A.done(nc.scalar.activation(kS[:], k, ACT.Tanh))
            t_a = A.done(nc.scalar.activation(aS[:], a, ACT.Sigmoid, bias=bcol["two"][:, 0:1]))
            t_g = A.done(nc.scalar.activation(gS[:], g, ACT.Sigmoid))
            t_v = A.done(nc.scalar.copy(vS[:], v))
            t_q = A.done(nc.scalar.activation(sb0["qsq"][:], q, ACT.Square))
            t = PE.done(PE.after(t_q).matmul(bank(6), consts["headmean"][:], sb0["qsq"][:], start=True, stop=True))
            t = A.done(A.after(t).activation(sb0["lnm"][:], bank(6), ACT.Ln, bias=bcol["eps32"][:, 0:1]))
            t_r = A.done(A.after(t).activation(sb0["rq"][:], sb0["lnm"][:], ACT.Exp, scale=-0.5))
            aC, aM, aR, pre, uu, mem = (sb0[n] for n in ("aC", "aM", "aR", "pre", "uu", "mem"))
            heads = lambda x: x[:].rearrange("p (c s) -> p c s", s=SCAN)[:, :, 0:1]
            t_u = V.done(V.after(t_k, t_v).tensor_tensor(uu[:], kS[:], vS[:], ALU.mult))
            t = V.done(V.after(t_a).tensor_scalar(aC[:], aS[:], 0.6, 0.9995, ALU.max, ALU.min))
            V.after(t)
            V.done(nc.vector.tensor_copy(aM[:], aC[:]))
            t = V.done(nc.vector.tensor_copy(heads(aR), heads(aC)))
            t = V.done(V.after(t).memset(heads(aM), 0.0))
            t = V.done(V.after(t).tensor_tensor_scan(pre[:], aM[:], aR[:], 0.0, ALU.mult, ALU.add))
            t = V.done(V.after(t).tensor_scalar(pre[:], pre[:], 1e6, 1.0, ALU.mult, ALU.min))
            t = V.done(V.after(t, t_u).tensor_tensor(uu[:], uu[:], pre[:], ALU.mult))
            t = V.done(V.after(t).tensor_tensor_scan(mem[:], aC[:], uu[:], 0.0, ALU.mult, ALU.add))
            yy, tq = sb0["yy"], sb0["tq"]
            t2 = V.done(V.after(t_r, t_q).tensor_tensor(tq[:], q, sb0["rq"][:], ALU.mult))
            t = V.done(V.after(t, t2).tensor_tensor(yy[:], tq[:], mem[:], ALU.mult))
            t = V.done(V.after(t).tensor_tensor(yy[:], yy[:], vS[:], ALU.subtract))
            t = V.done(V.after(t, t_g).tensor_tensor(yy[:], yy[:], gS[:], ALU.mult))
            t = V.done(V.after(t).tensor_tensor(yy[:], yy[:], vS[:], ALU.add))
            t = token_major((t,), lambda f, j: yy[:, j * P:(j + 1) * P], lambda f: w_out0[:], 1)
            t = V.done(V.after(t).scalar_tensor_tensor(x1[:], chunk(7), RES, Xc, ALU.mult, ALU.add))
            t = rms_norm(x1[:], 1e-6, t)
            t = transposed(t)
            PE.after(t)
            for n in range(4):
                t = PE.done(nc.tensor.matmul(bank(1 + n), w_fc[:, n * P:(n + 1) * P], xT[:], start=True, stop=True))
                t_h = A.done(A.after(t).activation(hT[:, n, :], bank(1 + n), ACT.Silu))
            t = token_major((t_h,), lambda f, j: hT[:, f, j * P:(j + 1) * P], lambda f: w_pr[:, f, :], 4)
            t = V.done(V.after(t).scalar_tensor_tensor(tot[:], chunk(7), RES, x1[:], ALU.mult, ALU.add))
            t = V.done(V.after(t).tensor_tensor(tot[:], tot[:], Xc, ALU.add))
            layer_norm(tot, Xc, t)

        wt = sb("wt", [P, 512])
        wt2 = sb("wt2", [P, 512])
        wsum = sb("wsum", [P, 1])
        thr = sb("thr", [P, 2])
        V.after(L[1].here())
        PE.after(L[1].here())
        for w in (w_up[:], flat(w_dn[:])):
            t = V.done(V.after(V.here()).tensor_reduce(wsum[:], w, AX.X, ALU.add, apply_absolute_value=True))
            t = PE.done(PE.after(t, V.here()).matmul(PS[:, 6, 0:1], ones[:], wsum[:], start=True, stop=True))
            t = V.done(V.after(t).tensor_scalar(thr[:, 0:1], PS[:, 6, 0:1], 0.5 / (D * 512), None, ALU.mult))
            t = V.done(V.after(t).tensor_scalar(thr[:, 1:2], thr[:, 0:1], -1.0, None, ALU.mult))
            V.after(t)
            V.done(nc.vector.tensor_scalar(wt[:], w, thr[:, 0:1], None, ALU.is_gt))
            t = V.done(nc.vector.tensor_scalar(wt2[:], w, thr[:, 1:2], None, ALU.is_lt))
            t = V.done(V.after(t).tensor_tensor(wt[:], wt[:], wt2[:], ALU.subtract))
            t = V.done(V.after(t).tensor_tensor(wt[:], wt[:], w, ALU.subtract))
            t_w = V.done(V.after(t).tensor_tensor(w, w, wt[:], ALU.add))
        PE.after(t_w)
        ssp = sb("ssp", [P, CT])
        hsq = in_zone(0, [4, S])
        with loop(B, "ternary") as lp:
            at_start()
            Xc = X[:, ds(lp.i * CT, CT), :]

            def inv_rms(ready, src, n):
                t = PO.done(PO.plain(ready).tensor_scalar(va[:], src, 1.0 / n, 0.0, ALU.mult, ALU.add))
                t = PO.done(PO.after(t).tensor_tensor(rs[:], va[:], half[:, 0:CT], ALU.pow))
                t = PO.done(PO.plain(t).tensor_scalar(va[:], rs[:], 1.0, 1e-8, ALU.mult, ALU.add))
                return V.done(V.after(t).reciprocal(rs[:], va[:]))

            t = sum_squares(Xc)
            t = inv_rms(t, ss[:], D)
            t = scaled(xn[:], Xc, rs[:], t)
            t = transposed(t)
            PE.after(t)
            for n in range(4):
                t = PE.done(nc.tensor.matmul(bank(1 + n), w_up[:, n * P:(n + 1) * P], xT[:], start=True, stop=True))
                t_h = A.done(A.after(t).activation(hT[:, n, :], bank(1 + n), ACT.Gelu))
            t_s = A.done(A.after(t_h).activation(hsq[:], hT[:], ACT.Square))
            t_o = token_major((t_h,), lambda f, j: hT[:, f, j * P:(j + 1) * P], lambda f: w_dn[:, f, :], 4)
            PE.after(t_s)
            for j in range(CT):
                for f in range(4):
                    mm = nc.tensor.matmul(PS[:, 6, j:j + 1], hsq[:, f, j * P:(j + 1) * P], ones[:, 0:1],
                                          start=(f == 0), stop=(f == 3))
            t = PE.done(mm)
            t = V.done(V.after(t).tensor_copy(ssp[:], PS[:, 6, 0:CT]))
            t = inv_rms(t, ssp[:], 512)
            V.after(t, t_o)
            for j in range(CT):
                t = V.done(nc.vector.scalar_tensor_tensor(tot[:, j, :], chunk(7)[:, j, :], rs[:, j:j + 1],
                                                          X[:, ds(lp.i * CT + j, 1), :].rearrange("p a d -> p (a d)"),
                                                          ALU.mult, ALU.add))
            layer_norm(tot, Xc, t)


        scratch = nc.dram_tensor("score_parts", (2, B * G, 3, HD * R, S), BF16, kind="Internal").ap()
        parts = sb("parts", [P, 2, 3, S], BF16)
        qkf = in_zone(8192, [2, S])
        qkr = in_zone(9216, [2, S])
        Vt = sb("Vt", [P, B * G, CT, R, HD + 1])
        O = sb("O", [P, B * G, CT, R, HD])
        NB = 4
        OQ = in_zone(0, [NB, R, S], BF16, 96)
        OK = in_zone(4096, [NB, R, S], BF16, 96)
        VS = sb("VS", [P, NB, CT, R, 32])
        PB = in_zone(8192, [2, R, S])
        oT = sb("oT", [P, S])
        negm = sb("negm", [P, R * CT])
        nmp = sb("nmp", [P, 2, R * CT], BF16)
        mT = sb("mT", [32, NB, P], BF16)
        rden = sb("rden", [P, R * CT])
        OPER = [dma(f"operand{i}") for i in range(NB)]
        MROW = [dma(f"mrow{i}") for i in range(NB)]
        for t in OPER + MROW:
            t.engine.sem_inc(t.sem, t.step)
            tracks.append(t)
        t_vt = PO.done(nc.gpsimd.memset(Vt[:], 1.0))
        t_vs = PO.done(nc.gpsimd.memset(VS[:], 0.0))
        V.after(t_vt)
        PO.after(t_vt, t_vs)
        rows16 = nc.dram_tensor("rows16", (2, NLIN + 2, S), BF16, kind="Internal").ap()
        CAST.done(nc.gpsimd.dma_start(rows16[0], args["c_rows_q"]))
        t_rows16 = CAST.done(nc.gpsimd.dma_start(rows16[1], args["c_rows_k"]))
        ROWS.plain(t_rows16)

        def constant_rows(lin):
            KR = NCOMBO + (NLIN if lin else 0)
            ROWS.plain(PE.here(), V.here(), A.here())
            for dst, src in ([(OQ[NCOMBO:KR], rows16[0, 0:NLIN]), (OK[NCOMBO:KR], rows16[1, 0:NLIN])] if lin else []) + [
                    (OK[KR:KR + 2], rows16[1, NLIN:NLIN + 2])]:
                ROWS.done(nc.sync.dma_start(dst.rearrange("p s r q -> p (s r) q"),
                                            src.unsqueeze(1).broadcast_to([src.shape[0], NB * R, S])))

        def attention_prep(name, wq, wk, wv, qs, qb=None, kb=None, vb=None):
            with loop(B, name + "_prep") as lp:
                at_start()
                SPILL.plain(V.here())
                V.after(SPILL.here())
                A.after(SPILL.here())
                Xc = X[:, ds(lp.i * CT, CT), :]
                t = A.done(nc.scalar.copy(xn[:], Xc))
                t = transposed(t)
                PE.after(t)
                for n, w in enumerate((wq, wk)):
                    t = PE.done(nc.tensor.matmul(bank(1 + n), w, xT[:], start=True, stop=True))
                t_v = token_major((), lambda f, j: xT[:, j * P:(j + 1) * P], lambda f: wv, 1)
                A.after(t)
                for n, (sc, bi) in enumerate(((qs, qb), (1.0, kb))):
                    bi = 0.0 if bi is None else bi
                    nc.scalar.activation(parts[:, n, 0, :], bank(1 + n), ACT.Identity, scale=sc, bias=bi)
                    t = A.done(nc.scalar.activation(qkf[:, n, :], bank(1 + n), ACT.Identity, scale=sc, bias=bi))
                t = V.done(V.after(t).tensor_tensor(qkr[:], qkf[:], parts[:, :, 0, :], ALU.subtract))
                t = V.done(V.after(t).tensor_copy(parts[:, :, 1, :], qkr[:]))
                t = V.done(V.after(t).tensor_tensor(parts[:, :, 2, :], qkr[:], parts[:, :, 1, :], ALU.subtract))
                SPILL.plain(t)
                for n in range(2):
                    for g in range(G):
                        SPILL.done(nc.sync.dma_start(
                            scratch[n, ds(lp.i * G + g, 1)].rearrange("a i x q -> x (a i) q"),
                            parts[32 * g:32 * g + 32, n]))
                V.after(t_v)
                for j in range(CT):
                    o = Vt[:, ds(lp.i * G, G), j, :, 0:HD]
                    i_ = chunk(7)[:, j, :].rearrange("p (g r d) -> p g r d", g=G, r=R)
                    if vb is None:
                        V.done(nc.vector.tensor_copy(o, i_))
                    else:
                        V.done(nc.vector.tensor_tensor(o, i_, vb.rearrange("p (g r d) -> p g r d", g=G, r=R), ALU.add))

        def attention(name, causal=False, diag_kq=None, diag_qk=None, slope=None, void=None, lin=False):
            KR = NCOMBO + (NLIN if lin else 0)
            KM = KR + 2
            spilled = SPILL.here()
            PE.after(ROWS.here())
            last = {}

            def ring_slot():
                n = last["ring"]
                last["ring"] = n + 1
                PE.after(last[("ring", n % 3)])
                return n % 3

            def load(u, s):
                T = OPER[s]
                T.plain(last[("oper", s)], spilled)
                unit = scratch[:, ds(u, 1)] if not isinstance(u, int) else scratch[:, u:u + 1]
                T.done(nc.sync.dma_start(
                    OQ[0:NCOMBO, s].rearrange("a r q -> a (r q)"),
                    unit[0].rearrange("o i (a r) q -> o (i a) (r q)", r=R).broadcast_to([3, 3 * HD, R * S])))
                for j in range(3):
                    t = T.done(nc.sync.dma_start(
                        OK[24 * j:24 * j + 24, s].rearrange("a r q -> a (r q)"),
                        unit[1, :, j].rearrange("o (a r) q -> o a (r q)", r=R).broadcast_to([3, HD, R * S])))
                last[("loaded", s)] = t

            def load_values(u, s):
                src = Vt[:, ds(u, 1)] if not isinstance(u, int) else Vt[:, u:u + 1]
                PO.after(last[("vs", s)])
                for kt in range(CT):
                    t = PO.done(nc.gpsimd.tensor_copy(VS[:, s, kt, :, 0:HD + 1],
                                                      src[:, :, kt].rearrange("p a r d -> p (a r) d")))
                last[("vs_in", s)] = t

            def max_slot(s, n):
                qt, r = n // R, n % R
                b = ring_slot()
                if n == 0:
                    PE.after(last[("loaded", s)])
                nk = (qt + 1) * P if causal else S
                diag = diag_qk is not None
                mm = nc.tensor.matmul(PS[:, b, 0:nk], OQ[0:KR, s, r, qt * P:(qt + 1) * P], OK[0:KR, s, r, 0:nk],
                                      start=True, stop=True)
                if diag:
                    mm = nc.tensor.matmul(PS[:, b, qt * P:(qt + 1) * P], bf["ident"][:], diag_qk[:],
                                          start=False, stop=True, skip_group_check=True)
                t = PE.done(mm)
                k = r * CT + qt
                t = V.done(V.after(t, last["nmp"] if n == 0 else None).tensor_reduce(
                    negm[:, k:k + 1], PS[:, b, 0:nk], AX.X, ALU.max, negate=True))
                last[("ring", b)] = t
                return t

            def max_void(s, g):
                b = ring_slot()
                for r in range(R):
                    for qt in range(CT):
                        k = r * CT + qt
                        mm = nc.tensor.matmul(PS[:, b, k:k + 1], OQ[0:KR, s, r, qt * P:(qt + 1) * P],
                                              void[0][0:KR, g, r, 0:1], start=True, stop=True, skip_group_check=True)
                t = PE.done(mm)
                t = V.done(V.after(t).tensor_scalar(rden[:], PS[:, b, 0:16], -1.0, None, ALU.mult))
                last[("ring", b)] = t
                return V.done(V.after(t, V.here()).tensor_tensor(negm[:], negm[:], rden[:], ALU.min))

            def max_rows(s, t):
                t = V.done(V.after(t, last["nmp_pe"]).tensor_copy(nmp[:, 0, :], negm[:]))
                t = V.done(V.after(t).tensor_tensor(nmp[:, 1, :], negm[:], nmp[:, 0, :], ALU.subtract))
                last["nmp"] = t
                b = ring_slot()
                pt = PS[0:32, b, 0:64].bitcast(BF16)
                t = PE.done(PE.after(t).transpose(pt, nmp[:].rearrange("p a b -> p (a b)"), bf["ident"][:]))
                last["nmp_pe"] = t
                t = V.done(V.after(t, last[("mrow", s)]).tensor_copy(mT[:, s, :], pt))
                last[("ring", b)] = t
                MROW[s].plain(t, last[("oper", s)])
                for i in range(2):
                    t = MROW[s].done(nc.sync.dma_start(
                        OQ[KR + i:KR + i + 1, s].rearrange("a r (t q) -> a (r t) q", t=CT), mT[16 * i:16 * i + 16, s, :]))
                last[("mrow", s)] = t

            def scores(s, kt, rp):
                q0 = kt * P if causal else 0
                if kt == 0 and rp == 0:
                    PE.after(last[("mrow", s)])
                PE.after(last[("pair", rp)])
                for r in (2 * rp, 2 * rp + 1):
                    b = 3 + r
                    diag = diag_kq is not None
                    mm = nc.tensor.matmul(PS[:, b, q0:S], OK[0:KM, s, r, kt * P:(kt + 1) * P], OQ[0:KM, s, r, q0:S],
                                          start=True, stop=True)
                    if diag:
                        mm = nc.tensor.matmul(PS[:, b, kt * P:(kt + 1) * P], bf["ident"][:], diag_kq[:],
                                              start=False, stop=True, skip_group_check=True)
                t = PE.done(mm)
                if kt == CT - 1 and rp == 1 and void is None:
                    last[("oper", s)] = t
                A.after(t, last[("pb", kt % 2)])
                if slope is None:
                    t = A.done(nc.scalar.activation(PB[:, kt % 2, 2 * rp:2 * rp + 2, q0:S],
                                                    PS[:, 3 + 2 * rp:5 + 2 * rp, q0:S], ACT.Exp))
                else:
                    for r in (2 * rp, 2 * rp + 1):
                        t = A.done(nc.scalar.activation(PB[:, kt % 2, r, q0:S], PS[:, 3 + r, q0:S], ACT.Exp,
                                                        scale=slope(s, r)))
                last[("pair", rp)] = t
                last[("exp", kt)] = t

            def values(s, kt):
                q0 = kt * P if causal else 0
                PE.after(last[("exp", kt)])
                if kt == 0:
                    PE.after(last["acc"], last[("vs_in", s)])
                for r in range(R):
                    mm = nc.tensor.matmul(PS[32 * r:32 * r + 32, 7, q0:S], VS[:, s, kt, r, :], PB[:, kt % 2, r, q0:S],
                                          start=(kt == 0), stop=True, skip_group_check=True)
                t = PE.done(mm)
                last[("pb", kt % 2)] = t
                last[("vs", s)] = t
                last["acc_in"] = t

            def void_key(s, g):
                PE.after(last[("pair", 0)])
                for r in range(R):
                    mm = nc.tensor.matmul(PS[32 * r:32 * r + 32, 3, :], void[0][0:KM, g, r, :], OQ[0:KM, s, r, :],
                                          start=True, stop=True, skip_group_check=True)
                t = PE.done(mm)
                last[("oper", s)] = t
                t = A.done(A.after(t, last["pvo"]).activation(pvo[:], bank(3), ACT.Exp))
                last[("pair", 0)] = t
                last["pvo_in"] = t

            def void_value(g):
                t = PE.done(PE.after(last["pvo_in"]).matmul(bank(7), void[1][:, g, :], pvo[:], start=False, stop=True,
                                                            skip_group_check=True))
                last["pvo"] = t
                last["acc_in"] = t

            def evacuate():
                t = A.done(A.after(last["acc_in"], last["oT"]).copy(oT[:], bank(7)))
                last["acc"] = t
                last["oT_in"] = t

            def normalise(u):
                b = ring_slot()
                PE.after(last["oT_in"])
                for j in range(CT):
                    mm = nc.tensor.transpose(PS[:, b, j * P:(j + 1) * P], oT[:, j * P:(j + 1) * P], ident[:])
                t = PE.done(mm)
                last["oT"] = t
                acc = bank(b).rearrange("p (x d) -> p x d", d=32)
                t = V.done(V.after(t, last["rden"]).reciprocal(rden[:].unsqueeze(2), acc[:, :, HD:HD + 1]))
                dst = O[:, ds(u, 1)].rearrange("p a t r d -> p (a t r) d") if not isinstance(u, int) else \
                    O[:, u].rearrange("p t r d -> p (t r) d")
                t = V.done(V.after(t).tensor_tensor(dst, acc[:, :, 0:HD],
                                                    rden[:].unsqueeze(2).broadcast_to([P, R * CT, HD]), ALU.mult))
                last["rden"] = t
                last[("ring", b)] = t

            def step(s, u_exp=None, u_max=None, u_norm=None, u_load=None, finish=None):
                s2, s0 = (s + 2) % NB, (s - 1) % NB
                if u_load is not None:
                    load(u_load, s0)
                t = None
                for n in range(2 * CT):
                    kt, rp = n // 2, n % 2
                    if u_max is not None:
                        max_slot(s2, 2 * n)
                        t = max_slot(s2, 2 * n + 1)
                    if u_exp is not None:
                        scores(s, kt, rp)
                    if n == 0 and u_norm is not None:
                        values(s0, CT - 1)
                        if void is not None:
                            void_value(s0)
                        evacuate()
                    if n == 0 and u_load is not None:
                        load_values(u_load, s0)
                    if n == 2 and u_norm is not None:
                        normalise(u_norm)
                    if rp == 1 and kt > 0 and u_exp is not None:
                        values(s, kt - 1)
                if u_exp is not None and void is not None:
                    void_key(s, s)
                if u_max is not None:
                    if void is not None:
                        t = max_void(s2, s2)
                    max_rows(s2, t)

            def fresh():
                now = {"V": V.here(), "A": A.here(), "PE": PE.here(), "PO": PO.here()}
                last["ring"] = 0
                for b in range(3):
                    last[("ring", b)] = now["V"]
                for s in range(NB):
                    last[("oper", s)] = now["PE"]
                    last[("vs", s)] = now["PE"]
                    last[("vs_in", s)] = now["PO"]
                    last[("loaded", s)] = OPER[s].here()
                    last[("mrow", s)] = MROW[s].here()
                for b in range(2):
                    last[("pair", b)] = now["A"]
                    last[("pb", b)] = now["PE"]
                for kt in range(CT):
                    last[("exp", kt)] = now["A"]
                last["nmp"] = last["rden"] = now["V"]
                last["nmp_pe"] = now["PE"]
                last["acc"] = last["oT_in"] = last["pvo_in"] = now["A"]
                last["acc_in"] = last["oT"] = last["pvo"] = now["PE"]

            fresh()
            for u in range(2):
                load(u, u)
                load_values(u, u)
            step(NB - 2, u_max=0)
            load(2, 2)
            load_values(2, 2)
            step(NB - 1, u_max=1)
            step(0, u_exp=0, u_max=2, u_load=3)
            with loop(B - 1, name) as lp:
                fresh()
                for g in range(G):
                    u = lp.i * G + (g + 1)
                    step((g + 1) % G, u_exp=u, u_max=u + 2, u_norm=lp.i * G + g if g else lp.i * G, u_load=u + 3)
            fresh()
            for u in range(B * G - 3, B * G):
                step(u % G, u_exp=u, u_max=u + 2 if u + 2 < B * G else None, u_norm=u - 1,
                     u_load=u + 3 if u + 3 < B * G else None)
            step(0, u_norm=B * G - 1)

        def attention_out(name, wo, bias=None):
            with loop(B, name + "_out") as lp:
                at_start()
                Xc = X[:, ds(lp.i * CT, CT), :]
                for j in range(CT):
                    t = V.done(nc.vector.tensor_copy(
                        xn[:, j, :].rearrange("p (g x) -> p g x", g=G),
                        O[:, ds(lp.i * G, G), j].rearrange("p g r d -> p g (r d)")))
                t = transposed(t)
                t = token_major((t,), lambda f, j: xT[:, j * P:(j + 1) * P], lambda f: wo, 1)
                t = V.done(V.after(t).tensor_tensor(tot[:], chunk(7), Xc, ALU.add))
                if bias is not None:
                    t = V.done(V.after(t).tensor_tensor(
                        tot[:], tot[:], bias.unsqueeze(1).broadcast_to([P, CT, D]), ALU.add))
                layer_norm(tot, Xc, t)

        PE.after(L[2].here())
        constant_rows(False)
        attention_prep("a1", wq1[:], wk1[:], wv1[:], HD ** -0.5)
        attention("a1", causal=True, diag_kq=bf["causal_kq"], diag_qk=bf["causal_qk"])
        attention_out("a1", wo1[:])


        LG = sb("LG", [P, NT, E])
        M1 = sb("M1", [P, NT, E])
        M2 = sb("M2", [P, NT, E])
        G2 = sb("G2", [P, NT, E])
        CW = sb("CW", [P, NT, E])
        mk = sb("mk", [P, NT])
        mk2 = sb("mk2", [P, NT])
        M1b = sb("M1b", [P, NT, E], BF16)
        trib, oneb = bf["tri"], onesb

        def col3(c):
            return c[:].unsqueeze(2).broadcast_to([P, NT, E])

        def first_of(dst, src, t):
            t = V.done(V.after(t).tensor_reduce(mk[:], src, AX.X, ALU.max))
            t = V.done(V.after(t).tensor_tensor(dst, src, col3(mk), ALU.is_equal))
            t = V.done(V.after(t).tensor_tensor(dst, dst, rank[:].unsqueeze(1).broadcast_to([P, NT, E]), ALU.mult))
            t = V.done(V.after(t).tensor_reduce(mk[:], dst, AX.X, ALU.max))
            return V.done(V.after(t).tensor_tensor(dst, dst, col3(mk), ALU.is_equal))

        def second_of(t):
            t = V.done(V.after(t).tensor_scalar(G2[:], M1[:], -1.0, 1.0, ALU.mult, ALU.add))
            return V.done(V.after(t).tensor_tensor(G2[:], G2[:], LG[:], ALU.mult))

        def softmax_gates(t):
            t = V.done(V.after(t).tensor_reduce(mk[:], LG[:], AX.X, ALU.max))
            t = V.done(V.after(t).tensor_tensor(LG[:], LG[:], col3(mk), ALU.subtract))
            t = A.done(A.after(t).activation(LG[:], LG[:], ACT.Exp))
            return V.done(V.after(t).tensor_reduce(mk[:], LG[:], AX.X, ALU.add))

        rw1 = load(L[3], "rw1", [P, E], args["L1_ffn_router_w"])
        w1 = load(L[3], "w1", [P, E, 512], args["L1_ffn_w1"].rearrange("e d f -> d e f"))
        w2 = sb("w2", [P, E, 4, D])
        for e in range(E):
            L[3].done(nc.sync.dma_start(w2[:, e], args["L1_ffn_w2"][e].rearrange("(f p) d -> p f d", p=P)))
        b1 = load(L[3], "b1", [P, E, 4], args["L1_ffn_b1"])
        b2 = load(L[3], "b2", [E, D], args["L1_ffn_b2"])
        s1 = load(L[3], "s1", [P, 512], args["L1_ffn_sw1"])
        s2 = load(L[3], "s2", [P, 4, D], args["L1_ffn_sw2"].rearrange("(f p) d -> p f d", p=P))
        sb1 = load(L[3], "sb1", [P, 4], args["L1_ffn_sb1"])
        sb2 = load(L[3], "sb2", [P, D], args["L1_ffn_sb2"].unsqueeze(0).broadcast_to([P, D]))
        yacc = sb("yacc", [P, CT, D])
        cwT = sb("cwT", [E, CT, P])
        PE.after(L[3].here())
        A.after(L[3].here())
        V.after(L[3].here())
        with loop(B, "route1") as lp:
            at_start()
            t = A.done(nc.scalar.copy(xn[:], X[:, ds(lp.i * CT, CT), :]))
            t = transposed(t)
            PE.after(t)
            for j in range(CT):
                mm = nc.tensor.matmul(PS[:, 6, j * E:(j + 1) * E], xT[:, j * P:(j + 1) * P], rw1[:], start=True, stop=True)
            t = PE.done(mm)
            t = V.done(V.after(t).tensor_copy(LG[:, ds(lp.i * CT, CT), :],
                                              PS[:, 6, 0:CT * E].rearrange("p (j e) -> p j e", e=E)))
        t = softmax_gates(t)
        t = V.done(V.after(t).reciprocal(mk2[:], mk[:]))
        t = V.done(V.after(t).tensor_tensor(LG[:], LG[:], col3(mk2), ALU.mult))
        t = first_of(M1[:], LG[:], t)
        t = second_of(t)
        t = first_of(M2[:], G2[:], t)

        def earlier(mask, t):
            t = V.done(V.after(t).tensor_copy(M1b[:], mask))
            PE.after(t)
            pos = PS[:, 6, 0:NT * E].rearrange("p (j e) -> p j e", e=E)
            mm = nc.tensor.matmul(pos, trib[:], M1b[:], start=True, stop=True)
            for j in range(NT - 1):
                mm = nc.tensor.matmul(pos[:, j + 1:NT], oneb[:], M1b[:, j:j + 1].broadcast_to([P, NT - 1 - j, E]),
                                      start=False, stop=True, skip_group_check=True)
            return mm, pos

        mm, pos = earlier(M1[:], t)
        t = PE.done(mm)
        t = V.done(V.after(t).tensor_scalar(G2[:], pos, float(CAP), None, ALU.is_lt))
        t = V.done(V.after(t).tensor_tensor(M1[:], M1[:], G2[:], ALU.mult))
        mm, pos = earlier(M2[:], t)
        t = PE.done(mm)
        t = V.done(V.after(t).tensor_copy(M1b[:], M1[:]))
        PE.after(t)
        for j in range(NT):
            mm = nc.tensor.matmul(pos, oneb[:], M1b[:, j:j + 1].broadcast_to([P, NT, E]),
                                  start=False, stop=True, skip_group_check=True)
        t = PE.done(mm)
        t = V.done(V.after(t).tensor_scalar(G2[:], pos, float(CAP), None, ALU.is_lt))
        t = V.done(V.after(t).tensor_tensor(M2[:], M2[:], G2[:], ALU.mult))
        t = V.done(V.after(t).tensor_tensor(M1[:], M1[:], LG[:], ALU.mult))
        t = V.done(V.after(t).tensor_tensor(M2[:], M2[:], LG[:], ALU.mult))
        t = V.done(V.after(t).tensor_tensor(CW[:], M1[:], M2[:], ALU.add))
        t = V.done(V.after(t).tensor_reduce(mk[:], CW[:], AX.X, ALU.add))
        t = V.done(V.after(t).tensor_scalar(mk[:], mk[:], EPS32, None, ALU.max))
        t = V.done(V.after(t).reciprocal(mk2[:], mk[:]))
        t_cw = V.done(V.after(t).tensor_tensor(CW[:], CW[:], col3(mk2), ALU.mult))
        V.after(t_cw)
        A.after(t_cw)
        with loop(B, "experts1") as lp:
            at_start()
            Xc = X[:, ds(lp.i * CT, CT), :]
            cw = CW[:, ds(lp.i * CT, CT), :]
            t = A.done(nc.scalar.copy(xn[:], Xc))
            t_x = transposed(t)
            t = A.done(A.after(t).copy(sq[:, :, 0:E], cw))
            PE.after(t)
            for j in range(CT):
                mm = nc.tensor.transpose(PS[0:E, 6, j * P:(j + 1) * P], sq[:, j, 0:E], ident[:])
            t = PE.done(mm)
            t = A.done(A.after(t).copy(cwT[:], PS[0:E, 6, :].rearrange("e (j p) -> e j p", j=CT)))
            t = token_major((t,), lambda f, j: cwT[:, j, :], lambda f: b2[:], 1)
            t = V.done(V.after(t).tensor_tensor(yacc[:], chunk(7), Xc, ALU.add))
            PE.after(t_x)
            t_ev = [None] * 4
            t_h = [None] * 4
            for e in range(E + 1):
                wa = w1[:, e, :] if e < E else s1[:]
                wb = w2[:, e] if e < E else s2[:]
                for n in range(4):
                    u = PE.done(PE.after(t_ev[n]).matmul(bank(1 + n), wa[:, n * P:(n + 1) * P], xT[:], start=True, stop=True))
                    bias = b1[:, e, n:n + 1] if e < E else sb1[:, n:n + 1]
                    t_ev[n] = A.done(A.after(u, PE.here() if e and n == 0 else None).activation(
                        hT[:, n, :], bank(1 + n), ACT.Silu, bias=bias)) if not (e and n == 0) else A.done(
                        A.after(u, t_down).activation(hT[:, n, :], bank(1 + n), ACT.Silu, bias=bias))
                bk = 5 + 2 * (e % 2)
                t_down = token_major((t_ev[3], t), lambda f, j: hT[:, f, j * P:(j + 1) * P], lambda f: wb[:, f, :], 4, bk)
                V.after(t_down)
                if e < E:
                    for j in range(CT):
                        t = V.done(V.after(t).scalar_tensor_tensor(
                            yacc[:, j, :], chunk(bk)[:, j, :], cw[:, j, e:e + 1], yacc[:, j, :], ALU.mult, ALU.add))
                else:
                    t = V.done(V.after(t).tensor_tensor(tot[:], chunk(bk), sb2[:].unsqueeze(1).broadcast_to([P, CT, D]), ALU.add))
                    t = V.done(V.after(t).scalar_tensor_tensor(tot[:], tot[:], 0.1, yacc[:], ALU.mult, ALU.add))
            layer_norm(tot, Xc, t)

        w2qkv = load(L[4], "w2qkv", [P, 3 * D], args["L2_attn_W_qkv"])
        w2p = load(L[4], "w2p", [P, D], args["L2_attn_W_proj"])
        b2q = load(L[4], "b2q", [P, 2], args["L2_attn_b_qk"])
        b2v = load(L[4], "b2v", [P, D], args["L2_attn_b_v"].unsqueeze(0).broadcast_to([P, D]))
        b2p = load(L[4], "b2p", [P, D], args["L2_attn_b_proj"].unsqueeze(0).broadcast_to([P, D]))
        V.after(L[4].here())
        t = V.done(nc.vector.tensor_tensor(b2q[:, 0:1], b2q[:, 0:1], qscale2[:], ALU.mult))
        PE.after(L[4].here())
        A.after(t, L[4].here())
        constant_rows(True)
        attention_prep("a2", w2qkv[:, 0:D], w2qkv[:, D:2 * D], w2qkv[:, 2 * D:], qscale2[:, 0:1],
                       b2q[:, 0:1], b2q[:, 1:2], b2v[:])
        attention("a2", diag_kq=bf["alibi_kq"], diag_qk=bf["alibi_qk"], lin=True,
                  slope=lambda g, r: float(2.0 ** (-0.5 * (g * R + r + 1))))
        attention_out("a2", w2p[:], b2p[:])

        NJ = 8
        win = load(L[5], "win", [P, NJ * P], args["L2_ffn_Win"])
        binr = load(L[5], "binr", [P, NJ], args["L2_ffn_bin_"])
        cw1 = load(L[5], "cw1", [P, NJ], args["L2_ffn_W1"])
        cb1 = load(L[5], "cb1", [P, NJ], args["L2_ffn_b1"])
        cw2 = load(L[5], "cw2", [P, NJ], args["L2_ffn_W2"])
        cb2 = load(L[5], "cb2", [64, 1], args["L2_ffn_b2"])
        wout = load(L[5], "wout", [P, NJ, D], args["L2_ffn_Wout_rep"])
        wout1 = load(L[5], "wout1", [64, D], args["L2_ffn_Wout"])
        bout = load(L[5], "bout", [P, D], args["L2_ffn_bout"].unsqueeze(0).broadcast_to([P, D]))
        h8 = in_zone(0, [NJ, S])
        cb2w = sb("cb2w", [64, P])
        V.after(L[5].here())
        t = V.done(nc.vector.tensor_tensor(binr[:], binr[:], cw1[:], ALU.mult))
        t = V.done(V.after(t).tensor_tensor(cb1[:], cb1[:], binr[:], ALU.add))
        t = V.done(nc.vector.tensor_tensor(wout[:], wout[:], cw2[:].unsqueeze(2).broadcast_to([P, NJ, D]), ALU.mult))
        t = V.done(V.after(t).tensor_copy(cb2w[:], cb2[:].broadcast_to([64, P])))
        t = PE.done(PE.after(t, L[5].here()).matmul(PS[:, 6, 0:D], cb2w[:], wout1[:], start=True, stop=True))
        t = V.done(V.after(t).tensor_tensor(bout[:], bout[:], PS[:, 6, 0:D], ALU.add))
        V.after(t)
        A.after(t, L[5].here())
        with loop(B, "channels") as lp:
            at_start()
            Xc = X[:, ds(lp.i * CT, CT), :]
            t = A.done(nc.scalar.copy(xn[:], Xc))
            t = transposed(t)
            PE.after(t)
            t_ev = {}
            for n in range(NJ):
                u = PE.done(PE.after(t_ev.get(n % 4)).matmul(bank(1 + n % 4), win[:, n * P:(n + 1) * P], xT[:], start=True, stop=True))
                t_ev[n % 4] = A.done(A.after(u).activation(h8[:, n, :], bank(1 + n % 4), ACT.Relu,
                                                           scale=cw1[:, n:n + 1], bias=cb1[:, n:n + 1]))
            t = token_major((t_ev[3],), lambda f, j: h8[:, f, j * P:(j + 1) * P], lambda f: wout[:, f, :], NJ)
            t = V.done(V.after(t).tensor_tensor(tot[:], chunk(7), Xc, ALU.add))
            t = V.done(V.after(t).tensor_tensor(tot[:], tot[:], bout[:].unsqueeze(1).broadcast_to([P, CT, D]), ALU.add))
            layer_norm(tot, Xc, t)

        w3qkv = load(L[6], "w3qkv", [P, 3 * D], args["L3_attn_w_qkv"])
        w3o = load(L[6], "w3o", [P, D], args["L3_attn_w_out"])
        b3o = load(L[6], "b3o", [P, D], args["L3_attn_b_out"].unsqueeze(0).broadcast_to([P, D]))
        tr3 = load(L[6], "tr3", [P, 2], args["L3_attn_trace_tf"])
        vk3 = load(L[6], "vk3", [HD, G * R], args["L3_attn_void_k"])
        vvb = sb("vvb", [P, G, P])
        t = V.done(V.after(V.here()).memset(vvb[:], 0.0))
        L[7].plain(t)
        for g in range(G):
            for r in range(R):
                L[7].done(nc.sync.dma_start(vvb[32 * r:32 * r + 1, g, 32 * r:32 * r + HD], args["L3_attn_void_v"][g * R + r:g * R + r + 1]))
                L[7].done(nc.sync.dma_start(vvb[32 * r:32 * r + 1, g, 32 * r + HD:32 * r + HD + 1], args["c_ident"][0:1, 0:1]))
        V.after(L[6].here())
        q3 = sb("q3", [P, 1])
        t = V.done(nc.vector.tensor_scalar(q3[:], tr3[:, 0:1], -1.0, None, ALU.mult))
        t = V.done(V.after(t).tensor_tensor(q3[:], q3[:], tr3[:, 0:1], ALU.max))
        t = V.done(V.after(t).tensor_tensor(q3[:], q3[:], tr3[:, 1:2], ALU.mult))
        t = V.done(V.after(t).tensor_scalar(q3[:], q3[:], 1.0, 1.0, ALU.add, ALU.max))
        t = V.done(V.after(t).reciprocal(q3[:], q3[:]))
        t_q3 = V.done(V.after(t).tensor_scalar(q3[:], q3[:], D ** -0.5, None, ALU.mult))
        vkp = sb("vkp", [HD, 3, G * R], BF16)
        vkr = sb("vkr", [HD, G * R])
        t = V.done(nc.vector.tensor_copy(vkp[:, 0], vk3[:]))
        t = V.done(V.after(t).tensor_tensor(vkr[:], vk3[:], vkp[:, 0], ALU.subtract))
        t = V.done(V.after(t).tensor_copy(vkp[:, 1], vkr[:]))
        t = V.done(V.after(t).tensor_tensor(vkp[:, 2], vkr[:], vkp[:, 1], ALU.subtract))
        vko = sb("vko", [96, G, R, 32], BF16)
        vkc = sb("vkc", [96, G * R], BF16)
        t2 = V.done(nc.vector.memset(vko[:], 0.0))
        t2 = V.done(nc.vector.memset(vkc[:], 1.0))
        L[8].plain(t, t2)
        for j in range(3):
            for i in range(3):
                u = L[8].done(nc.sync.dma_start(vkc[24 * j + 8 * i:24 * j + 8 * i + 8, :], vkp[:, j]))
        t = V.done(V.after(u).tensor_copy(vko[:, :, :, 0:1], vkc[:].rearrange("p (g r o) -> p g r o", g=G, o=1)))
        pvo = sb("pvo", [P, S])
        PE.after(L[6].here(), L[7].here(), t)
        A.after(t_q3)
        V.after(t)
        constant_rows(False)
        attention_prep("a3", w3qkv[:, 0:D], w3qkv[:, D:2 * D], w3qkv[:, 2 * D:], q3[:, 0:1])
        attention("a3", void=(vko, vvb))
        attention_out("a3", w3o[:], b3o[:])

        rw3 = load(L[7], "rw3", [P, E], args["L3_ffn_router_w"])
        lng = load(L[7], "lng", [P, 2], args["L3_ffn_ln"])
        gu3 = w1
        dn3 = w2[:].rearrange("p e f d -> p (e f d)")[:, 0:E * 2 * D].rearrange("p (e f d) -> p e f d", e=E, f=2)
        L[7].plain(PE.here())
        L[7].done(nc.sync.dma_start(gu3[:], args["L3_ffn_gate_up_w"].rearrange("e d f -> d e f")))
        for e in range(E):
            L[7].done(nc.sync.dma_start(dn3[:, e], args["L3_ffn_down_w"][e].rearrange("(f p) d -> p f d", p=P)))
        xeT = sb("xeT", [P, 2, S])
        selr = sb("selr", [E, E, P])
        L[7].done(nc.sync.dma_start(selr[:], args["c_select"]))
        PE.after(L[7].here())
        A.after(L[7].here())
        V.after(L[7].here())

        def normed_T(lp):
            layer_norm(X[:, ds(lp.i * CT, CT), :], xn, None)
            return transposed(V.here(), scale=lng[:, 0:1], bias=lng[:, 1:2])

        with loop(B, "route3") as lp:
            at_start()
            t = normed_T(lp)
            PE.after(t)
            for j in range(CT):
                mm = nc.tensor.matmul(PS[:, 6, j * E:(j + 1) * E], xT[:, j * P:(j + 1) * P], rw3[:], start=True, stop=True)
            t = PE.done(mm)
            t = V.done(V.after(t).tensor_scalar(LG[:, ds(lp.i * CT, CT), :],
                                                PS[:, 6, 0:CT * E].rearrange("p (j e) -> p j e", e=E),
                                                -10000.0, 10000.0, ALU.max, ALU.min))
        t = softmax_gates(t)
        t = V.done(V.after(t).tensor_scalar(mk[:], mk[:], 1e-8, None, ALU.add))
        t = V.done(V.after(t).reciprocal(mk2[:], mk[:]))
        t = V.done(V.after(t).tensor_tensor(LG[:], LG[:], col3(mk2), ALU.mult))
        t = V.done(V.after(t).tensor_scalar(LG[:], LG[:], 1e-8, 1.0, ALU.max, ALU.min))
        t = first_of(M1[:], LG[:], t)
        t = second_of(t)
        t = first_of(M2[:], G2[:], t)
        t = V.done(V.after(t).tensor_tensor(M1[:], M1[:], M2[:], ALU.add))
        t = V.done(V.after(t).tensor_tensor(CW[:], M1[:], LG[:], ALU.mult))
        V.after(t)
        A.after(t)
        with loop(B, "experts3") as lp:
            at_start()
            Xc = X[:, ds(lp.i * CT, CT), :]
            t = normed_T(lp)
            t_c = A.done(A.after(t).copy(sq[:, :, 0:E], CW[:, ds(lp.i * CT, CT), :]))
            PE.after(t_c)
            for j in range(CT):
                mm = nc.tensor.transpose(PS[0:E, 6, j * P:(j + 1) * P], sq[:, j, 0:E], ident[:])
            t_c = PE.done(mm)
            t_c = A.done(A.after(t_c).copy(cwT[:], PS[0:E, 6, :].rearrange("e (j p) -> e j p", j=CT)))
            t_ev = [None] * 4
            t_bc = t_gu = t_m = t_dn = None
            for e in range(E):
                PE.after(t_c, t_bc)
                u = PE.done(nc.tensor.matmul(bank(5), selr[:, e, :], cwT[:].rearrange("e j p -> e (j p)"), start=True, stop=True))
                t_bc = V.done(V.after(u, t_gu, t).tensor_tensor(xeT[:, e % 2, :], bank(5), xT[:], ALU.mult))
                PE.after(t_bc)
                for n in (0, 2, 1, 3):
                    u = PE.done(PE.after(t_ev[n]).matmul(bank(1 + n), gu3[:, e, n * P:(n + 1) * P], xeT[:, e % 2, :], start=True, stop=True))
                    if n < 2:
                        t_ev[n] = A.done(A.after(u, t_m).activation(hsq[:, n, :], bank(1 + n), ACT.Silu))
                    else:
                        t_ev[n] = V.done(V.after(u, t_ev[n - 2], t_dn).tensor_tensor(
                            hT[:, n - 2, :], bank(1 + n), hsq[:, n - 2, :], ALU.mult))
                t_gu, t_m = u, t_ev[3]
                PE.after(t_ev[2], t_ev[3])
                for f in range(2):
                    for j in range(CT):
                        mm = nc.tensor.matmul(PS[:, 7, j * D:(j + 1) * D], hT[:, f, j * P:(j + 1) * P], dn3[:, e, f, :],
                                              start=(e == 0 and f == 0 and j == 0), stop=True, skip_group_check=True)
                t_dn = PE.done(mm)
            t = V.done(V.after(t_dn).tensor_tensor(tot[:], chunk(7), Xc, ALU.add))
            t = V.done(V.after(t).tensor_tensor(tot[:], tot[:], Xc, ALU.add))
            layer_norm(tot, Xc, t)

        OUT.plain(V.here())
        for b in range(B):
            t = OUT.done(nc.sync.dma_start(out[b].rearrange("(j p) d -> p j d", p=P), X[:, b * CT:(b + 1) * CT, :]))
        nc.sync.wait_ge(OUT.sem, t.value())


def layout(x):
    f = np.float32
    a = {k: np.ascontiguousarray(v) for k, v in x.items()}
    o = {"x": a["L0_attn_x"]}
    for n in ("L0_attn_in_proj_w", "L0_attn_out_proj_w", "L0_attn_fc_w", "L0_attn_proj_w", "L0_ffn_w_up", "L0_ffn_w_down"):
        o[n] = np.ascontiguousarray(a[n].T)
    for n in ("L0_attn_norm1_w", "L0_attn_norm2_w"):
        o[n] = a[n].reshape(D, 1)
    perm = np.arange(D).reshape(G, R, HD).transpose(0, 2, 1).reshape(-1)
    for n in ("q_heads", "k_heads"):
        o["L1_attn_" + n] = np.ascontiguousarray(a["L1_attn_" + n].T[:, perm])
    for n in ("v_heads", "output_proj"):
        o["L1_attn_" + n] = np.ascontiguousarray(a["L1_attn_" + n].T)
    for n in ("router_w", "w1", "w2", "b2", "sw1", "sw2", "sb2"):
        o["L1_ffn_" + n] = a["L1_ffn_" + n]
    o["L1_ffn_b1"] = np.ascontiguousarray(a["L1_ffn_b1"].reshape(E, 4, P).transpose(2, 0, 1))
    o["L1_ffn_sb1"] = np.ascontiguousarray(a["L1_ffn_sb1"].reshape(4, P).T)
    w, b = a["L2_attn_W_qkv"], a["L2_attn_b_qkv"]
    o["L2_attn_W_qkv"] = np.ascontiguousarray(np.concatenate([w[:, 0:D][:, perm], w[:, D:2 * D][:, perm], w[:, 2 * D:]], 1))
    o["L2_attn_b_qk"] = np.ascontiguousarray(np.stack([b[0:D][perm], b[D:2 * D][perm]], 1))
    o["L2_attn_b_v"] = np.ascontiguousarray(b[2 * D:])
    o["L2_attn_W_proj"], o["L2_attn_b_proj"] = a["L2_attn_W_proj"], a["L2_attn_b_proj"]
    per = lambda v: np.ascontiguousarray(v.reshape(8, P).T)
    o["L2_ffn_Win"] = np.repeat(a["L2_ffn_Win"], 16, axis=1)
    o["L2_ffn_bin_"] = per(np.repeat(a["L2_ffn_bin_"], 16))
    for n in ("W1", "b1", "W2"):
        o["L2_ffn_" + n] = per(a["L2_ffn_" + n])
    o["L2_ffn_b2"] = a["L2_ffn_b2"].reshape(64, 1)
    o["L2_ffn_Wout"] = a["L2_ffn_Wout"]
    o["L2_ffn_Wout_rep"] = np.ascontiguousarray(np.repeat(a["L2_ffn_Wout"], 16, axis=0).reshape(8, P, D).transpose(1, 0, 2))
    o["L2_ffn_bout"] = a["L2_ffn_bout"]
    w = a["L3_attn_w_qkv"]
    o["L3_attn_w_qkv"] = np.ascontiguousarray(np.concatenate([w[:, 0:D][:, perm], w[:, D:2 * D][:, perm], w[:, 2 * D:]], 1))
    o["L3_attn_w_out"], o["L3_attn_b_out"] = a["L3_attn_w_out"], a["L3_attn_b_out"]
    head = perm // HD
    o["L3_attn_trace_tf"] = np.ascontiguousarray(np.stack(
        [a["L3_attn_attention_trace"].reshape(H)[head], a["L3_attn_temperature_factor"].reshape(H)[head]], 1))
    o["L3_attn_void_k"] = np.ascontiguousarray(a["L3_attn_void_k"].reshape(H, HD).T)
    o["L3_attn_void_v"] = a["L3_attn_void_v"].reshape(H, HD)
    o["L3_ffn_router_w"] = np.ascontiguousarray(a["L3_ffn_router_w"].T)
    o["L3_ffn_ln"] = np.ascontiguousarray(np.stack([a["L3_ffn_ln_gamma"], a["L3_ffn_ln_beta"]], 1))
    o["L3_ffn_gate_up_w"] = np.ascontiguousarray(a["L3_ffn_gate_up_w"].transpose(0, 2, 1))
    o["L3_ffn_down_w"] = np.ascontiguousarray(a["L3_ffn_down_w"].transpose(0, 2, 1))
    i = np.arange(P)
    o["c_select"] = np.ascontiguousarray(np.repeat(np.eye(E, dtype=f)[:, :, None], P, axis=2))
    k, q = i[:, None], i[None, :]
    o["c_ident"] = np.eye(P, dtype=f)
    o["c_causal_kq"] = np.where(k > q, NEG, 0).astype(f)
    o["c_causal_qk"] = np.ascontiguousarray(o["c_causal_kq"].T)
    o["c_alibi_kq"] = np.minimum(k - q, 0).astype(f)
    o["c_alibi_qk"] = np.ascontiguousarray(o["c_alibi_kq"].T)
    o["c_headmean"] = np.where(k // HD == q // HD, 1.0 / HD, 0).astype(f)
    o["c_tri"] = (k < q).astype(f)
    o["c_rank"] = np.tile(E - np.arange(E), (P, 1)).astype(f)
    slope = 2.0 ** (-0.5 * (np.arange(H) + 1))
    o["c_slopes"] = np.tile(slope, (P, 1)).astype(f)
    o["c_qscale2"] = (HD ** -0.5 / slope[perm // HD]).reshape(D, 1).astype(f)
    pos = np.arange(S)
    rk, rq = np.zeros((NLIN + 2, S), f), np.zeros((NLIN + 2, S), f)
    for s in range(3):
        own, behind = pos // P == s, pos // P > s
        rk[3 * s][own], rk[3 * s + 1][own], rk[3 * s + 2][own] = pos[own] % P, 1, 1
        rq[3 * s][behind], rq[3 * s + 1][behind] = 1, -(pos[behind] % P)
        rq[3 * s + 2][behind] = -P * (pos[behind] // P - s)
    rk[NLIN:] = 1
    o["c_rows_k"], o["c_rows_q"] = rk, rq
    return o


def kernel(**inputs):
    import concourse.bacc as bacc
    from concourse.bass_utils import run_bass_kernel_spmd

    nc = bacc.Bacc("TRN2", target_bir_lowering=False, num_devices=1)
    arrays, args = {}, {}
    for name, a in layout(inputs).items():
        arrays["in_" + name] = a
        args[name] = nc.dram_tensor("in_" + name, a.shape, mybir.dt.from_np(a.dtype), kind="ExternalInput").ap()
    out = nc.dram_tensor("out_0", (B, S, D), F32, kind="ExternalOutput").ap()
    build_program(nc, args, out)
    r = run_bass_kernel_spmd(nc, [arrays], core_ids=[0])
    return r.results[0]["out_0"]
```

```python
from contextlib import ExitStack, contextmanager

import numpy as np

import concourse.bass as bass
from concourse import mybir

F32 = mybir.dt.float32
BF16 = mybir.dt.bfloat16
ALU = mybir.AluOpType
ACT = mybir.ActivationFunctionType
AX = mybir.AxisListType
ds = bass.ds

P = 128
D = 128
B, S = 4, 512
NT = B * S // P
CT = S // P
H, HD = 16, 8
G, R = 4, 4
E = 8
SCAN = 64
CAP = 640
RES = float(1.0 / np.sqrt(2.0))
EPS32 = float(np.finfo(np.float32).eps)
NEG = -1.0e30
NCOMBO = 72
NLIN = 9


class Track:

    def __init__(self, name, engine, sem, step=1):
        self.name, self.engine, self.sem, self.step = name, engine, sem, step
        self.count = step
        self.gate = None

    def done(self, instruction):
        instruction.then_inc(self.sem, self.step)
        self.count += self.step
        return Token(self, self.count, tuple(LOOPS))

    def here(self):
        return Token(self, self.count, tuple(LOOPS))

    def after(self, *tokens):
        for t in tokens:
            if t is not None:
                self.engine.wait_ge(t.track.sem, t.value())
        return self.engine

    def plain(self, *tokens):
        self.after(*tokens)
        self.engine.sem_inc(self.gate, 1)
        return self.engine


LOOPS = []


class Token:
    def __init__(self, track, count, loops):
        self.track, self.count, self.loops = track, count, loops

    def value(self):
        v = self.count
        for loop in self.loops:
            per = loop.per.get(self.track.name, 0)
            if loop in LOOPS:
                if per:
                    v = loop.i * per + v
            else:
                v = v + (loop.n - 1) * per
        return v


PER = {
 'mixer': {'vector': 70, 'scalar': 26, 'tensor': 28, 'gpsimd': 12, 'lane0': 1, 'lane1': 1},
 'ternary': {'vector': 44, 'scalar': 12, 'tensor': 14, 'gpsimd': 16, 'lane0': 1, 'lane1': 1},
 'a1_prep': {'vector': 14, 'scalar': 8, 'tensor': 8, 'spill0': 96, 'spill1': 96, 'lane0': 1, 'lane1': 1},
 'a1': {'vector': 84,
        'scalar': 36,
        'tensor': 120,
        'gpsimd': 16,
        'operand0': 64,
        'operand1': 64,
        'operand2': 64,
        'operand3': 64,
        'mrow0': 32,
        'mrow1': 32,
        'mrow2': 32,
        'mrow3': 32},
 'a1_out': {'vector': 34, 'scalar': 2, 'tensor': 4, 'gpsimd': 4, 'lane0': 1, 'lane1': 1},
 'route1': {'vector': 2, 'scalar': 4, 'tensor': 4, 'lane0': 1, 'lane1': 1},
 'experts1': {'vector': 94, 'scalar': 80, 'tensor': 96, 'gpsimd': 4, 'lane0': 1, 'lane1': 1},
 'a2_prep': {'vector': 14, 'scalar': 8, 'tensor': 8, 'spill0': 96, 'spill1': 96, 'lane0': 1, 'lane1': 1},
 'a2': {'vector': 84,
        'scalar': 68,
        'tensor': 120,
        'gpsimd': 16,
        'operand0': 64,
        'operand1': 64,
        'operand2': 64,
        'operand3': 64,
        'mrow0': 32,
        'mrow1': 32,
        'mrow2': 32,
        'mrow3': 32},
 'a2_out': {'vector': 36, 'scalar': 2, 'tensor': 4, 'gpsimd': 4, 'lane0': 1, 'lane1': 1},
 'channels': {'vector': 28, 'scalar': 20, 'tensor': 20, 'gpsimd': 4, 'lane0': 1, 'lane1': 1},
 'a3_prep': {'vector': 14, 'scalar': 8, 'tensor': 8, 'spill0': 96, 'spill1': 96, 'lane0': 1, 'lane1': 1},
 'a3': {'vector': 92,
        'scalar': 40,
        'tensor': 132,
        'gpsimd': 16,
        'operand0': 64,
        'operand1': 64,
        'operand2': 64,
        'operand3': 64,
        'mrow0': 32,
        'mrow1': 32,
        'mrow2': 32,
        'mrow3': 32},
 'a3_out': {'vector': 36, 'scalar': 2, 'tensor': 4, 'gpsimd': 4, 'lane0': 1, 'lane1': 1},
 'route3': {'vector': 26, 'scalar': 2, 'tensor': 4, 'gpsimd': 4, 'lane0': 1, 'lane1': 1},
 'experts3': {'vector': 100, 'scalar': 38, 'tensor': 100, 'gpsimd': 8, 'lane0': 1, 'lane1': 1}}


class Loop:
    def __init__(self, nc, tracks, n, name):
        self.nc, self.tracks, self.n, self.name, self.per = nc, tracks, n, name, PER.get(name, {})

    @contextmanager
    def run(self):
        with self.nc.Fori(0, self.n) as i:
            self.i = i
            self.start = {t.name: t.count for t in self.tracks}
            LOOPS.append(self)
            yield self
            LOOPS.pop()
        got = {t.name: t.count - self.start[t.name] for t in self.tracks if t.count != self.start[t.name]}
        assert got == self.per, f"{self.name}: a turn counts {got}"
        for t in self.tracks:
            t.count += (self.n - 1) * self.per.get(t.name, 0)


def build_program(nc, args, out):
    ctx = ExitStack()
    with ctx:
        def sb(name, shape, dt=F32):
            return ctx.enter_context(nc.sbuf_tensor(name, shape, dt))

        def sem(name):
            return ctx.enter_context(nc.semaphore(name))

        V = Track("vector", nc.vector, sem("vector"))
        A = Track("scalar", nc.scalar, sem("scalar"))
        PE = Track("tensor", nc.tensor, sem("tensor"))
        PO = Track("gpsimd", nc.gpsimd, sem("gpsimd"))

        PE.gate, A.gate = sem("tensor_gate"), sem("scalar_gate")
        V.gate, PO.gate = sem("vector_gate"), sem("gpsimd_gate")
        sync_gate = sem("sync_gate")
        dma_tracks = []

        def dma(name, engine=None):
            t = Track(name, engine or nc.sync, sem("dma_" + name), 16)
            t.gate = sync_gate
            dma_tracks.append(t)
            return t

        LD0 = [dma(f"load{i}") for i in range(9)]
        CONST = dma("const")
        SPILLS = [dma("spill0"), dma("spill1")]
        ROWS = dma("rows")
        CAST = dma("cast", nc.gpsimd)
        OUT = dma("out")
        tracks = [V, A, PE, PO] + dma_tracks
        CAST.count = 0
        for t in tracks:
            if t is not CAST:
                t.engine.sem_inc(t.sem, t.step)

        def loop(n, name):
            return Loop(nc, tracks, n, name).run()

        X = sb("X", [P, NT, D])
        zone = sb("zone", [P, 12288])

        def in_zone(at, shape, dt=F32, parts=P):
            n = int(np.prod(shape)) * (2 if dt == BF16 else 4) // 4
            v = zone[0:parts, at:at + n]
            if dt == BF16:
                v = v.bitcast(BF16)
            names = " ".join("abcd"[:len(shape)])
            return v.rearrange(f"p ({names}) -> p {names}", **{"abcd"[i]: shape[i] for i in range(len(shape))})

        ZL = 7680
        keep = sb("keep", [P, 6400])
        PS = ctx.enter_context(nc.psum_tensor("PS", [P, 8, 512], F32))

        def bank(i):
            return PS[:, i, :]

        def chunk(i):
            return PS[:, i, :].rearrange("p (j d) -> p j d", j=CT)

        def flat(t):
            return t.rearrange("p a b -> p (a b)")

        class Lane:

            def __init__(self, k):
                self.k, self.b0 = k, 4 * k
                self.banks = [4 * k, 4 * k + 1, 4 * k + 2]
                self.out = 4 * k + 3
                self.finished = Track(f"lane{k}", nc.vector, sem(f"lane{k}"), 1)
                self.free = {}
                self.turn = 0

                def buf(name, at, shape):
                    return sb(name, [P] + shape) if k == 0 else in_zone(ZL + at, shape)

                self.hT = buf("hT", 0, [4, S])
                self.xn = buf("xn", 2048, [CT, D])
                self.xT = buf("xT", 2560, [S])
                self.tot = buf("tot", 3072, [CT, D])
                self.pair = buf("pair", 3584, [2, S])
                self.x1 = self.pair[:, 0].rearrange("p (j d) -> p j d", j=CT)
                self.sq = self.pair[:, 1].rearrange("p (j d) -> p j d", j=CT)
                self.ss, self.va, self.rs = (sb(f"{n}{k}", [P, CT]) for n in ("ss", "va", "rs"))
                self.bn6 = sb(f"bn6_{k}", [P, CT, 6])
                self.mv = sb(f"mv{k}", [P, CT, 2])

            def bank(self):
                b = self.banks[self.turn % 3]
                self.turn += 1
                return b

        consts = {}
        for name in ("ident", "causal_kq", "causal_qk", "alibi_kq", "alibi_qk", "headmean", "tri"):
            consts[name] = sb("c_" + name, [P, P])
            nc.sync.dma_start(consts[name][:], args["c_" + name]).then_inc(CONST.sem, 16)
            CONST.count += 16
        rank = sb("rank", [P, E])
        slopes = sb("slopes", [P, H])
        qscale2 = sb("qscale2", [P, 1])
        for t, n in ((rank, "c_rank"), (slopes, "c_slopes"), (qscale2, "c_qscale2")):
            nc.sync.dma_start(t[:], args[n]).then_inc(CONST.sem, 16)
            CONST.count += 16
        const_in = CONST.here()
        ident = consts["ident"]

        def load(track, name, shape, src):
            t = sb(name, shape)
            track.done(nc.sync.dma_start(t[:], src))
            return t

        LD = LD0
        for b in range(B):
            x_in = LD[8].done(nc.sync.dma_start(X[:, b * CT:(b + 1) * CT, :], args["x"][b].rearrange("(j p) d -> p j d", p=P)))
        w_in = load(LD[0], "w_in", [P, 5 * D], args["L0_attn_in_proj_w"])
        w_out0 = load(LD[0], "w_out0", [P, D], args["L0_attn_out_proj_w"])
        w_fc = load(LD[0], "w_fc", [P, 512], args["L0_attn_fc_w"])
        w_pr = load(LD[0], "w_pr", [P, 4, D], args["L0_attn_proj_w"].rearrange("(f p) d -> p f d", p=P))
        n1 = load(LD[0], "n1", [P, 1], args["L0_attn_norm1_w"])
        n2 = load(LD[0], "n2", [P, 1], args["L0_attn_norm2_w"])
        w_up = load(LD[1], "w_up", [P, 512], args["L0_ffn_w_up"])
        w_dn = load(LD[1], "w_dn", [P, 4, D], args["L0_ffn_w_down"].rearrange("(f p) d -> p f d", p=P))
        wq1, wk1, wv1, wo1 = [load(LD[2], n, [P, D], args[a]) for n, a in (
            ("wq1", "L1_attn_q_heads"), ("wk1", "L1_attn_k_heads"), ("wv1", "L1_attn_v_heads"), ("wo1", "L1_attn_output_proj"))]

        ones = sb("ones", [P, P])
        onesb = sb("onesb", [P, P], BF16)
        half = sb("half", [P, NT])
        mhalf = sb("mhalf", [P, NT])
        m_one = sb("m_one", [P, NT])
        PO.done(nc.gpsimd.memset(ones[:], 1.0))
        PO.done(nc.gpsimd.memset(onesb[:], 1.0))
        PO.done(nc.gpsimd.memset(half[:], 0.5))
        PO.done(nc.gpsimd.memset(m_one[:], -1.0))
        pool_ready = PO.done(nc.gpsimd.memset(mhalf[:], -0.5))
        bf = {}
        V.after(const_in)
        for name in ("ident", "causal_kq", "causal_qk", "alibi_kq", "alibi_qk", "tri"):
            bf[name] = sb("b_" + name, [P, P], BF16)
            bf_ready = V.done(nc.vector.tensor_copy(bf[name][:], consts[name][:]))
        bcol = {}
        for name, val in (("two", 2.0), ("eps32", EPS32)):
            bcol[name] = sb("bc_" + name, [P, 1])
            bcol_ready = PO.done(nc.gpsimd.memset(bcol[name][:], val))
        PE.after(const_in, pool_ready, bf_ready)
        A.after(bcol_ready, const_in)
        PO.after(pool_ready)
        V.after(bcol_ready)

        st = {}

        lanes = [Lane(0), Lane(1)]
        for L in lanes:
            L.finished.engine.sem_inc(L.finished.sem, 1)
            tracks.append(L.finished)

        def join():
            now = [t.here() for t in (V, A, PE, PO)]
            for t in (V, A, PE, PO):
                t.after(*now)

        def in_lanes(name, stages):
            join()
            with loop(B // 2, name) as lp:
                running = []
                for L in lanes:
                    L.at = lp.i * (2 * CT) + L.k * CT
                    L.Xc = X[:, ds(L.at, CT), :]
                    L.free, L.turn = {}, 0
                    running.append(stages(L))
                    V.after(L.finished.here())
                    A.after(L.finished.here())
                    next(running[-1], None)
                while running:
                    running = [r for r in running if next(r, "end") != "end"]

        def finish(L, t):
            V.after(t).sem_inc(L.finished.sem, 1)
            L.finished.count += 1

        def rms_norm(L, src, eps, *ready):
            t = V.done(V.after(*ready).tensor_tensor(L.sq[:], src, src, ALU.mult))
            t = V.done(V.after(t).tensor_reduce(L.ss[:], L.sq[:], AX.X, ALU.add))
            t = PO.done(PO.plain(t).tensor_scalar(L.va[:], L.ss[:], 1.0 / D, eps, ALU.mult, ALU.add))
            t = PO.done(PO.after(t).tensor_tensor(L.rs[:], L.va[:], mhalf[:, 0:CT], ALU.pow))
            yield
            return V.done(V.after(t).tensor_tensor(L.xn[:], src, spread(L.rs), ALU.mult))

        def spread(col):
            return col[:].unsqueeze(2).broadcast_to([P, CT, D])

        def transposed(L, ready, scale=1.0, bias=0.0):
            b = L.bank()
            PE.after(ready)
            for j in range(CT):
                t = nc.tensor.transpose(PS[:, b, j * P:(j + 1) * P], L.xn[:, j, :], ident[:])
            t = PE.done(t)
            yield
            if isinstance(scale, float):
                t = A.done(A.after(t).copy(L.xT[:], bank(b)))
            else:
                t = A.done(A.after(t).activation(L.xT[:], bank(b), ACT.Identity, scale=scale, bias=bias))
            L.free[b] = t
            return t

        def layer_norm(L, src, dst, *ready):
            V.after(*ready)
            for j in range(CT):
                t = V.done(nc.vector.bn_stats(L.bn6[:, j, :], src[:, j, :]))
            V.plain(t)
            for j in range(CT):
                t = V.done(nc.vector.bn_aggr(L.mv[:, j, :], L.bn6[:, j, :]))
            t = PO.done(PO.plain(t).tensor_scalar(L.va[:], L.mv[:, :, 1], 1.0, 1e-5, ALU.mult, ALU.add))
            t = PO.done(PO.after(t).tensor_tensor(L.rs[:], L.va[:], mhalf[:, 0:CT], ALU.pow))
            yield
            V.after(t)
            for j in range(CT):
                t = V.done(nc.vector.tensor_scalar(dst[:, j, :], src[:, j, :], L.mv[:, j, 0:1], L.rs[:, j:j + 1],
                                                   ALU.subtract, ALU.mult))
            return t

        def product(L, w, x):
            b = L.bank()
            return b, PE.done(PE.after(L.free.get(b)).matmul(bank(b), w, x, start=True, stop=True))

        def token_major(L, ready, lhs, rhs, nf, first=True):
            PE.after(*ready)
            for j in range(CT):
                for f in range(nf):
                    mm = nc.tensor.matmul(PS[:, L.out, j * D:(j + 1) * D], lhs(f, j), rhs(f),
                                          start=(first and f == 0), stop=(f == nf - 1), skip_group_check=not first)
            return PE.done(mm)

        V.after(LD[0].here())
        t1 = V.done(nc.vector.tensor_scalar(w_in[:], w_in[:], n1[:, 0:1], None, ALU.mult))
        t2 = V.done(nc.vector.tensor_scalar(w_fc[:], w_fc[:], n2[:, 0:1], None, ALU.mult))
        tmp = [{n: (in_zone(512 * i, [S]) if k == 0 else keep[:, 512 * i:512 * i + 512]) for i, n in enumerate((
            "v", "k", "a", "g", "q", "clamped", "cut", "heads", "u"))} for k in range(2)]
        t3 = PO.done(nc.gpsimd.memset(tmp[0]["heads"][:], 0.0))
        t4 = PO.done(nc.gpsimd.memset(tmp[1]["heads"][:], 0.0))
        PE.after(t1, t2, LD[0].here())
        V.after(x_in, t3, t4)

        def mixer(L):
            T = tmp[L.k]
            t = yield from rms_norm(L, L.Xc, 1e-6)
            t = yield from transposed(L, t)
            PE.after(t)
            yield
            (b_k, t_k), (b_a, t_a), (b_g, t_g) = (
                product(L, w_in[:, n * D:(n + 1) * D], L.xT[:]) for n in (1, 3, 4))
            t_k = L.free[b_k] = A.done(A.after(t_k).activation(T["k"][:], bank(b_k), ACT.Tanh))
            b_v, t_v = product(L, w_in[:, 2 * D:3 * D], L.xT[:])
            t_a = L.free[b_a] = A.done(A.after(t_a).activation(T["a"][:], bank(b_a), ACT.Sigmoid, bias=bcol["two"][:, 0:1]))
            b_q, t_q = product(L, w_in[:, 0:D], L.xT[:])
            t_g = L.free[b_g] = A.done(A.after(t_g).activation(T["g"][:], bank(b_g), ACT.Sigmoid))
            t_v = L.free[b_v] = A.done(A.after(t_v).copy(T["v"][:], bank(b_v)))
            t_q = A.done(A.after(t_q).activation(T["q"][:], bank(b_q), ACT.Square))
            yield
            PE.after(t_q)
            b, t = product(L, consts["headmean"][:], T["q"][:])
            yield
            t = L.free[b] = A.done(A.after(t).activation(T["q"][:], bank(b), ACT.Ln, bias=bcol["eps32"][:, 0:1]))
            t_r = A.done(A.after(t).activation(T["q"][:], T["q"][:], ACT.Exp, scale=-0.5))
            heads = lambda x: x[:].rearrange("p (c s) -> p c s", s=SCAN)[:, :, 0:1]
            t_u = V.done(V.after(t_k, t_v).tensor_tensor(T["u"][:], T["k"][:], T["v"][:], ALU.mult))
            t = V.done(V.after(t_a).tensor_scalar(T["clamped"][:], T["a"][:], 0.6, 0.9995, ALU.max, ALU.min))
            V.after(t)
            V.done(nc.vector.tensor_copy(T["cut"][:], T["clamped"][:]))
            t = V.done(nc.vector.tensor_copy(heads(T["heads"]), heads(T["clamped"])))
            t = V.done(V.after(t).memset(heads(T["cut"]), 0.0))
            pre = T["a"]
            t = V.done(V.after(t).tensor_tensor_scan(pre[:], T["cut"][:], T["heads"][:], 0.0, ALU.mult, ALU.add))
            t = V.done(V.after(t).tensor_scalar(pre[:], pre[:], 1e6, 1.0, ALU.mult, ALU.min))
            t = V.done(V.after(t, t_u).tensor_tensor(T["u"][:], T["u"][:], pre[:], ALU.mult))
            mem = T["cut"]
            t = V.done(V.after(t).tensor_tensor_scan(mem[:], T["clamped"][:], T["u"][:], 0.0, ALU.mult, ALU.add))
            yy = T["k"]
            t2 = V.done(V.after(t_r, t_q).tensor_tensor(T["q"][:], bank(b_q), T["q"][:], ALU.mult))
            t = V.done(V.after(t, t2).tensor_tensor(yy[:], T["q"][:], mem[:], ALU.mult))
            t = V.done(V.after(t).tensor_tensor(yy[:], yy[:], T["v"][:], ALU.subtract))
            t = V.done(V.after(t, t_g).tensor_tensor(yy[:], yy[:], T["g"][:], ALU.mult))
            t = V.done(V.after(t).tensor_tensor(yy[:], yy[:], T["v"][:], ALU.add))
            yield
            t = token_major(L, (t,), lambda f, j: yy[:, j * P:(j + 1) * P], lambda f: w_out0[:], 1)
            yield
            t = V.done(V.after(t).scalar_tensor_tensor(L.x1[:], chunk(L.out), RES, L.Xc, ALU.mult, ALU.add))
            L.free[b_q] = t
            t = yield from rms_norm(L, L.x1[:], 1e-6, t)
            t = yield from transposed(L, t)
            yield
            PE.after(t)
            for n in range(4):
                b, t = product(L, w_fc[:, n * P:(n + 1) * P], L.xT[:])
                t_h = L.free[b] = A.done(A.after(t).activation(L.hT[:, n, :], bank(b), ACT.Silu))
            yield
            t = token_major(L, (t_h,), lambda f, j: L.hT[:, f, j * P:(j + 1) * P], lambda f: w_pr[:, f, :], 4)
            yield
            t = V.done(V.after(t).scalar_tensor_tensor(L.tot[:], chunk(L.out), RES, L.x1[:], ALU.mult, ALU.add))
            t = V.done(V.after(t).tensor_tensor(L.tot[:], L.tot[:], L.Xc, ALU.add))
            t = yield from layer_norm(L, L.tot, L.Xc, t)
            finish(L, t)

        in_lanes("mixer", mixer)

        wt = sb("wt", [P, 512])
        wt2 = sb("wt2", [P, 512])
        wsum = sb("wsum", [P, 1])
        thr = sb("thr", [P, 2])
        V.after(LD[1].here())
        PE.after(LD[1].here())
        for w in (w_up[:], flat(w_dn[:])):
            t = V.done(V.after(V.here()).tensor_reduce(wsum[:], w, AX.X, ALU.add, apply_absolute_value=True))
            t = PE.done(PE.after(t, V.here()).matmul(PS[:, 6, 0:1], ones[:], wsum[:], start=True, stop=True))
            t = V.done(V.after(t).tensor_scalar(thr[:, 0:1], PS[:, 6, 0:1], 0.5 / (D * 512), None, ALU.mult))
            t = V.done(V.after(t).tensor_scalar(thr[:, 1:2], thr[:, 0:1], -1.0, None, ALU.mult))
            V.after(t)
            V.done(nc.vector.tensor_scalar(wt[:], w, thr[:, 0:1], None, ALU.is_gt))
            t = V.done(nc.vector.tensor_scalar(wt2[:], w, thr[:, 1:2], None, ALU.is_lt))
            t = V.done(V.after(t).tensor_tensor(wt[:], wt[:], wt2[:], ALU.subtract))
            t = V.done(V.after(t).tensor_tensor(wt[:], wt[:], w, ALU.subtract))
            t_w = V.done(V.after(t).tensor_tensor(w, w, wt[:], ALU.add))
        PE.after(t_w)
        ssp = [sb(f"ssp{k}", [P, CT]) for k in range(2)]
        hsq = [in_zone(2048 * k, [4, S]) for k in range(2)]

        def inv_rms(L, ready, src, n):
            t = PO.done(PO.plain(ready).tensor_scalar(L.va[:], src, 1.0 / n, 0.0, ALU.mult, ALU.add))
            t = PO.done(PO.after(t).tensor_tensor(L.rs[:], L.va[:], half[:, 0:CT], ALU.pow))
            t = PO.done(PO.plain(t).tensor_scalar(L.va[:], L.rs[:], 1.0, 1e-8, ALU.mult, ALU.add))
            yield
            return V.done(V.after(t).reciprocal(L.rs[:], L.va[:]))

        def ternary(L):
            t = V.done(nc.vector.tensor_tensor(L.sq[:], L.Xc, L.Xc, ALU.mult))
            t = V.done(V.after(t).tensor_reduce(L.ss[:], L.sq[:], AX.X, ALU.add))
            t = yield from inv_rms(L, t, L.ss[:], D)
            t = V.done(V.after(t).tensor_tensor(L.xn[:], L.Xc, spread(L.rs), ALU.mult))
            t = yield from transposed(L, t)
            yield
            PE.after(t)
            for n in range(4):
                b, t = product(L, w_up[:, n * P:(n + 1) * P], L.xT[:])
                t_h = L.free[b] = A.done(A.after(t).activation(L.hT[:, n, :], bank(b), ACT.Gelu))
            t_s = A.done(A.after(t_h).activation(hsq[L.k][:], L.hT[:], ACT.Square))
            yield
            t_o = token_major(L, (t_h,), lambda f, j: L.hT[:, f, j * P:(j + 1) * P], lambda f: w_dn[:, f, :], 4)
            yield
            b = L.bank()
            PE.after(t_s, L.free.get(b))
            for j in range(CT):
                for f in range(4):
                    mm = nc.tensor.matmul(PS[:, b, j:j + 1], hsq[L.k][:, f, j * P:(j + 1) * P], ones[:, 0:1],
                                          start=(f == 0), stop=(f == 3))
            t = PE.done(mm)
            yield
            t = V.done(V.after(t).tensor_copy(ssp[L.k][:], PS[:, b, 0:CT]))
            t = yield from inv_rms(L, t, ssp[L.k][:], 512)
            V.after(t, t_o)
            for j in range(CT):
                t = V.done(nc.vector.scalar_tensor_tensor(L.tot[:, j, :], chunk(L.out)[:, j, :], L.rs[:, j:j + 1],
                                                          X[:, ds(L.at + j, 1), :].rearrange("p a d -> p (a d)"),
                                                          ALU.mult, ALU.add))
            t = yield from layer_norm(L, L.tot, L.Xc, t)
            finish(L, t)

        in_lanes("ternary", ternary)

        scratch = nc.dram_tensor("score_parts", (2, B * G, 3, HD * R, S), BF16, kind="Internal").ap()
        VT = B * G * CT * R * (HD + 1)
        Vt = keep[:, 0:VT].rearrange("p (u j r d) -> p u j r d", u=B * G, j=CT, r=R)
        O = keep[:, VT:VT + 2048].rearrange("p (u j r d) -> p u j r d", u=B * G, j=CT, r=R)
        parts = [sb("parts", [P, 2, 3, S], BF16),
                 keep[:, VT:VT + 1536].bitcast(BF16).rearrange("p (n i q) -> p n i q", n=2, i=3)]
        NB = 4
        OQ = in_zone(0, [NB, R, S], BF16, 96)
        OK = in_zone(4096, [NB, R, S], BF16, 96)
        VS = keep[:, VT + 2048:VT + 4096].rearrange("p (s j r d) -> p s j r d", s=NB, j=CT, r=R)
        PB = in_zone(8192, [2, R, S])
        oT = sb("oT", [P, S])
        negm = sb("negm", [P, R * CT])
        nmp = sb("nmp", [P, 2, R * CT], BF16)
        mT = sb("mT", [32, NB, P], BF16)
        rden = sb("rden", [P, R * CT])
        OPER = [dma(f"operand{i}") for i in range(NB)]
        MROW = [dma(f"mrow{i}") for i in range(NB)]
        for t in OPER + MROW:
            t.engine.sem_inc(t.sem, t.step)
            tracks.append(t)
        join()
        t_vt = PO.done(nc.gpsimd.memset(Vt[:], 1.0))
        t_vs = PO.done(nc.gpsimd.memset(VS[:], 0.0))
        V.after(t_vt)
        PO.after(t_vt, t_vs)
        rows16 = nc.dram_tensor("rows16", (2, NLIN + 2, S), BF16, kind="Internal").ap()
        CAST.done(nc.gpsimd.dma_start(rows16[0], args["c_rows_q"]))
        t_rows16 = CAST.done(nc.gpsimd.dma_start(rows16[1], args["c_rows_k"]))
        ROWS.plain(t_rows16)

        def constant_rows(lin):
            KR = NCOMBO + (NLIN if lin else 0)
            ROWS.plain(PE.here(), V.here(), A.here())
            for dst, src in ([(OQ[NCOMBO:KR], rows16[0, 0:NLIN]), (OK[NCOMBO:KR], rows16[1, 0:NLIN])] if lin else []) + [
                    (OK[KR:KR + 2], rows16[1, NLIN:NLIN + 2])]:
                ROWS.done(nc.sync.dma_start(dst.rearrange("p s r q -> p (s r) q"),
                                            src.unsqueeze(1).broadcast_to([src.shape[0], NB * R, S])))

        def attention_prep(name, wq, wk, wv, qs, qb=None, kb=None, vb=None):
            def prep(L):
                mine = parts[L.k]
                t = A.done(nc.scalar.copy(L.xn[:], L.Xc))
                t = yield from transposed(L, t)
                PE.after(t)
                yield
                ends = [product(L, w, L.xT[:]) for w in (wq, wk)]
                t_v = token_major(L, (), lambda f, j: L.xT[:, j * P:(j + 1) * P], lambda f: wv, 1)
                A.after(SPILLS[L.k].here())
                for n, (sc, bi) in enumerate(((qs, qb), (1.0, kb))):
                    bi = 0.0 if bi is None else bi
                    A.after(ends[n][1])
                    nc.scalar.activation(mine[:, n, 0, :], bank(ends[n][0]), ACT.Identity, scale=sc, bias=bi)
                    t = A.done(nc.scalar.activation(L.pair[:, n, :], bank(ends[n][0]), ACT.Identity, scale=sc, bias=bi))
                yield
                t = V.done(V.after(t).tensor_tensor(L.pair[:], L.pair[:], mine[:, :, 0, :], ALU.subtract))
                t = V.done(V.after(t).tensor_copy(mine[:, :, 1, :], L.pair[:]))
                t = V.done(V.after(t).tensor_tensor(mine[:, :, 2, :], L.pair[:], mine[:, :, 1, :], ALU.subtract))
                T = SPILLS[L.k]
                T.plain(t)
                for n in range(2):
                    for i in range(3):
                        T.done(nc.sync.dma_start(
                            scratch[n, ds(L.at, G), i], mine[:, n, i]))
                V.after(t_v)
                for j in range(CT):
                    o = Vt[:, ds(L.at, G), j, :, 0:HD]
                    i_ = chunk(L.out)[:, j, :].rearrange("p (g r d) -> p g r d", g=G, r=R)
                    if vb is None:
                        t = V.done(nc.vector.tensor_copy(o, i_))
                    else:
                        t = V.done(nc.vector.tensor_tensor(o, i_, vb.rearrange("p (g r d) -> p g r d", g=G, r=R), ALU.add))
                finish(L, t)

            in_lanes(name + "_prep", prep)

        def attention(name, causal=False, diag_kq=None, diag_qk=None, slope=None, void=None, lin=False):
            KR = NCOMBO + (NLIN if lin else 0)
            KM = KR + 2
            spilled = [t.here() for t in SPILLS]
            join()
            PE.after(ROWS.here())
            last = {}

            def ring_slot():
                n = last["ring"]
                last["ring"] = n + 1
                PE.after(last[("ring", n % 3)])
                return n % 3

            def load(u, s):
                T = OPER[s]
                T.plain(last[("oper", s)], *spilled)
                unit = scratch[:, ds(u, 1)] if not isinstance(u, int) else scratch[:, u:u + 1]
                T.done(nc.sync.dma_start(
                    OQ[0:NCOMBO, s].rearrange("a r q -> a (r q)"),
                    unit[0].rearrange("o i (a r) q -> o (i a) (r q)", r=R).broadcast_to([3, 3 * HD, R * S])))
                for j in range(3):
                    t = T.done(nc.sync.dma_start(
                        OK[24 * j:24 * j + 24, s].rearrange("a r q -> a (r q)"),
                        unit[1, :, j].rearrange("o (a r) q -> o a (r q)", r=R).broadcast_to([3, HD, R * S])))
                last[("loaded", s)] = t

            def load_values(u, s):
                src = Vt[:, ds(u, 1)] if not isinstance(u, int) else Vt[:, u:u + 1]
                PO.after(last[("vs", s)])
                for kt in range(CT):
                    t = PO.done(nc.gpsimd.tensor_copy(VS[:, s, kt, :, 0:HD + 1],
                                                      src[:, :, kt].rearrange("p a r d -> p (a r) d")))
                last[("vs_in", s)] = t

            def max_slot(s, n):
                qt, r = n // R, n % R
                b = ring_slot()
                if n == 0:
                    PE.after(last[("loaded", s)])
                nk = (qt + 1) * P if causal else S
                diag = diag_qk is not None
                mm = nc.tensor.matmul(PS[:, b, 0:nk], OQ[0:KR, s, r, qt * P:(qt + 1) * P], OK[0:KR, s, r, 0:nk],
                                      start=True, stop=True)
                if diag:
                    mm = nc.tensor.matmul(PS[:, b, qt * P:(qt + 1) * P], bf["ident"][:], diag_qk[:],
                                          start=False, stop=True, skip_group_check=True)
                t = PE.done(mm)
                k = r * CT + qt
                t = V.done(V.after(t, last["nmp"] if n == 0 else None).tensor_reduce(
                    negm[:, k:k + 1], PS[:, b, 0:nk], AX.X, ALU.max, negate=True))
                last[("ring", b)] = t
                return t

            def max_void(s, g):
                b = ring_slot()
                for r in range(R):
                    for qt in range(CT):
                        k = r * CT + qt
                        mm = nc.tensor.matmul(PS[:, b, k:k + 1], OQ[0:KR, s, r, qt * P:(qt + 1) * P],
                                              void[0][0:KR, g, r, 0:1], start=True, stop=True, skip_group_check=True)
                t = PE.done(mm)
                t = V.done(V.after(t).tensor_scalar(rden[:], PS[:, b, 0:16], -1.0, None, ALU.mult))
                last[("ring", b)] = t
                return V.done(V.after(t, V.here()).tensor_tensor(negm[:], negm[:], rden[:], ALU.min))

            def max_rows(s, t):
                t = V.done(V.after(t, last["nmp_pe"]).tensor_copy(nmp[:, 0, :], negm[:]))
                t = V.done(V.after(t).tensor_tensor(nmp[:, 1, :], negm[:], nmp[:, 0, :], ALU.subtract))
                last["nmp"] = t
                b = ring_slot()
                pt = PS[0:32, b, 0:64].bitcast(BF16)
                t = PE.done(PE.after(t).transpose(pt, nmp[:].rearrange("p a b -> p (a b)"), bf["ident"][:]))
                last["nmp_pe"] = t
                t = V.done(V.after(t, last[("mrow", s)]).tensor_copy(mT[:, s, :], pt))
                last[("ring", b)] = t
                MROW[s].plain(t, last[("oper", s)])
                for i in range(2):
                    t = MROW[s].done(nc.sync.dma_start(
                        OQ[KR + i:KR + i + 1, s].rearrange("a r (t q) -> a (r t) q", t=CT), mT[16 * i:16 * i + 16, s, :]))
                last[("mrow", s)] = t

            def scores(s, kt, rp):
                q0 = kt * P if causal else 0
                if kt == 0 and rp == 0:
                    PE.after(last[("mrow", s)])
                PE.after(last[("pair", rp)])
                for r in (2 * rp, 2 * rp + 1):
                    b = 3 + r
                    diag = diag_kq is not None
                    mm = nc.tensor.matmul(PS[:, b, q0:S], OK[0:KM, s, r, kt * P:(kt + 1) * P], OQ[0:KM, s, r, q0:S],
                                          start=True, stop=True)
                    if diag:
                        mm = nc.tensor.matmul(PS[:, b, kt * P:(kt + 1) * P], bf["ident"][:], diag_kq[:],
                                              start=False, stop=True, skip_group_check=True)
                t = PE.done(mm)
                if kt == CT - 1 and rp == 1 and void is None:
                    last[("oper", s)] = t
                A.after(t, last[("pb", kt % 2)])
                if slope is None:
                    t = A.done(nc.scalar.activation(PB[:, kt % 2, 2 * rp:2 * rp + 2, q0:S],
                                                    PS[:, 3 + 2 * rp:5 + 2 * rp, q0:S], ACT.Exp))
                else:
                    for r in (2 * rp, 2 * rp + 1):
                        t = A.done(nc.scalar.activation(PB[:, kt % 2, r, q0:S], PS[:, 3 + r, q0:S], ACT.Exp,
                                                        scale=slope(s, r)))
                last[("pair", rp)] = t
                last[("exp", kt)] = t

            def values(s, kt):
                q0 = kt * P if causal else 0
                PE.after(last[("exp", kt)])
                if kt == 0:
                    PE.after(last["acc"], last[("vs_in", s)])
                for r in range(R):
                    mm = nc.tensor.matmul(PS[32 * r:32 * r + 32, 7, q0:S], VS[:, s, kt, r, :], PB[:, kt % 2, r, q0:S],
                                          start=(kt == 0), stop=True, skip_group_check=True)
                t = PE.done(mm)
                last[("pb", kt % 2)] = t
                last[("vs", s)] = t
                last["acc_in"] = t

            def void_key(s, g):
                PE.after(last[("pair", 0)])
                for r in range(R):
                    mm = nc.tensor.matmul(PS[32 * r:32 * r + 32, 3, :], void[0][0:KM, g, r, :], OQ[0:KM, s, r, :],
                                          start=True, stop=True, skip_group_check=True)
                t = PE.done(mm)
                last[("oper", s)] = t
                t = A.done(A.after(t, last["pvo"]).activation(pvo[:], bank(3), ACT.Exp))
                last[("pair", 0)] = t
                last["pvo_in"] = t

            def void_value(g):
                t = PE.done(PE.after(last["pvo_in"]).matmul(bank(7), void[1][:, g, :], pvo[:], start=False, stop=True,
                                                            skip_group_check=True))
                last["pvo"] = t
                last["acc_in"] = t

            def evacuate():
                t = A.done(A.after(last["acc_in"], last["oT"]).copy(oT[:], bank(7)))
                last["acc"] = t
                last["oT_in"] = t

            def normalise(u):
                b = ring_slot()
                PE.after(last["oT_in"])
                for j in range(CT):
                    mm = nc.tensor.transpose(PS[:, b, j * P:(j + 1) * P], oT[:, j * P:(j + 1) * P], ident[:])
                t = PE.done(mm)
                last["oT"] = t
                acc = bank(b).rearrange("p (x d) -> p x d", d=32)
                t = V.done(V.after(t, last["rden"]).reciprocal(rden[:].unsqueeze(2), acc[:, :, HD:HD + 1]))
                dst = O[:, ds(u, 1)].rearrange("p a t r d -> p (a t r) d") if not isinstance(u, int) else \
                    O[:, u].rearrange("p t r d -> p (t r) d")
                t = V.done(V.after(t).tensor_tensor(dst, acc[:, :, 0:HD],
                                                    rden[:].unsqueeze(2).broadcast_to([P, R * CT, HD]), ALU.mult))
                last["rden"] = t
                last[("ring", b)] = t

            def step(s, u_exp=None, u_max=None, u_norm=None, u_load=None, finish=None):
                s2, s0 = (s + 2) % NB, (s - 1) % NB
                if u_load is not None:
                    load(u_load, s0)
                t = None
                for n in range(2 * CT):
                    kt, rp = n // 2, n % 2
                    if u_max is not None:
                        max_slot(s2, 2 * n)
                        t = max_slot(s2, 2 * n + 1)
                    if u_exp is not None:
                        scores(s, kt, rp)
                    if n == 0 and u_norm is not None:
                        values(s0, CT - 1)
                        if void is not None:
                            void_value(s0)
                        evacuate()
                    if n == 0 and u_load is not None:
                        load_values(u_load, s0)
                    if n == 2 and u_norm is not None:
                        normalise(u_norm)
                    if rp == 1 and kt > 0 and u_exp is not None:
                        values(s, kt - 1)
                if u_exp is not None and void is not None:
                    void_key(s, s)
                if u_max is not None:
                    if void is not None:
                        t = max_void(s2, s2)
                    max_rows(s2, t)

            def fresh():
                now = {"V": V.here(), "A": A.here(), "PE": PE.here(), "PO": PO.here()}
                last["ring"] = 0
                for b in range(3):
                    last[("ring", b)] = now["V"]
                for s in range(NB):
                    last[("oper", s)] = now["PE"]
                    last[("vs", s)] = now["PE"]
                    last[("vs_in", s)] = now["PO"]
                    last[("loaded", s)] = OPER[s].here()
                    last[("mrow", s)] = MROW[s].here()
                for b in range(2):
                    last[("pair", b)] = now["A"]
                    last[("pb", b)] = now["PE"]
                for kt in range(CT):
                    last[("exp", kt)] = now["A"]
                last["nmp"] = last["rden"] = now["V"]
                last["nmp_pe"] = now["PE"]
                last["acc"] = last["oT_in"] = last["pvo_in"] = now["A"]
                last["acc_in"] = last["oT"] = last["pvo"] = now["PE"]

            fresh()
            for u in range(2):
                load(u, u)
                load_values(u, u)
            step(NB - 2, u_max=0)
            load(2, 2)
            load_values(2, 2)
            step(NB - 1, u_max=1)
            step(0, u_exp=0, u_max=2, u_load=3)
            with loop(B - 1, name) as lp:
                fresh()
                for g in range(G):
                    u = lp.i * G + (g + 1)
                    step((g + 1) % G, u_exp=u, u_max=u + 2, u_norm=lp.i * G + g if g else lp.i * G, u_load=u + 3)
            fresh()
            for u in range(B * G - 3, B * G):
                step(u % G, u_exp=u, u_max=u + 2 if u + 2 < B * G else None, u_norm=u - 1,
                     u_load=u + 3 if u + 3 < B * G else None)
            step(0, u_norm=B * G - 1)

        def attention_out(name, wo, bias=None):
            def out_stages(L):
                for j in range(CT):
                    t = V.done(nc.vector.tensor_copy(
                        L.xn[:, j, :].rearrange("p (g x) -> p g x", g=G),
                        O[:, ds(L.at, G), j].rearrange("p g r d -> p g (r d)")))
                t = yield from transposed(L, t)
                yield
                t = token_major(L, (t,), lambda f, j: L.xT[:, j * P:(j + 1) * P], lambda f: wo, 1)
                yield
                t = V.done(V.after(t).tensor_tensor(L.tot[:], chunk(L.out), L.Xc, ALU.add))
                if bias is not None:
                    t = V.done(V.after(t).tensor_tensor(
                        L.tot[:], L.tot[:], bias.unsqueeze(1).broadcast_to([P, CT, D]), ALU.add))
                t = yield from layer_norm(L, L.tot, L.Xc, t)
                finish(L, t)

            in_lanes(name + "_out", out_stages)

        PE.after(LD[2].here())
        constant_rows(False)
        attention_prep("a1", wq1[:], wk1[:], wv1[:], HD ** -0.5)
        attention("a1", causal=True, diag_kq=bf["causal_kq"], diag_qk=bf["causal_qk"])
        attention_out("a1", wo1[:])


        LG = sb("LG", [P, NT, E])
        M1 = sb("M1", [P, NT, E])
        M2 = sb("M2", [P, NT, E])
        G2 = sb("G2", [P, NT, E])
        CW = sb("CW", [P, NT, E])
        mk = sb("mk", [P, NT])
        mk2 = sb("mk2", [P, NT])
        M1b = sb("M1b", [P, NT, E], BF16)
        trib, oneb = bf["tri"], onesb

        def router_logits(L, t, w):
            PE.after(t)
            for j in range(CT):
                mm = nc.tensor.matmul(PS[:, L.out, j * E:(j + 1) * E], L.xT[:, j * P:(j + 1) * P], w[:], start=True, stop=True)
            return PE.done(mm), PS[:, L.out, 0:CT * E].rearrange("p (j e) -> p j e", e=E)

        def col3(c):
            return c[:].unsqueeze(2).broadcast_to([P, NT, E])

        def first_of(dst, src, t):
            t = V.done(V.after(t).tensor_reduce(mk[:], src, AX.X, ALU.max))
            t = V.done(V.after(t).tensor_tensor(dst, src, col3(mk), ALU.is_equal))
            t = V.done(V.after(t).tensor_tensor(dst, dst, rank[:].unsqueeze(1).broadcast_to([P, NT, E]), ALU.mult))
            t = V.done(V.after(t).tensor_reduce(mk[:], dst, AX.X, ALU.max))
            return V.done(V.after(t).tensor_tensor(dst, dst, col3(mk), ALU.is_equal))

        def second_of(t):
            t = V.done(V.after(t).tensor_scalar(G2[:], M1[:], -1.0, 1.0, ALU.mult, ALU.add))
            return V.done(V.after(t).tensor_tensor(G2[:], G2[:], LG[:], ALU.mult))

        def softmax_gates(t):
            t = V.done(V.after(t).tensor_reduce(mk[:], LG[:], AX.X, ALU.max))
            t = V.done(V.after(t).tensor_tensor(LG[:], LG[:], col3(mk), ALU.subtract))
            t = A.done(A.after(t).activation(LG[:], LG[:], ACT.Exp))
            return V.done(V.after(t).tensor_reduce(mk[:], LG[:], AX.X, ALU.add))

        rw1 = load(LD[3], "rw1", [P, E], args["L1_ffn_router_w"])
        w1 = load(LD[3], "w1", [P, E, 512], args["L1_ffn_w1"].rearrange("e d f -> d e f"))
        w2 = sb("w2", [P, E, 4, D])
        for e in range(E):
            LD[3].done(nc.sync.dma_start(w2[:, e], args["L1_ffn_w2"][e].rearrange("(f p) d -> p f d", p=P)))
        b1 = load(LD[3], "b1", [P, E, 4], args["L1_ffn_b1"])
        b2 = load(LD[3], "b2", [E, D], args["L1_ffn_b2"])
        s1 = load(LD[3], "s1", [P, 512], args["L1_ffn_sw1"])
        s2 = load(LD[3], "s2", [P, 4, D], args["L1_ffn_sw2"].rearrange("(f p) d -> p f d", p=P))
        sb1 = load(LD[3], "sb1", [P, 4], args["L1_ffn_sb1"])
        sb2 = load(LD[3], "sb2", [P, D], args["L1_ffn_sb2"].unsqueeze(0).broadcast_to([P, D]))
        cwT = [sb("cwT", [E, CT, P]), in_zone(0, [CT, P], parts=E)]
        PE.after(LD[3].here())
        A.after(LD[3].here())
        V.after(LD[3].here())

        def route1(L):
            t = A.done(nc.scalar.copy(L.xn[:], L.Xc))
            t = yield from transposed(L, t)
            yield
            t, pos = router_logits(L, t, rw1)
            yield
            t = V.done(V.after(t).tensor_copy(LG[:, ds(L.at, CT), :], pos))
            finish(L, t)

        in_lanes("route1", route1)
        join()
        t = V.here()
        t = softmax_gates(t)
        t = V.done(V.after(t).reciprocal(mk2[:], mk[:]))
        t = V.done(V.after(t).tensor_tensor(LG[:], LG[:], col3(mk2), ALU.mult))
        t = first_of(M1[:], LG[:], t)
        t = second_of(t)
        t = first_of(M2[:], G2[:], t)

        def earlier(mask, t):
            t = V.done(V.after(t).tensor_copy(M1b[:], mask))
            PE.after(t)
            pos = PS[:, 6, 0:NT * E].rearrange("p (j e) -> p j e", e=E)
            mm = nc.tensor.matmul(pos, trib[:], M1b[:], start=True, stop=True)
            for j in range(NT - 1):
                mm = nc.tensor.matmul(pos[:, j + 1:NT], oneb[:], M1b[:, j:j + 1].broadcast_to([P, NT - 1 - j, E]),
                                      start=False, stop=True, skip_group_check=True)
            return mm, pos

        mm, pos = earlier(M1[:], t)
        t = PE.done(mm)
        t = V.done(V.after(t).tensor_scalar(G2[:], pos, float(CAP), None, ALU.is_lt))
        t = V.done(V.after(t).tensor_tensor(M1[:], M1[:], G2[:], ALU.mult))
        mm, pos = earlier(M2[:], t)
        t = PE.done(mm)
        t = V.done(V.after(t).tensor_copy(M1b[:], M1[:]))
        PE.after(t)
        for j in range(NT):
            mm = nc.tensor.matmul(pos, oneb[:], M1b[:, j:j + 1].broadcast_to([P, NT, E]),
                                  start=False, stop=True, skip_group_check=True)
        t = PE.done(mm)
        t = V.done(V.after(t).tensor_scalar(G2[:], pos, float(CAP), None, ALU.is_lt))
        t = V.done(V.after(t).tensor_tensor(M2[:], M2[:], G2[:], ALU.mult))
        t = V.done(V.after(t).tensor_tensor(M1[:], M1[:], LG[:], ALU.mult))
        t = V.done(V.after(t).tensor_tensor(M2[:], M2[:], LG[:], ALU.mult))
        t = V.done(V.after(t).tensor_tensor(CW[:], M1[:], M2[:], ALU.add))
        t = V.done(V.after(t).tensor_reduce(mk[:], CW[:], AX.X, ALU.add))
        t = V.done(V.after(t).tensor_scalar(mk[:], mk[:], EPS32, None, ALU.max))
        t = V.done(V.after(t).reciprocal(mk2[:], mk[:]))
        t_cw = V.done(V.after(t).tensor_tensor(CW[:], CW[:], col3(mk2), ALU.mult))

        def experts1(L):
            cw = CW[:, ds(L.at, CT), :]
            t = A.done(nc.scalar.copy(L.xn[:], L.Xc))
            t_x = yield from transposed(L, t)
            t = A.done(nc.scalar.copy(L.sq[:, :, 0:E], cw))
            yield
            b = L.bank()
            PE.after(t, L.free.get(b))
            for j in range(CT):
                mm = nc.tensor.transpose(PS[0:E, b, j * P:(j + 1) * P], L.sq[:, j, 0:E], ident[:])
            t = PE.done(mm)
            yield
            t = L.free[b] = A.done(A.after(t).copy(cwT[L.k][:], PS[0:E, b, :].rearrange("e (j p) -> e j p", j=CT)))
            yield
            t = token_major(L, (t,), lambda f, j: cwT[L.k][:, j, :], lambda f: b2[:], 1)
            yacc = L.x1
            t_y = V.done(V.after(t).tensor_tensor(yacc[:], chunk(L.out), L.Xc, ALU.add))
            PE.after(t_x)
            t_down = None
            for e in range(E + 1):
                wa = w1[:, e, :] if e < E else s1[:]
                wb = w2[:, e] if e < E else s2[:]
                for n in range(4):
                    b, t = product(L, wa[:, n * P:(n + 1) * P], L.xT[:])
                    bias = b1[:, e, n:n + 1] if e < E else sb1[:, n:n + 1]
                    t = L.free[b] = A.done(A.after(t, t_down).activation(L.hT[:, n, :], bank(b), ACT.Silu, bias=bias))
                yield
                t_down = token_major(L, (t, t_y), lambda f, j: L.hT[:, f, j * P:(j + 1) * P], lambda f: wb[:, f, :], 4)
                V.after(t_down)
                if e < E:
                    for j in range(CT):
                        t_y = V.done(V.after(t_y).scalar_tensor_tensor(
                            yacc[:, j, :], chunk(L.out)[:, j, :], cw[:, j, e:e + 1], yacc[:, j, :], ALU.mult, ALU.add))
                else:
                    t = V.done(nc.vector.tensor_tensor(L.tot[:], chunk(L.out), sb2[:].unsqueeze(1).broadcast_to([P, CT, D]), ALU.add))
                    t = V.done(V.after(t, t_y).scalar_tensor_tensor(L.tot[:], L.tot[:], 0.1, yacc[:], ALU.mult, ALU.add))
            yield
            t = yield from layer_norm(L, L.tot, L.Xc, t)
            finish(L, t)

        in_lanes("experts1", experts1)

        w2qkv = load(LD[4], "w2qkv", [P, 3 * D], args["L2_attn_W_qkv"])
        w2p = load(LD[4], "w2p", [P, D], args["L2_attn_W_proj"])
        b2q = load(LD[4], "b2q", [P, 2], args["L2_attn_b_qk"])
        b2v = load(LD[4], "b2v", [P, D], args["L2_attn_b_v"].unsqueeze(0).broadcast_to([P, D]))
        b2p = load(LD[4], "b2p", [P, D], args["L2_attn_b_proj"].unsqueeze(0).broadcast_to([P, D]))
        V.after(LD[4].here())
        t = V.done(nc.vector.tensor_tensor(b2q[:, 0:1], b2q[:, 0:1], qscale2[:], ALU.mult))
        PE.after(LD[4].here())
        A.after(t, LD[4].here())
        constant_rows(True)
        attention_prep("a2", w2qkv[:, 0:D], w2qkv[:, D:2 * D], w2qkv[:, 2 * D:], qscale2[:, 0:1],
                       b2q[:, 0:1], b2q[:, 1:2], b2v[:])
        attention("a2", diag_kq=bf["alibi_kq"], diag_qk=bf["alibi_qk"], lin=True,
                  slope=lambda g, r: float(2.0 ** (-0.5 * (g * R + r + 1))))
        attention_out("a2", w2p[:], b2p[:])

        NJ = 8
        win = load(LD[5], "win", [P, NJ * P], args["L2_ffn_Win"])
        binr = load(LD[5], "binr", [P, NJ], args["L2_ffn_bin_"])
        cw1 = load(LD[5], "cw1", [P, NJ], args["L2_ffn_W1"])
        cb1 = load(LD[5], "cb1", [P, NJ], args["L2_ffn_b1"])
        cw2 = load(LD[5], "cw2", [P, NJ], args["L2_ffn_W2"])
        cb2 = load(LD[5], "cb2", [64, 1], args["L2_ffn_b2"])
        wout = load(LD[5], "wout", [P, NJ, D], args["L2_ffn_Wout_rep"])
        wout1 = load(LD[5], "wout1", [64, D], args["L2_ffn_Wout"])
        bout = load(LD[5], "bout", [P, D], args["L2_ffn_bout"].unsqueeze(0).broadcast_to([P, D]))
        h8 = [in_zone(4096 * k, [NJ, S]) for k in range(2)]
        cb2w = sb("cb2w", [64, P])
        V.after(LD[5].here())
        t = V.done(nc.vector.tensor_tensor(binr[:], binr[:], cw1[:], ALU.mult))
        t = V.done(V.after(t).tensor_tensor(cb1[:], cb1[:], binr[:], ALU.add))
        t = V.done(nc.vector.tensor_tensor(wout[:], wout[:], cw2[:].unsqueeze(2).broadcast_to([P, NJ, D]), ALU.mult))
        t = V.done(V.after(t).tensor_copy(cb2w[:], cb2[:].broadcast_to([64, P])))
        t = PE.done(PE.after(t, LD[5].here()).matmul(PS[:, 6, 0:D], cb2w[:], wout1[:], start=True, stop=True))
        t = V.done(V.after(t).tensor_tensor(bout[:], bout[:], PS[:, 6, 0:D], ALU.add))
        V.after(t)
        A.after(t, LD[5].here())

        def channels(L):
            h = h8[L.k]
            t = A.done(nc.scalar.copy(L.xn[:], L.Xc))
            t = yield from transposed(L, t)
            yield
            PE.after(t)
            for n in range(NJ):
                b, t = product(L, win[:, n * P:(n + 1) * P], L.xT[:])
                t = L.free[b] = A.done(A.after(t).activation(h[:, n, :], bank(b), ACT.Relu,
                                                             scale=cw1[:, n:n + 1], bias=cb1[:, n:n + 1]))
            yield
            t = token_major(L, (t,), lambda f, j: h[:, f, j * P:(j + 1) * P], lambda f: wout[:, f, :], NJ)
            yield
            t = V.done(V.after(t).tensor_tensor(L.tot[:], chunk(L.out), L.Xc, ALU.add))
            t = V.done(V.after(t).tensor_tensor(L.tot[:], L.tot[:], bout[:].unsqueeze(1).broadcast_to([P, CT, D]), ALU.add))
            t = yield from layer_norm(L, L.tot, L.Xc, t)
            finish(L, t)

        in_lanes("channels", channels)

        w3qkv = load(LD[6], "w3qkv", [P, 3 * D], args["L3_attn_w_qkv"])
        w3o = load(LD[6], "w3o", [P, D], args["L3_attn_w_out"])
        b3o = load(LD[6], "b3o", [P, D], args["L3_attn_b_out"].unsqueeze(0).broadcast_to([P, D]))
        tr3 = load(LD[6], "tr3", [P, 2], args["L3_attn_trace_tf"])
        vk3 = load(LD[6], "vk3", [HD, G * R], args["L3_attn_void_k"])
        vvb = sb("vvb", [P, G, P])
        t = V.done(V.after(V.here()).memset(vvb[:], 0.0))
        LD[7].plain(t)
        for g in range(G):
            for r in range(R):
                LD[7].done(nc.sync.dma_start(vvb[32 * r:32 * r + 1, g, 32 * r:32 * r + HD], args["L3_attn_void_v"][g * R + r:g * R + r + 1]))
                LD[7].done(nc.sync.dma_start(vvb[32 * r:32 * r + 1, g, 32 * r + HD:32 * r + HD + 1], args["c_ident"][0:1, 0:1]))
        V.after(LD[6].here())
        q3 = sb("q3", [P, 1])
        t = V.done(nc.vector.tensor_scalar(q3[:], tr3[:, 0:1], -1.0, None, ALU.mult))
        t = V.done(V.after(t).tensor_tensor(q3[:], q3[:], tr3[:, 0:1], ALU.max))
        t = V.done(V.after(t).tensor_tensor(q3[:], q3[:], tr3[:, 1:2], ALU.mult))
        t = V.done(V.after(t).tensor_scalar(q3[:], q3[:], 1.0, 1.0, ALU.add, ALU.max))
        t = V.done(V.after(t).reciprocal(q3[:], q3[:]))
        t_q3 = V.done(V.after(t).tensor_scalar(q3[:], q3[:], D ** -0.5, None, ALU.mult))
        vkp = sb("vkp", [HD, 3, G * R], BF16)
        vkr = sb("vkr", [HD, G * R])
        t = V.done(nc.vector.tensor_copy(vkp[:, 0], vk3[:]))
        t = V.done(V.after(t).tensor_tensor(vkr[:], vk3[:], vkp[:, 0], ALU.subtract))
        t = V.done(V.after(t).tensor_copy(vkp[:, 1], vkr[:]))
        t = V.done(V.after(t).tensor_tensor(vkp[:, 2], vkr[:], vkp[:, 1], ALU.subtract))
        vko = sb("vko", [96, G, R, 32], BF16)
        vkc = sb("vkc", [96, G * R], BF16)
        t2 = V.done(nc.vector.memset(vko[:], 0.0))
        t2 = V.done(nc.vector.memset(vkc[:], 1.0))
        LD[8].plain(t, t2)
        for j in range(3):
            for i in range(3):
                u = LD[8].done(nc.sync.dma_start(vkc[24 * j + 8 * i:24 * j + 8 * i + 8, :], vkp[:, j]))
        t = V.done(V.after(u).tensor_copy(vko[:, :, :, 0:1], vkc[:].rearrange("p (g r o) -> p g r o", g=G, o=1)))
        pvo = sb("pvo", [P, S])
        PE.after(LD[6].here(), LD[7].here(), t)
        A.after(t_q3)
        V.after(t)
        constant_rows(False)
        attention_prep("a3", w3qkv[:, 0:D], w3qkv[:, D:2 * D], w3qkv[:, 2 * D:], q3[:, 0:1])
        attention("a3", void=(vko, vvb))
        attention_out("a3", w3o[:], b3o[:])

        rw3 = load(LD[7], "rw3", [P, E], args["L3_ffn_router_w"])
        lng = load(LD[7], "lng", [P, 2], args["L3_ffn_ln"])
        gu3 = w1
        dn3 = w2[:].rearrange("p e f d -> p (e f d)")[:, 0:E * 2 * D].rearrange("p (e f d) -> p e f d", e=E, f=2)
        LD[7].plain(PE.here())
        LD[7].done(nc.sync.dma_start(gu3[:], args["L3_ffn_gate_up_w"].rearrange("e d f -> d e f")))
        for e in range(E):
            LD[7].done(nc.sync.dma_start(dn3[:, e], args["L3_ffn_down_w"][e].rearrange("(f p) d -> p f d", p=P)))
        selr = sb("selr", [3 * E, E, P])
        LD[7].done(nc.sync.dma_start(selr[:], args["c_select"]))
        sel16 = sb("sel16", [3 * E, E, P], BF16)
        CW3 = sb("CW3", [P, NT, 3, E], BF16)
        cwT3 = [sb(f"cwT3_{k}", [3 * E, S], BF16) for k in range(2)]
        xeT = [in_zone(1024 * k, [2, S]) for k in range(2)]
        gate = [in_zone(2048 + 1024 * k, [2, S]) for k in range(2)]
        PE.after(LD[7].here())
        A.after(LD[7].here())
        V.after(LD[7].here())


        def normed(L):
            t = yield from layer_norm(L, L.Xc, L.xn)
            return (yield from transposed(L, t, scale=lng[:, 0:1], bias=lng[:, 1:2]))

        def route3(L):
            t = yield from normed(L)
            yield
            t, pos = router_logits(L, t, rw3)
            yield
            t = V.done(V.after(t).tensor_scalar(LG[:, ds(L.at, CT), :], pos, -10000.0, 10000.0, ALU.max, ALU.min))
            finish(L, t)

        in_lanes("route3", route3)
        join()
        t = V.here()
        t = softmax_gates(t)
        t = V.done(V.after(t).tensor_scalar(mk[:], mk[:], 1e-8, None, ALU.add))
        t = V.done(V.after(t).reciprocal(mk2[:], mk[:]))
        t = V.done(V.after(t).tensor_tensor(LG[:], LG[:], col3(mk2), ALU.mult))
        t = V.done(V.after(t).tensor_scalar(LG[:], LG[:], 1e-8, 1.0, ALU.max, ALU.min))
        t = first_of(M1[:], LG[:], t)
        t = second_of(t)
        t = first_of(M2[:], G2[:], t)
        t = V.done(V.after(t).tensor_tensor(M1[:], M1[:], M2[:], ALU.add))
        t = V.done(V.after(t).tensor_tensor(CW[:], M1[:], LG[:], ALU.mult))
        t = V.done(V.after(t).tensor_copy(CW3[:, :, 0], CW[:]))
        t = V.done(V.after(t).tensor_tensor(G2[:], CW[:], CW3[:, :, 0], ALU.subtract))
        t = V.done(V.after(t).tensor_copy(CW3[:, :, 1], G2[:]))
        t = V.done(V.after(t).tensor_tensor(CW3[:, :, 2], G2[:], CW3[:, :, 1], ALU.subtract))
        t = V.done(V.after(t).tensor_copy(sel16[:], selr[:]))

        def experts3(L):
            mine = cwT3[L.k]
            t_x = yield from normed(L)
            w = A.done(nc.scalar.copy(L.sq[:, :, 0:12].bitcast(BF16), CW3[:, ds(L.at, CT)].rearrange("p j i e -> p j (i e)")))
            yield
            b = L.bank()
            PE.after(w, L.free.get(b))
            turned = PS[0:3 * E, b, 0:S // 2].bitcast(BF16)
            for j in range(CT):
                mm = nc.tensor.transpose(turned[:, j * P:(j + 1) * P], L.sq[:, j, 0:12].bitcast(BF16), bf["ident"][:])
            t = PE.done(mm)
            yield
            t_c = L.free[b] = A.done(A.after(t).copy(mine[:], turned))
            yield
            t_m = t_dn = None
            PE.after(t_c)
            for e in range(E):
                b, u = product(L, sel16[:, e, :], mine[:])
                x = xeT[L.k][:, e % 2, :]
                t = L.free[b] = V.done(V.after(u, t_x).tensor_tensor(x, bank(b), L.xT[:], ALU.mult))
                yield
                PE.after(t)
                t_g = {}
                for n in (0, 2, 1, 3):
                    b, u = product(L, gu3[:, e, n * P:(n + 1) * P], x)
                    if n < 2:
                        t_g[n] = L.free[b] = A.done(A.after(u, t_m).activation(gate[L.k][:, n, :], bank(b), ACT.Silu))
                    else:
                        t = L.free[b] = V.done(V.after(u, t_g[n - 2], t_dn).tensor_tensor(
                            L.hT[:, n - 2, :], bank(b), gate[L.k][:, n - 2, :], ALU.mult))
                t_m = t
                yield
                PE.after(t)
                for f in range(2):
                    for j in range(CT):
                        mm = nc.tensor.matmul(PS[:, L.out, j * D:(j + 1) * D], L.hT[:, f, j * P:(j + 1) * P], dn3[:, e, f, :],
                                              start=(e == 0 and f == 0 and j == 0), stop=True, skip_group_check=True)
                t_dn = PE.done(mm)
            yield
            t = V.done(V.after(t_dn).tensor_tensor(L.tot[:], chunk(L.out), L.Xc, ALU.add))
            t = V.done(V.after(t).tensor_tensor(L.tot[:], L.tot[:], L.Xc, ALU.add))
            t = yield from layer_norm(L, L.tot, L.Xc, t)
            finish(L, t)

        in_lanes("experts3", experts3)

        OUT.plain(V.here())
        for b in range(B):
            t = OUT.done(nc.sync.dma_start(out[b].rearrange("(j p) d -> p j d", p=P), X[:, b * CT:(b + 1) * CT, :]))
        nc.sync.wait_ge(OUT.sem, t.value())


def layout(x):
    f = np.float32
    a = {k: np.ascontiguousarray(v) for k, v in x.items()}
    o = {"x": a["L0_attn_x"]}
    for n in ("L0_attn_in_proj_w", "L0_attn_out_proj_w", "L0_attn_fc_w", "L0_attn_proj_w", "L0_ffn_w_up", "L0_ffn_w_down"):
        o[n] = np.ascontiguousarray(a[n].T)
    for n in ("L0_attn_norm1_w", "L0_attn_norm2_w"):
        o[n] = a[n].reshape(D, 1)
    perm = np.arange(D).reshape(G, R, HD).transpose(0, 2, 1).reshape(-1)
    for n in ("q_heads", "k_heads"):
        o["L1_attn_" + n] = np.ascontiguousarray(a["L1_attn_" + n].T[:, perm])
    for n in ("v_heads", "output_proj"):
        o["L1_attn_" + n] = np.ascontiguousarray(a["L1_attn_" + n].T)
    for n in ("router_w", "w1", "w2", "b2", "sw1", "sw2", "sb2"):
        o["L1_ffn_" + n] = a["L1_ffn_" + n]
    o["L1_ffn_b1"] = np.ascontiguousarray(a["L1_ffn_b1"].reshape(E, 4, P).transpose(2, 0, 1))
    o["L1_ffn_sb1"] = np.ascontiguousarray(a["L1_ffn_sb1"].reshape(4, P).T)
    w, b = a["L2_attn_W_qkv"], a["L2_attn_b_qkv"]
    o["L2_attn_W_qkv"] = np.ascontiguousarray(np.concatenate([w[:, 0:D][:, perm], w[:, D:2 * D][:, perm], w[:, 2 * D:]], 1))
    o["L2_attn_b_qk"] = np.ascontiguousarray(np.stack([b[0:D][perm], b[D:2 * D][perm]], 1))
    o["L2_attn_b_v"] = np.ascontiguousarray(b[2 * D:])
    o["L2_attn_W_proj"], o["L2_attn_b_proj"] = a["L2_attn_W_proj"], a["L2_attn_b_proj"]
    per = lambda v: np.ascontiguousarray(v.reshape(8, P).T)
    o["L2_ffn_Win"] = np.repeat(a["L2_ffn_Win"], 16, axis=1)
    o["L2_ffn_bin_"] = per(np.repeat(a["L2_ffn_bin_"], 16))
    for n in ("W1", "b1", "W2"):
        o["L2_ffn_" + n] = per(a["L2_ffn_" + n])
    o["L2_ffn_b2"] = a["L2_ffn_b2"].reshape(64, 1)
    o["L2_ffn_Wout"] = a["L2_ffn_Wout"]
    o["L2_ffn_Wout_rep"] = np.ascontiguousarray(np.repeat(a["L2_ffn_Wout"], 16, axis=0).reshape(8, P, D).transpose(1, 0, 2))
    o["L2_ffn_bout"] = a["L2_ffn_bout"]
    w = a["L3_attn_w_qkv"]
    o["L3_attn_w_qkv"] = np.ascontiguousarray(np.concatenate([w[:, 0:D][:, perm], w[:, D:2 * D][:, perm], w[:, 2 * D:]], 1))
    o["L3_attn_w_out"], o["L3_attn_b_out"] = a["L3_attn_w_out"], a["L3_attn_b_out"]
    head = perm // HD
    o["L3_attn_trace_tf"] = np.ascontiguousarray(np.stack(
        [a["L3_attn_attention_trace"].reshape(H)[head], a["L3_attn_temperature_factor"].reshape(H)[head]], 1))
    o["L3_attn_void_k"] = np.ascontiguousarray(a["L3_attn_void_k"].reshape(H, HD).T)
    o["L3_attn_void_v"] = a["L3_attn_void_v"].reshape(H, HD)
    o["L3_ffn_router_w"] = np.ascontiguousarray(a["L3_ffn_router_w"].T)
    o["L3_ffn_ln"] = np.ascontiguousarray(np.stack([a["L3_ffn_ln_gamma"], a["L3_ffn_ln_beta"]], 1))
    o["L3_ffn_gate_up_w"] = np.ascontiguousarray(a["L3_ffn_gate_up_w"].transpose(0, 2, 1))
    o["L3_ffn_down_w"] = np.ascontiguousarray(a["L3_ffn_down_w"].transpose(0, 2, 1))
    i = np.arange(P)
    o["c_select"] = np.ascontiguousarray(np.repeat(np.tile(np.eye(E, dtype=f), (3, 1))[:, :, None], P, axis=2))
    k, q = i[:, None], i[None, :]
    o["c_ident"] = np.eye(P, dtype=f)
    o["c_causal_kq"] = np.where(k > q, NEG, 0).astype(f)
    o["c_causal_qk"] = np.ascontiguousarray(o["c_causal_kq"].T)
    o["c_alibi_kq"] = np.minimum(k - q, 0).astype(f)
    o["c_alibi_qk"] = np.ascontiguousarray(o["c_alibi_kq"].T)
    o["c_headmean"] = np.where(k // HD == q // HD, 1.0 / HD, 0).astype(f)
    o["c_tri"] = (k < q).astype(f)
    o["c_rank"] = np.tile(E - np.arange(E), (P, 1)).astype(f)
    slope = 2.0 ** (-0.5 * (np.arange(H) + 1))
    o["c_slopes"] = np.tile(slope, (P, 1)).astype(f)
    o["c_qscale2"] = (HD ** -0.5 / slope[perm // HD]).reshape(D, 1).astype(f)
    pos = np.arange(S)
    rk, rq = np.zeros((NLIN + 2, S), f), np.zeros((NLIN + 2, S), f)
    for s in range(3):
        own, behind = pos // P == s, pos // P > s
        rk[3 * s][own], rk[3 * s + 1][own], rk[3 * s + 2][own] = pos[own] % P, 1, 1
        rq[3 * s][behind], rq[3 * s + 1][behind] = 1, -(pos[behind] % P)
        rq[3 * s + 2][behind] = -P * (pos[behind] // P - s)
    rk[NLIN:] = 1
    o["c_rows_k"], o["c_rows_q"] = rk, rq
    return o


def kernel(**inputs):
    import concourse.bacc as bacc
    from concourse.bass_utils import run_bass_kernel_spmd

    nc = bacc.Bacc("TRN2", target_bir_lowering=False, num_devices=1)
    arrays, args = {}, {}
    for name, a in layout(inputs).items():
        arrays["in_" + name] = a
        args[name] = nc.dram_tensor("in_" + name, a.shape, mybir.dt.from_np(a.dtype), kind="ExternalInput").ap()
    out = nc.dram_tensor("out_0", (B, S, D), F32, kind="ExternalOutput").ap()
    build_program(nc, args, out)
    r = run_bass_kernel_spmd(nc, [arrays], core_ids=[0])
    return r.results[0]["out_0"]
```

```python
from contextlib import ExitStack, contextmanager

import numpy as np

import concourse.bass as bass
from concourse import mybir

F32 = mybir.dt.float32
BF16 = mybir.dt.bfloat16
ALU = mybir.AluOpType
ACT = mybir.ActivationFunctionType
AX = mybir.AxisListType
ds = bass.ds

P = 128
D = 128
B, S = 4, 512
NT = B * S // P
CT = S // P
H, HD = 16, 8
G, R = 4, 4
E = 8
SCAN = 64
CAP = 640
RES = float(1.0 / np.sqrt(2.0))
EPS32 = float(np.finfo(np.float32).eps)
NEG = -1.0e30
NCOMBO = 72
NLIN = 9


class Track:

    def __init__(self, name, engine, sem, step=1):
        self.name, self.engine, self.sem, self.step = name, engine, sem, step
        self.count = step
        self.gate = None

    def done(self, instruction):
        instruction.then_inc(self.sem, self.step)
        self.count += self.step
        return Token(self, self.count, tuple(LOOPS))

    def here(self):
        return Token(self, self.count, tuple(LOOPS))

    def after(self, *tokens):
        for t in tokens:
            if t is not None:
                self.engine.wait_ge(t.track.sem, t.value())
        return self.engine

    def plain(self, *tokens):
        self.after(*tokens)
        self.engine.sem_inc(self.gate, 1)
        return self.engine


LOOPS = []


class Token:
    def __init__(self, track, count, loops):
        self.track, self.count, self.loops = track, count, loops

    def value(self):
        v = self.count
        for loop in self.loops:
            per = loop.per.get(self.track.name, 0)
            if loop in LOOPS:
                if per:
                    v = loop.i * per + v
            else:
                v = v + (loop.n - 1) * per
        return v


PER = {'layer0': {'vector': 124,
            'scalar': 50,
            'tensor': 50,
            'gpsimd': 28,
            'spill0': 128,
            'spill1': 128,
            'lane0': 1,
            'lane1': 1},
 'a1': {'vector': 84,
        'scalar': 36,
        'tensor': 120,
        'gpsimd': 16,
        'operand0': 64,
        'operand1': 64,
        'operand2': 64,
        'operand3': 64,
        'mrow0': 32,
        'mrow1': 32,
        'mrow2': 32,
        'mrow3': 32},
 'route1': {'vector': 28, 'scalar': 14, 'tensor': 8, 'gpsimd': 4, 'lane0': 1, 'lane1': 1},
 'shared1': {'vector': 4, 'scalar': 12, 'tensor': 12, 'lane0': 1, 'lane1': 1},
 'experts1': {'vector': 4,
              'scalar': 20,
              'tensor': 22,
              'w1in0': 32,
              'w1in1': 32,
              'xin0': 16,
              'xin1': 16,
              'w2in0': 32,
              'w2in1': 32,
              'yout0': 16,
              'yout1': 16,
              'lane0': 1,
              'lane1': 1,
              'turned_x0': 1,
              'turned_x1': 1,
              'used_w10': 1,
              'used_w11': 1},
 'combine1': {'vector': 46,
              'scalar': 8,
              'tensor': 8,
              'gpsimd': 4,
              'spill0': 128,
              'spill1': 128,
              'lane0': 1,
              'lane1': 1},
 'a2': {'vector': 84,
        'scalar': 68,
        'tensor': 120,
        'gpsimd': 16,
        'operand0': 64,
        'operand1': 64,
        'operand2': 64,
        'operand3': 64,
        'mrow0': 32,
        'mrow1': 32,
        'mrow2': 32,
        'mrow3': 32},
 'layer2': {'vector': 68,
            'scalar': 38,
            'tensor': 32,
            'gpsimd': 10,
            'spill0': 128,
            'spill1': 128,
            'lane0': 1,
            'lane1': 1},
 'a3': {'vector': 92,
        'scalar': 40,
        'tensor': 132,
        'gpsimd': 16,
        'operand0': 64,
        'operand1': 64,
        'operand2': 64,
        'operand3': 64,
        'mrow0': 32,
        'mrow1': 32,
        'mrow2': 32,
        'mrow3': 32},
 'route3': {'vector': 52, 'scalar': 12, 'tensor': 8, 'gpsimd': 12, 'lane0': 1, 'lane1': 1},
 'experts3': {'vector': 74, 'scalar': 32, 'tensor': 96, 'gpsimd': 4, 'out': 32, 'lane0': 1, 'lane1': 1}}


class Loop:
    def __init__(self, nc, tracks, n, name):
        self.nc, self.tracks, self.n, self.name, self.per = nc, tracks, n, name, PER.get(name, {})

    @contextmanager
    def run(self):
        with self.nc.Fori(0, self.n) as i:
            self.i = i
            self.start = {t.name: t.count for t in self.tracks}
            LOOPS.append(self)
            yield self
            LOOPS.pop()
        got = {t.name: t.count - self.start[t.name] for t in self.tracks if t.count != self.start[t.name]}
        assert got == self.per, f"{self.name}: a turn counts {got}"
        for t in self.tracks:
            t.count += (self.n - 1) * self.per.get(t.name, 0)


def build_program(nc, args, out):
    ctx = ExitStack()
    with ctx:
        def sb(name, shape, dt=F32):
            return ctx.enter_context(nc.sbuf_tensor(name, shape, dt))

        def sem(name):
            return ctx.enter_context(nc.semaphore(name))

        V = Track("vector", nc.vector, sem("vector"))
        A = Track("scalar", nc.scalar, sem("scalar"))
        PE = Track("tensor", nc.tensor, sem("tensor"))
        PO = Track("gpsimd", nc.gpsimd, sem("gpsimd"))

        PE.gate, A.gate = sem("tensor_gate"), sem("scalar_gate")
        V.gate, PO.gate = sem("vector_gate"), sem("gpsimd_gate")
        sync_gate = sem("sync_gate")
        dma_tracks = []

        def dma(name, engine=None):
            t = Track(name, engine or nc.sync, sem("dma_" + name), 16)
            t.gate = {id(nc.scalar): A.gate, id(nc.gpsimd): PO.gate}.get(id(t.engine), sync_gate)
            dma_tracks.append(t)
            return t

        LD0 = [dma(f"load{i}") for i in range(9)]
        CONST = dma("const")
        SPILLS = [dma("spill0"), dma("spill1")]
        ROWS = dma("rows")
        CAST = dma("cast", nc.gpsimd)
        OUT = dma("out")
        ZERO = dma("zero")
        SCATTER = dma("scatter", nc.gpsimd)
        GATHER = dma("gather", nc.gpsimd)
        W1IN, XIN = ([dma(f"{n}{k}", nc.scalar) for k in range(2)] for n in ("w1in", "xin"))
        W2IN, YOUT = ([dma(f"{n}{k}") for k in range(2)] for n in ("w2in", "yout"))
        tracks = [V, A, PE, PO] + dma_tracks
        from_zero = (CAST, SCATTER, GATHER)
        for t in tracks:
            if t in from_zero:
                t.count = 0
            else:
                t.engine.sem_inc(t.sem, t.step)

        def loop(n, name):
            return Loop(nc, tracks, n, name).run()

        X = sb("X", [P, NT, D])
        zone = sb("zone", [P, 12288])

        def in_zone(at, shape, dt=F32, parts=P):
            n = int(np.prod(shape)) * (2 if dt == BF16 else 4) // 4
            v = zone[0:parts, at:at + n]
            if dt == BF16:
                v = v.bitcast(BF16)
            names = " ".join("abcd"[:len(shape)])
            return v.rearrange(f"p ({names}) -> p {names}", **{"abcd"[i]: shape[i] for i in range(len(shape))})

        ZL = 7680
        keep = sb("keep", [P, 6400])
        PS = ctx.enter_context(nc.psum_tensor("PS", [P, 8, 512], F32))

        def bank(i):
            return PS[:, i, :]

        def chunk(i):
            return PS[:, i, :].rearrange("p (j d) -> p j d", j=CT)

        def flat(t):
            return t.rearrange("p a b -> p (a b)")

        class Lane:

            def __init__(self, k):
                self.k, self.b0 = k, 4 * k
                self.banks = [4 * k, 4 * k + 1, 4 * k + 2]
                self.out = 4 * k + 3
                self.finished = Track(f"lane{k}", nc.vector, sem(f"lane{k}"), 1)
                self.free = {}
                self.turn = 0

                def buf(name, at, shape):
                    return sb(name, [P] + shape) if k == 0 else in_zone(ZL + at, shape)

                self.hT = buf("hT", 0, [4, S])
                self.xn = buf("xn", 2048, [CT, D])
                self.xT = buf("xT", 2560, [S])
                self.tot = buf("tot", 3072, [CT, D])
                self.pair = buf("pair", 3584, [2, S])
                self.x1 = self.pair[:, 0].rearrange("p (j d) -> p j d", j=CT)
                self.sq = self.pair[:, 1].rearrange("p (j d) -> p j d", j=CT)
                self.ss, self.va, self.rs = (sb(f"{n}{k}", [P, CT]) for n in ("ss", "va", "rs"))
                self.bn6 = sb(f"bn6_{k}", [P, CT, 6])
                self.mv = sb(f"mv{k}", [P, CT, 2])

            def bank(self):
                b = self.banks[self.turn % 3]
                self.turn += 1
                return b

        def load(track, name, shape, src):
            t = sb(name, shape)
            track.done(nc.sync.dma_start(t[:], src))
            return t

        LD = LD0
        w_up = load(LD[1], "w_up", [P, 512], args["L0_ffn_w_up"])
        w_dn = load(LD[1], "w_dn", [P, 4, D], args["L0_ffn_w_down"].rearrange("(f p) d -> p f d", p=P))
        for b in range(B):
            x_in = LD[8].done(nc.sync.dma_start(X[:, b * CT:(b + 1) * CT, :], args["x"][b].rearrange("(j p) d -> p j d", p=P)))
        consts = {}
        for name in ("ident", "causal_kq", "causal_qk", "alibi_kq", "alibi_qk", "headmean", "tri"):
            consts[name] = sb("c_" + name, [P, P])
            nc.sync.dma_start(consts[name][:], args["c_" + name]).then_inc(CONST.sem, 16)
            CONST.count += 16
        rank = sb("rank", [P, E])
        slopes = sb("slopes", [P, H])
        qscale2 = sb("qscale2", [P, 1])
        for t, n in ((rank, "c_rank"), (slopes, "c_slopes"), (qscale2, "c_qscale2")):
            nc.sync.dma_start(t[:], args[n]).then_inc(CONST.sem, 16)
            CONST.count += 16
        const_in = CONST.here()
        ident = consts["ident"]

        w_in = load(LD[0], "w_in", [P, 5 * D], args["L0_attn_in_proj_w"])
        w_out0 = load(LD[0], "w_out0", [P, D], args["L0_attn_out_proj_w"])
        w_fc = load(LD[0], "w_fc", [P, 512], args["L0_attn_fc_w"])
        w_pr = load(LD[0], "w_pr", [P, 4, D], args["L0_attn_proj_w"].rearrange("(f p) d -> p f d", p=P))
        n1 = load(LD[0], "n1", [P, 1], args["L0_attn_norm1_w"])
        n2 = load(LD[0], "n2", [P, 1], args["L0_attn_norm2_w"])
        wq1, wk1, wv1, wo1 = [load(LD[2], n, [P, D], args[a]) for n, a in (
            ("wq1", "L1_attn_q_heads"), ("wk1", "L1_attn_k_heads"), ("wv1", "L1_attn_v_heads"), ("wo1", "L1_attn_output_proj"))]

        ones = sb("ones", [P, P])
        onesb = sb("onesb", [P, P], BF16)
        half = sb("half", [P, NT])
        mhalf = sb("mhalf", [P, NT])
        m_one = sb("m_one", [P, NT])
        PO.done(nc.gpsimd.memset(ones[:], 1.0))
        PO.done(nc.gpsimd.memset(onesb[:], 1.0))
        PO.done(nc.gpsimd.memset(half[:], 0.5))
        PO.done(nc.gpsimd.memset(m_one[:], -1.0))
        pool_ready = PO.done(nc.gpsimd.memset(mhalf[:], -0.5))
        bf = {}
        V.after(const_in)
        for name in ("ident", "causal_kq", "causal_qk", "alibi_kq", "alibi_qk", "tri"):
            bf[name] = sb("b_" + name, [P, P], BF16)
            bf_ready = V.done(nc.vector.tensor_copy(bf[name][:], consts[name][:]))
        bcol = {}
        for name, val in (("two", 2.0), ("eps32", EPS32)):
            bcol[name] = sb("bc_" + name, [P, 1])
            bcol_ready = PO.done(nc.gpsimd.memset(bcol[name][:], val))
        PE.after(const_in, pool_ready, bf_ready)
        A.after(bcol_ready, const_in)
        PO.after(pool_ready)
        V.after(bcol_ready)

        SLOTS = E * CAP
        slots_x = nc.dram_tensor("slots_x", (SLOTS, D), F32, kind="Internal").ap()
        slots_y = nc.dram_tensor("slots_y", (SLOTS, D), F32, kind="Internal").ap()
        zeros = sb("zeros", [P, D])
        ZERO.plain(PO.done(nc.gpsimd.memset(zeros[:], 0.0)))
        ZERO.done(nc.sync.dma_start(slots_x.rearrange("(p n) d -> p n d", p=P),
                                    zeros[:].unsqueeze(1).broadcast_to([P, SLOTS // P, D])))

        st = {}

        lanes = [Lane(0), Lane(1)]
        for L in lanes:
            L.finished.engine.sem_inc(L.finished.sem, 1)
            tracks.append(L.finished)

        def join():
            now = [t.here() for t in (V, A, PE, PO)]
            for t in (V, A, PE, PO):
                t.after(*now)

        def in_lanes(name, *layers, lag=2, turns=B // 2, width=CT):
            join()
            with loop(turns, name) as lp:
                running = {}
                picks = "0" * lag + "01" * 200
                done = 0
                for pick in picks + "01" * 200:
                    L = lanes[int(pick)]
                    if L.k not in running:
                        L.at = lp.i * (2 * width) + L.k * width
                        L.Xc = X[:, ds(L.at, CT), :] if width == CT else None
                        L.free, L.turn = {}, 0
                        running[L.k] = stages(L, layers)
                        V.after(L.finished.here())
                        PO.plain(L.finished.here())
                        A.after(L.finished.here(), SPILLS[L.k].here())
                    if running[L.k] is None:
                        continue
                    if next(running[L.k], "end") == "end":
                        running[L.k] = None
                        done += 1
                        if done == 2:
                            break

        def stages(L, layers):
            t = None
            for layer in layers:
                t = yield from layer(L, t)
            V.after(t).sem_inc(L.finished.sem, 1)
            L.finished.count += 1

        def rms_norm(L, src, eps, *ready):
            t = A.done(A.plain(*ready).activation(L.sq[:], src, ACT.Square))
            t = V.done(V.after(t).tensor_reduce(L.ss[:], L.sq[:], AX.X, ALU.add))
            t = PO.done(PO.plain(t).tensor_scalar(L.va[:], L.ss[:], 1.0 / D, eps, ALU.mult, ALU.add))
            t = PO.done(PO.after(t).tensor_tensor(L.rs[:], L.va[:], mhalf[:, 0:CT], ALU.pow))
            yield
            return V.done(V.after(t).tensor_tensor(L.xn[:], src, spread(L.rs), ALU.mult))

        def spread(col):
            return col[:].unsqueeze(2).broadcast_to([P, CT, D])

        def transposed(L, ready, scale=1.0, bias=0.0):
            b = L.bank()
            PE.after(ready)
            for j in range(CT):
                t = nc.tensor.transpose(PS[:, b, j * P:(j + 1) * P], L.xn[:, j, :], ident[:])
            t = PE.done(t)
            yield
            if isinstance(scale, float):
                t = A.done(A.after(t).copy(L.xT[:], bank(b)))
            else:
                t = A.done(A.after(t).activation(L.xT[:], bank(b), ACT.Identity, scale=scale, bias=bias))
            L.free[b] = t
            return t

        def layer_norm(L, src, dst, *ready):
            V.plain(*ready)
            for j in range(CT):
                t = V.done(nc.vector.bn_stats(L.bn6[:, j, :], src[:, j, :]))
            V.plain(t)
            for j in range(CT):
                t = V.done(nc.vector.bn_aggr(L.mv[:, j, :], L.bn6[:, j, :]))
            t = PO.done(PO.plain(t).tensor_scalar(L.va[:], L.mv[:, :, 1], 1.0, 1e-5, ALU.mult, ALU.add))
            t = PO.done(PO.after(t).tensor_tensor(L.rs[:], L.va[:], mhalf[:, 0:CT], ALU.pow))
            yield
            V.after(t)
            for j in range(CT):
                t = V.done(nc.vector.tensor_scalar(dst[:, j, :], src[:, j, :], L.mv[:, j, 0:1], L.rs[:, j:j + 1],
                                                   ALU.subtract, ALU.mult))
            return t

        def product(L, w, x):
            b = L.bank()
            return b, PE.done(PE.after(L.free.get(b)).matmul(bank(b), w, x, start=True, stop=True))

        def token_major(L, ready, lhs, rhs, nf, first=True):
            PE.after(*ready)
            for j in range(CT):
                for f in range(nf):
                    mm = nc.tensor.matmul(PS[:, L.out, j * D:(j + 1) * D], lhs(f, j), rhs(f),
                                          start=(first and f == 0), stop=(f == nf - 1), skip_group_check=not first)
            return PE.done(mm)

        wt = sb("wt", [P, 512])
        wt2 = sb("wt2", [P, 512])
        wsum = sb("wsum", [P, 1])
        thr = sb("thr", [P, 2])
        V.after(LD[1].here())
        PE.after(LD[1].here())
        for w in (w_up[:], flat(w_dn[:])):
            t = V.done(V.after(V.here()).tensor_reduce(wsum[:], w, AX.X, ALU.add, apply_absolute_value=True))
            t = PE.done(PE.after(t, V.here()).matmul(PS[:, 6, 0:1], ones[:], wsum[:], start=True, stop=True))
            t = V.done(V.after(t).tensor_scalar(thr[:, 0:1], PS[:, 6, 0:1], 0.5 / (D * 512), None, ALU.mult))
            t = V.done(V.after(t).tensor_scalar(thr[:, 1:2], thr[:, 0:1], -1.0, None, ALU.mult))
            V.after(t)
            V.done(nc.vector.tensor_scalar(wt[:], w, thr[:, 0:1], None, ALU.is_gt))
            t = V.done(nc.vector.tensor_scalar(wt2[:], w, thr[:, 1:2], None, ALU.is_lt))
            t = V.done(V.after(t).tensor_tensor(wt[:], wt[:], wt2[:], ALU.subtract))
            t = V.done(V.after(t).tensor_tensor(wt[:], wt[:], w, ALU.subtract))
            t_w = V.done(V.after(t).tensor_tensor(w, w, wt[:], ALU.add))
        PE.after(t_w)

        V.after(LD[0].here())
        t1 = V.done(nc.vector.tensor_scalar(w_in[:], w_in[:], n1[:, 0:1], None, ALU.mult))
        t2 = V.done(nc.vector.tensor_scalar(w_fc[:], w_fc[:], n2[:, 0:1], None, ALU.mult))
        w1 = sb("w1", [P, E, 512])
        w2 = sb("w2", [P, E, 4, D])
        tmp = [{n: (in_zone(512 * i, [S]) if k == 0 else w1[:, i, :] if i < E else flat(w2[:, 0])) for i, n in enumerate((
            "v", "k", "a", "g", "q", "clamped", "cut", "heads", "u"))} for k in range(2)]
        t3 = PO.done(nc.gpsimd.memset(tmp[0]["heads"][:], 0.0))
        t4 = PO.done(nc.gpsimd.memset(tmp[1]["heads"][:], 0.0))
        PE.after(t1, t2, LD[0].here())
        V.after(x_in, t3, t4)

        def mixer(L, t):
            T = tmp[L.k]
            t = yield from rms_norm(L, L.Xc, 1e-6, t)
            t = yield from transposed(L, t)
            PE.after(t)
            yield
            (b_k, t_k), (b_a, t_a), (b_g, t_g) = (
                product(L, w_in[:, n * D:(n + 1) * D], L.xT[:]) for n in (1, 3, 4))
            t_k = L.free[b_k] = A.done(A.after(t_k).activation(T["k"][:], bank(b_k), ACT.Tanh))
            b_v, t_v = product(L, w_in[:, 2 * D:3 * D], L.xT[:])
            t_a = L.free[b_a] = A.done(A.after(t_a).activation(T["a"][:], bank(b_a), ACT.Sigmoid, bias=bcol["two"][:, 0:1]))
            b_q, t_q = product(L, w_in[:, 0:D], L.xT[:])
            t_g = L.free[b_g] = A.done(A.after(t_g).activation(T["g"][:], bank(b_g), ACT.Sigmoid))
            t_v = L.free[b_v] = A.done(A.after(t_v).copy(T["v"][:], bank(b_v)))
            t_q = A.done(A.after(t_q).activation(T["q"][:], bank(b_q), ACT.Square))
            yield
            PE.after(t_q)
            b, t = product(L, consts["headmean"][:], T["q"][:])
            yield
            t = L.free[b] = A.done(A.after(t).activation(T["q"][:], bank(b), ACT.Ln, bias=bcol["eps32"][:, 0:1]))
            t_r = A.done(A.after(t).activation(T["q"][:], T["q"][:], ACT.Exp, scale=-0.5))
            heads = lambda x: x[:].rearrange("p (c s) -> p c s", s=SCAN)[:, :, 0:1]
            t_u = V.done(V.after(t_k, t_v).tensor_tensor(T["u"][:], T["k"][:], T["v"][:], ALU.mult))
            t = V.done(V.after(t_a).tensor_scalar(T["clamped"][:], T["a"][:], 0.6, 0.9995, ALU.max, ALU.min))
            V.after(t)
            V.done(nc.vector.tensor_copy(T["cut"][:], T["clamped"][:]))
            t = V.done(nc.vector.tensor_copy(heads(T["heads"]), heads(T["clamped"])))
            t = V.done(V.after(t).memset(heads(T["cut"]), 0.0))
            pre = T["a"]
            t = V.done(V.after(t).tensor_tensor_scan(pre[:], T["cut"][:], T["heads"][:], 0.0, ALU.mult, ALU.add))
            t = V.done(V.after(t).tensor_scalar(pre[:], pre[:], 1e6, 1.0, ALU.mult, ALU.min))
            t = V.done(V.after(t, t_u).tensor_tensor(T["u"][:], T["u"][:], pre[:], ALU.mult))
            mem = T["cut"]
            t = V.done(V.after(t).tensor_tensor_scan(mem[:], T["clamped"][:], T["u"][:], 0.0, ALU.mult, ALU.add))
            yy = T["k"]
            t2 = V.done(V.after(t_r, t_q).tensor_tensor(T["q"][:], bank(b_q), T["q"][:], ALU.mult))
            t = V.done(V.after(t, t2).tensor_tensor(yy[:], T["q"][:], mem[:], ALU.mult))
            t = V.done(V.after(t).tensor_tensor(yy[:], yy[:], T["v"][:], ALU.subtract))
            t = V.done(V.after(t, t_g).tensor_tensor(yy[:], yy[:], T["g"][:], ALU.mult))
            t = V.done(V.after(t).tensor_tensor(yy[:], yy[:], T["v"][:], ALU.add))
            yield
            t = token_major(L, (t,), lambda f, j: yy[:, j * P:(j + 1) * P], lambda f: w_out0[:], 1)
            yield
            t = V.done(V.after(t).scalar_tensor_tensor(L.x1[:], chunk(L.out), RES, L.Xc, ALU.mult, ALU.add))
            L.free[b_q] = t
            t = yield from rms_norm(L, L.x1[:], 1e-6, t)
            t = yield from transposed(L, t)
            yield
            PE.after(t)
            for n in range(4):
                b, t = product(L, w_fc[:, n * P:(n + 1) * P], L.xT[:])
                t_h = L.free[b] = A.done(A.after(t).activation(L.hT[:, n, :], bank(b), ACT.Silu))
            yield
            t = token_major(L, (t_h,), lambda f, j: L.hT[:, f, j * P:(j + 1) * P], lambda f: w_pr[:, f, :], 4)
            yield
            t = V.done(V.after(t).scalar_tensor_tensor(L.tot[:], chunk(L.out), RES, L.x1[:], ALU.mult, ALU.add))
            t = V.done(V.after(t).tensor_tensor(L.tot[:], L.tot[:], L.Xc, ALU.add))
            t = yield from layer_norm(L, L.tot, L.Xc, t)
            return t

        ssp = [sb(f"ssp{k}", [P, CT]) for k in range(2)]
        hsq = [in_zone(0, [4, S]), w1[:, 0:4, :]]

        def inv_rms(L, ready, src, n):
            t = PO.done(PO.plain(ready).tensor_scalar(L.va[:], src, 1.0 / n, 0.0, ALU.mult, ALU.add))
            t = PO.done(PO.after(t).tensor_tensor(L.rs[:], L.va[:], half[:, 0:CT], ALU.pow))
            t = PO.done(PO.plain(t).tensor_scalar(L.va[:], L.rs[:], 1.0, 1e-8, ALU.mult, ALU.add))
            yield
            return V.done(V.after(t).reciprocal(L.rs[:], L.va[:]))

        def ternary(L, t):
            t = V.done(V.after(t).tensor_tensor(L.sq[:], L.Xc, L.Xc, ALU.mult))
            t = V.done(V.after(t).tensor_reduce(L.ss[:], L.sq[:], AX.X, ALU.add))
            t = yield from inv_rms(L, t, L.ss[:], D)
            t = V.done(V.after(t).tensor_tensor(L.xn[:], L.Xc, spread(L.rs), ALU.mult))
            t = yield from transposed(L, t)
            yield
            PE.after(t)
            for n in range(4):
                b, t = product(L, w_up[:, n * P:(n + 1) * P], L.xT[:])
                t_h = L.free[b] = A.done(A.after(t).activation(L.hT[:, n, :], bank(b), ACT.Gelu))
            t_s = A.done(A.after(t_h).activation(hsq[L.k][:], L.hT[:], ACT.Square))
            yield
            t_o = token_major(L, (t_h,), lambda f, j: L.hT[:, f, j * P:(j + 1) * P], lambda f: w_dn[:, f, :], 4)
            yield
            b = L.bank()
            PE.after(t_s, L.free.get(b))
            for j in range(CT):
                for f in range(4):
                    mm = nc.tensor.matmul(PS[:, b, j:j + 1], hsq[L.k][:, f, j * P:(j + 1) * P], ones[:, 0:1],
                                          start=(f == 0), stop=(f == 3))
            t = PE.done(mm)
            yield
            t = V.done(V.after(t).tensor_copy(ssp[L.k][:], PS[:, b, 0:CT]))
            t = yield from inv_rms(L, t, ssp[L.k][:], 512)
            V.after(t, t_o)
            for j in range(CT):
                t = V.done(nc.vector.scalar_tensor_tensor(L.tot[:, j, :], chunk(L.out)[:, j, :], L.rs[:, j:j + 1],
                                                          X[:, ds(L.at + j, 1), :].rearrange("p a d -> p (a d)"),
                                                          ALU.mult, ALU.add))
            t = yield from layer_norm(L, L.tot, L.Xc, t)
            return t

        scratch = nc.dram_tensor("score_parts", (2, B * G, 3, HD * R, S), BF16, kind="Internal").ap()
        VT = B * G * CT * R * (HD + 1)
        Vt = keep[:, 0:VT].rearrange("p (u j r d) -> p u j r d", u=B * G, j=CT, r=R)
        O = keep[:, VT:VT + 2048].rearrange("p (u j r d) -> p u j r d", u=B * G, j=CT, r=R)
        parts = [sb("parts", [P, 2, 3, S], BF16), in_zone(8192, [2, 3, S], BF16)]
        NB = 4
        OQ = in_zone(0, [NB, R, S], BF16, 96)
        OK = in_zone(4096, [NB, R, S], BF16, 96)
        VS = keep[:, VT + 2048:VT + 4096].rearrange("p (s j r d) -> p s j r d", s=NB, j=CT, r=R)
        PB = in_zone(8192, [2, R, S])
        oT = sb("oT", [P, S])
        negm = sb("negm", [P, R * CT])
        nmp = sb("nmp", [P, 2, R * CT], BF16)
        mT = sb("mT", [32, NB, P], BF16)
        rden = sb("rden", [P, R * CT])
        OPER = [dma(f"operand{i}") for i in range(NB)]
        MROW = [dma(f"mrow{i}") for i in range(NB)]
        for t in OPER + MROW:
            t.engine.sem_inc(t.sem, t.step)
            tracks.append(t)
        join()
        t_vt = PO.done(nc.gpsimd.memset(Vt[:], 1.0))
        t_vs = PO.done(nc.gpsimd.memset(VS[:], 0.0))
        V.after(t_vt)
        PO.after(t_vt, t_vs)
        rows16 = nc.dram_tensor("rows16", (2, NLIN + 2, S), BF16, kind="Internal").ap()
        CAST.done(nc.gpsimd.dma_start(rows16[0], args["c_rows_q"]))
        t_rows16 = CAST.done(nc.gpsimd.dma_start(rows16[1], args["c_rows_k"]))
        ROWS.plain(t_rows16)

        def constant_rows(lin):
            KR = NCOMBO + (NLIN if lin else 0)
            ROWS.plain(PE.here(), V.here(), A.here())
            for dst, src in ([(OQ[NCOMBO:KR], rows16[0, 0:NLIN]), (OK[NCOMBO:KR], rows16[1, 0:NLIN])] if lin else []) + [
                    (OK[KR:KR + 2], rows16[1, NLIN:NLIN + 2])]:
                ROWS.done(nc.sync.dma_start(dst.rearrange("p s r q -> p (s r) q"),
                                            src.unsqueeze(1).broadcast_to([src.shape[0], NB * R, S])))

        def attention_prep(wq, wk, wv, qs, qb=None, kb=None, vb=None):
            def prep(L, t):
                mine = parts[L.k]
                t = A.done(A.plain(t).copy(L.xn[:], L.Xc))
                t = yield from transposed(L, t)
                PE.after(t)
                yield
                ends = [product(L, w, L.xT[:]) for w in (wq, wk)]
                t_v = token_major(L, (), lambda f, j: L.xT[:, j * P:(j + 1) * P], lambda f: wv, 1)
                for n, (sc, bi) in enumerate(((qs, qb), (1.0, kb))):
                    bi = 0.0 if bi is None else bi
                    A.after(ends[n][1])
                    nc.scalar.activation(mine[:, n, 0, :], bank(ends[n][0]), ACT.Identity, scale=sc, bias=bi)
                    t = A.done(nc.scalar.activation(L.pair[:, n, :], bank(ends[n][0]), ACT.Identity, scale=sc, bias=bi))
                yield
                t = V.done(V.after(t).tensor_tensor(L.pair[:], L.pair[:], mine[:, :, 0, :], ALU.subtract))
                t = V.done(V.after(t).tensor_copy(mine[:, :, 1, :], L.pair[:]))
                t = V.done(V.after(t).tensor_tensor(mine[:, :, 2, :], L.pair[:], mine[:, :, 1, :], ALU.subtract))
                T = SPILLS[L.k]
                T.plain(t)
                for n in range(2):
                    for g in range(G):
                        T.done(nc.sync.dma_start(scratch[n, ds(L.at + g, 1)].rearrange("a i x q -> x (a i) q"),
                                                 mine[32 * g:32 * g + 32, n]))
                V.after(t_v)
                for j in range(CT):
                    o = Vt[:, ds(L.at, G), j, :, 0:HD]
                    i_ = chunk(L.out)[:, j, :].rearrange("p (g r d) -> p g r d", g=G, r=R)
                    if vb is None:
                        t = V.done(nc.vector.tensor_copy(o, i_))
                    else:
                        t = V.done(nc.vector.tensor_tensor(o, i_, vb.rearrange("p (g r d) -> p g r d", g=G, r=R), ALU.add))
                return t

            return prep

        def attention(name, causal=False, diag_kq=None, diag_qk=None, slope=None, void=None, lin=False):
            KR = NCOMBO + (NLIN if lin else 0)
            KM = KR + 2
            spilled = [t.here() for t in SPILLS]
            join()
            PE.after(ROWS.here())
            last = {}

            def ring_slot():
                n = last["ring"]
                last["ring"] = n + 1
                PE.after(last[("ring", n % 3)])
                return n % 3

            def load(u, s):
                T = OPER[s]
                T.plain(last[("oper", s)], *spilled)
                unit = scratch[:, ds(u, 1)] if not isinstance(u, int) else scratch[:, u:u + 1]
                T.done(nc.sync.dma_start(
                    OQ[0:NCOMBO, s].rearrange("a r q -> a (r q)"),
                    unit[0].rearrange("o i (a r) q -> (o i a) (r q)", r=R).unsqueeze(1).broadcast_to([3 * HD, 3, R * S])))
                for i in range(3):
                    t = T.done(nc.sync.dma_start(
                        OK[24 * i:24 * i + 24, s].rearrange("a r q -> a (r q)"),
                        unit[1].rearrange("o j (a r) q -> a (o j) (r q)", r=R)))
                last[("loaded", s)] = t

            def load_values(u, s):
                src = Vt[:, ds(u, 1)] if not isinstance(u, int) else Vt[:, u:u + 1]
                PO.after(last[("vs", s)])
                for kt in range(CT):
                    t = PO.done(nc.gpsimd.tensor_copy(VS[:, s, kt, :, 0:HD + 1],
                                                      src[:, :, kt].rearrange("p a r d -> p (a r) d")))
                last[("vs_in", s)] = t

            def max_slot(s, n):
                qt, r = n // R, n % R
                b = ring_slot()
                if n == 0:
                    PE.after(last[("loaded", s)])
                nk = (qt + 1) * P if causal else S
                diag = diag_qk is not None
                mm = nc.tensor.matmul(PS[:, b, 0:nk], OQ[0:KR, s, r, qt * P:(qt + 1) * P], OK[0:KR, s, r, 0:nk],
                                      start=True, stop=True)
                if diag:
                    mm = nc.tensor.matmul(PS[:, b, qt * P:(qt + 1) * P], bf["ident"][:], diag_qk[:],
                                          start=False, stop=True, skip_group_check=True)
                t = PE.done(mm)
                k = r * CT + qt
                t = V.done(V.after(t, last["nmp"] if n == 0 else None).tensor_reduce(
                    negm[:, k:k + 1], PS[:, b, 0:nk], AX.X, ALU.max, negate=True))
                last[("ring", b)] = t
                return t

            def max_void(s, g):
                b = ring_slot()
                for r in range(R):
                    for qt in range(CT):
                        k = r * CT + qt
                        mm = nc.tensor.matmul(PS[:, b, k:k + 1], OQ[0:KR, s, r, qt * P:(qt + 1) * P],
                                              void[0][0:KR, g, r, 0:1], start=True, stop=True, skip_group_check=True)
                t = PE.done(mm)
                t = V.done(V.after(t).tensor_scalar(rden[:], PS[:, b, 0:16], -1.0, None, ALU.mult))
                last[("ring", b)] = t
                return V.done(V.after(t, V.here()).tensor_tensor(negm[:], negm[:], rden[:], ALU.min))

            def max_rows(s, t):
                t = V.done(V.after(t, last["nmp_pe"]).tensor_copy(nmp[:, 0, :], negm[:]))
                t = V.done(V.after(t).tensor_tensor(nmp[:, 1, :], negm[:], nmp[:, 0, :], ALU.subtract))
                last["nmp"] = t
                b = ring_slot()
                pt = PS[0:32, b, 0:64].bitcast(BF16)
                t = PE.done(PE.after(t).transpose(pt, nmp[:].rearrange("p a b -> p (a b)"), bf["ident"][:]))
                last["nmp_pe"] = t
                t = V.done(V.after(t, last[("mrow", s)]).tensor_copy(mT[:, s, :], pt))
                last[("ring", b)] = t
                MROW[s].plain(t, last[("oper", s)])
                for i in range(2):
                    t = MROW[s].done(nc.sync.dma_start(
                        OQ[KR + i:KR + i + 1, s].rearrange("a r (t q) -> a (r t) q", t=CT), mT[16 * i:16 * i + 16, s, :]))
                last[("mrow", s)] = t

            def scores(s, kt, rp):
                q0 = kt * P if causal else 0
                if kt == 0 and rp == 0:
                    PE.after(last[("mrow", s)])
                PE.after(last[("pair", rp)])
                for r in (2 * rp, 2 * rp + 1):
                    b = 3 + r
                    diag = diag_kq is not None
                    mm = nc.tensor.matmul(PS[:, b, q0:S], OK[0:KM, s, r, kt * P:(kt + 1) * P], OQ[0:KM, s, r, q0:S],
                                          start=True, stop=True)
                    if diag:
                        mm = nc.tensor.matmul(PS[:, b, kt * P:(kt + 1) * P], bf["ident"][:], diag_kq[:],
                                              start=False, stop=True, skip_group_check=True)
                t = PE.done(mm)
                if kt == CT - 1 and rp == 1 and void is None:
                    last[("oper", s)] = t
                A.after(t, last[("pb", kt % 2)])
                if slope is None:
                    t = A.done(nc.scalar.activation(PB[:, kt % 2, 2 * rp:2 * rp + 2, q0:S],
                                                    PS[:, 3 + 2 * rp:5 + 2 * rp, q0:S], ACT.Exp))
                else:
                    for r in (2 * rp, 2 * rp + 1):
                        t = A.done(nc.scalar.activation(PB[:, kt % 2, r, q0:S], PS[:, 3 + r, q0:S], ACT.Exp,
                                                        scale=slope(s, r)))
                last[("pair", rp)] = t
                last[("exp", kt)] = t

            def values(s, kt):
                q0 = kt * P if causal else 0
                PE.after(last[("exp", kt)])
                if kt == 0:
                    PE.after(last["acc"], last[("vs_in", s)])
                for r in range(R):
                    mm = nc.tensor.matmul(PS[32 * r:32 * r + 32, 7, q0:S], VS[:, s, kt, r, :], PB[:, kt % 2, r, q0:S],
                                          start=(kt == 0), stop=True, skip_group_check=True)
                t = PE.done(mm)
                last[("pb", kt % 2)] = t
                last[("vs", s)] = t
                last["acc_in"] = t

            def void_key(s, g):
                PE.after(last[("pair", 0)])
                for r in range(R):
                    mm = nc.tensor.matmul(PS[32 * r:32 * r + 32, 3, :], void[0][0:KM, g, r, :], OQ[0:KM, s, r, :],
                                          start=True, stop=True, skip_group_check=True)
                t = PE.done(mm)
                last[("oper", s)] = t
                t = A.done(A.after(t, last["pvo"]).activation(pvo[:], bank(3), ACT.Exp))
                last[("pair", 0)] = t
                last["pvo_in"] = t

            def void_value(g):
                t = PE.done(PE.after(last["pvo_in"]).matmul(bank(7), void[1][:, g, :], pvo[:], start=False, stop=True,
                                                            skip_group_check=True))
                last["pvo"] = t
                last["acc_in"] = t

            def evacuate():
                t = A.done(A.after(last["acc_in"], last["oT"]).copy(oT[:], bank(7)))
                last["acc"] = t
                last["oT_in"] = t

            def normalise(u):
                b = ring_slot()
                PE.after(last["oT_in"])
                for j in range(CT):
                    mm = nc.tensor.transpose(PS[:, b, j * P:(j + 1) * P], oT[:, j * P:(j + 1) * P], ident[:])
                t = PE.done(mm)
                last["oT"] = t
                acc = bank(b).rearrange("p (x d) -> p x d", d=32)
                t = V.done(V.after(t, last["rden"]).reciprocal(rden[:].unsqueeze(2), acc[:, :, HD:HD + 1]))
                dst = O[:, ds(u, 1)].rearrange("p a t r d -> p (a t r) d") if not isinstance(u, int) else \
                    O[:, u].rearrange("p t r d -> p (t r) d")
                t = V.done(V.after(t).tensor_tensor(dst, acc[:, :, 0:HD],
                                                    rden[:].unsqueeze(2).broadcast_to([P, R * CT, HD]), ALU.mult))
                last["rden"] = t
                last[("ring", b)] = t

            def step(s, u_exp=None, u_max=None, u_norm=None, u_load=None, finish=None):
                s2, s0 = (s + 2) % NB, (s - 1) % NB
                if u_load is not None:
                    load(u_load, s0)
                t = None
                for n in range(2 * CT):
                    kt, rp = n // 2, n % 2
                    if u_max is not None:
                        max_slot(s2, 2 * n)
                        t = max_slot(s2, 2 * n + 1)
                    if u_exp is not None:
                        scores(s, kt, rp)
                    if n == 0 and u_norm is not None:
                        values(s0, CT - 1)
                        if void is not None:
                            void_value(s0)
                        evacuate()
                    if n == 0 and u_load is not None:
                        load_values(u_load, s0)
                    if n == 2 and u_norm is not None:
                        normalise(u_norm)
                    if rp == 1 and kt > 0 and u_exp is not None:
                        values(s, kt - 1)
                if u_exp is not None and void is not None:
                    void_key(s, s)
                if u_max is not None:
                    if void is not None:
                        t = max_void(s2, s2)
                    max_rows(s2, t)

            def fresh():
                now = {"V": V.here(), "A": A.here(), "PE": PE.here(), "PO": PO.here()}
                last["ring"] = 0
                for b in range(3):
                    last[("ring", b)] = now["V"]
                for s in range(NB):
                    last[("oper", s)] = now["PE"]
                    last[("vs", s)] = now["PE"]
                    last[("vs_in", s)] = now["PO"]
                    last[("loaded", s)] = OPER[s].here()
                    last[("mrow", s)] = MROW[s].here()
                for b in range(2):
                    last[("pair", b)] = now["A"]
                    last[("pb", b)] = now["PE"]
                for kt in range(CT):
                    last[("exp", kt)] = now["A"]
                last["nmp"] = last["rden"] = now["V"]
                last["nmp_pe"] = now["PE"]
                last["acc"] = last["oT_in"] = last["pvo_in"] = now["A"]
                last["acc_in"] = last["oT"] = last["pvo"] = now["PE"]

            fresh()
            for u in range(2):
                load(u, u)
                load_values(u, u)
            step(NB - 2, u_max=0)
            load(2, 2)
            load_values(2, 2)
            step(NB - 1, u_max=1)
            step(0, u_exp=0, u_max=2, u_load=3)
            with loop(B - 1, name) as lp:
                fresh()
                for g in range(G):
                    u = lp.i * G + (g + 1)
                    step((g + 1) % G, u_exp=u, u_max=u + 2, u_norm=lp.i * G + g if g else lp.i * G, u_load=u + 3)
            fresh()
            for u in range(B * G - 3, B * G):
                step(u % G, u_exp=u, u_max=u + 2 if u + 2 < B * G else None, u_norm=u - 1,
                     u_load=u + 3 if u + 3 < B * G else None)
            step(0, u_norm=B * G - 1)

        def attention_out(wo, bias=None):
            def out_stages(L, t):
                t_b = t
                if bias is not None:
                    t_b = PO.done(PO.plain(t).tensor_tensor(L.x1[:], L.Xc, bias.unsqueeze(1).broadcast_to([P, CT, D]), ALU.add))
                A.plain(t)
                for j in range(CT):
                    t = A.done(nc.scalar.copy(
                        L.xn[:, j, :].rearrange("p (g x) -> p g x", g=G),
                        O[:, ds(L.at, G), j].rearrange("p g r d -> p g (r d)")))
                t = yield from transposed(L, t)
                yield
                t = token_major(L, (t,), lambda f, j: L.xT[:, j * P:(j + 1) * P], lambda f: wo, 1)
                yield
                t = V.done(V.after(t, t_b).tensor_tensor(L.tot[:], chunk(L.out), L.Xc if bias is None else L.x1[:], ALU.add))
                t = yield from layer_norm(L, L.tot, L.Xc, t)
                return t

            return out_stages

        PE.after(LD[2].here())
        in_lanes("layer0", mixer, ternary, attention_prep(wq1[:], wk1[:], wv1[:], HD ** -0.5))
        join()
        constant_rows(False)
        attention("a1", causal=True, diag_kq=bf["causal_kq"], diag_qk=bf["causal_qk"])


        LG = sb("LG", [P, NT, E])
        M1 = sb("M1", [P, NT, E])
        M2 = sb("M2", [P, NT, E])
        G2 = sb("G2", [P, NT, E])
        mk = sb("mk", [P, NT])
        mk2 = sb("mk2", [P, NT])
        M1b = sb("M1b", [P, NT, E], BF16)
        trib, oneb = bf["tri"], onesb

        def router_logits(L, t, w):
            PE.after(t)
            for j in range(CT):
                mm = nc.tensor.matmul(PS[:, L.out, j * E:(j + 1) * E], L.xT[:, j * P:(j + 1) * P], w[:], start=True, stop=True)
            return PE.done(mm), PS[:, L.out, 0:CT * E].rearrange("p (j e) -> p j e", e=E)

        def over(col):
            return col[:].unsqueeze(2).broadcast_to([P, NT, E])

        def softmax(t, eps=0.0):
            t = V.done(V.after(t).tensor_reduce(mk[:], LG[:], AX.X, ALU.max))
            t = V.done(V.after(t).tensor_tensor(LG[:], LG[:], over(mk), ALU.subtract))
            t = A.done(A.after(t).activation(LG[:], LG[:], ACT.Exp))
            t = V.done(V.after(t).tensor_reduce(mk[:], LG[:], AX.X, ALU.add))
            if eps:
                t = V.done(V.after(t).tensor_scalar(mk[:], mk[:], eps, None, ALU.add))
            t = V.done(V.after(t).reciprocal(mk[:], mk[:]))
            return V.done(V.after(t).tensor_tensor(LG[:], LG[:], over(mk), ALU.mult))

        def first_of(dst, src, t):
            t = V.done(V.after(t).tensor_reduce(mk[:], src, AX.X, ALU.max))
            t = V.done(V.after(t).tensor_tensor(dst, src, over(mk), ALU.is_equal))
            t = V.done(V.after(t).tensor_tensor(dst, dst, rank[:].unsqueeze(1).broadcast_to([P, NT, E]), ALU.mult))
            t = V.done(V.after(t).tensor_reduce(mk[:], dst, AX.X, ALU.max))
            return V.done(V.after(t).tensor_tensor(dst, dst, over(mk), ALU.is_equal))

        def top2(t):
            t = first_of(M1[:], LG[:], t)
            t = V.done(V.after(t).tensor_scalar(G2[:], M1[:], -1.0, 1.0, ALU.mult, ALU.add))
            t = V.done(V.after(t).tensor_tensor(G2[:], G2[:], LG[:], ALU.mult))
            return first_of(M2[:], G2[:], t)

        rw1 = load(LD[3], "rw1", [P, E], args["L1_ffn_router_w"])
        s1 = load(LD[3], "s1", [P, 512], args["L1_ffn_sw1"])
        s2 = load(LD[3], "s2", [P, 4, D], args["L1_ffn_sw2"].rearrange("(f p) d -> p f d", p=P))
        sb1 = load(LD[3], "sb1", [P, 4], args["L1_ffn_sb1"])
        sb2 = load(LD[3], "sb2", [P, D], args["L1_ffn_sb2"].unsqueeze(0).broadcast_to([P, D]))
        slot_row = sb("slot_row", [P, E])
        scatter_to = sb("scatter_to", [P, 2, NT], mybir.dt.uint32)
        gather_from = sb("gather_from", [P, 2, NT], mybir.dt.uint32)
        slot = sb("slot", [P, NT])
        kept = sb("kept", [P, NT])
        share = sb("share", [P, 2, NT])
        PE.after(LD[3].here())
        A.after(LD[3].here())
        V.after(LD[3].here())

        def route1(L, t):
            t = A.done(A.plain(t).copy(L.xn[:], L.Xc))
            t = yield from transposed(L, t)
            yield
            t, pos = router_logits(L, t, rw1)
            yield
            t = V.done(V.after(t).tensor_copy(LG[:, ds(L.at, CT), :], pos))
            return t

        in_lanes("route1", attention_out(wo1[:]), route1, lag=0)
        join()
        t = softmax(V.here())
        t = top2(t)

        def earlier(mask, t):
            t = V.done(V.after(t).tensor_copy(M1b[:], mask))
            PE.after(t)
            pos = PS[:, 6, 0:NT * E].rearrange("p (j e) -> p j e", e=E)
            mm = nc.tensor.matmul(pos, trib[:], M1b[:], start=True, stop=True)
            for j in range(NT - 1):
                mm = nc.tensor.matmul(pos[:, j + 1:NT], oneb[:], M1b[:, j:j + 1].broadcast_to([P, NT - 1 - j, E]),
                                      start=False, stop=True, skip_group_check=True)
            return mm, pos

        t = V.done(V.after(t).tensor_scalar(slot_row[:], rank[:], -float(CAP), float(CAP * E), ALU.mult, ALU.add))

        def slots_of(c, M, pos, t):
            t = V.done(V.after(t).tensor_scalar(G2[:], pos, float(CAP), None, ALU.is_lt))
            t = V.done(V.after(t).tensor_tensor(M[:], M[:], G2[:], ALU.mult))
            t = V.done(V.after(t).tensor_tensor(G2[:], pos, slot_row[:].unsqueeze(1).broadcast_to([P, NT, E]), ALU.add))
            t = V.done(V.after(t).tensor_tensor(G2[:], G2[:], M[:], ALU.mult))
            t = V.done(V.after(t).tensor_reduce(slot[:], G2[:], AX.X, ALU.add))
            t = V.done(V.after(t).tensor_copy(gather_from[:, c], slot[:]))
            t = V.done(V.after(t).tensor_reduce(kept[:], M[:], AX.X, ALU.add))
            t = V.done(V.after(t).tensor_scalar(kept[:], kept[:], -2.0 * SLOTS, 2.0 * SLOTS, ALU.mult, ALU.add))
            t = V.done(V.after(t).tensor_tensor(slot[:], slot[:], kept[:], ALU.add))
            return V.done(V.after(t).tensor_copy(scatter_to[:, c], slot[:]))

        def scatter(c, t):
            for j in range(NT):
                SCATTER.done(SCATTER.after(t if j == 0 else None).indirect_dma_start(
                    slots_x, bass.IndirectOffsetOnAxis(ap=scatter_to[:, c, j:j + 1], axis=0), X[:, j, :], None,
                    bounds_check=SLOTS - 1, oob_is_err=False))

        mm, pos = earlier(M1[:], t)
        t = slots_of(0, M1, pos, PE.done(mm))
        PO.after(ZERO.here())
        scatter(0, t)
        mm, pos = earlier(M2[:], t)
        t = PE.done(mm)
        t = V.done(V.after(t).tensor_copy(M1b[:], M1[:]))
        PE.after(t)
        for j in range(NT):
            mm = nc.tensor.matmul(pos, oneb[:], M1b[:, j:j + 1].broadcast_to([P, NT, E]),
                                  start=False, stop=True, skip_group_check=True)
        t = slots_of(1, M2, pos, PE.done(mm))
        scatter(1, t)
        for c, M in ((0, M1), (1, M2)):
            t = V.done(V.after(t).tensor_tensor(M[:], M[:], LG[:], ALU.mult))
            t = V.done(V.after(t).tensor_reduce(share[:, c], M[:], AX.X, ALU.add))
        t = V.done(V.after(t).tensor_tensor(mk[:], share[:, 0], share[:, 1], ALU.add))
        t = V.done(V.after(t).tensor_scalar(mk[:], mk[:], EPS32, None, ALU.max))
        t = V.done(V.after(t).reciprocal(mk2[:], mk[:]))
        t = V.done(V.after(t).tensor_tensor(share[:], share[:], mk2[:].unsqueeze(1).broadcast_to([P, 2, NT]), ALU.mult))

        Y = keep[:, VT:VT + 2048].rearrange("p (t d) -> p t d", t=NT)

        def shared(L, t):
            t = A.done(A.plain(t).copy(L.xn[:], L.Xc))
            t = yield from transposed(L, t)
            yield
            PE.after(t)
            for n in range(4):
                b, t = product(L, s1[:, n * P:(n + 1) * P], L.xT[:])
                t = L.free[b] = A.done(A.after(t).activation(L.hT[:, n, :], bank(b), ACT.Silu, bias=sb1[:, n:n + 1]))
            yield
            t = token_major(L, (t,), lambda f, j: L.hT[:, f, j * P:(j + 1) * P], lambda f: s2[:, f, :], 4)
            yield
            t = V.done(V.after(t).tensor_tensor(L.tot[:], chunk(L.out), sb2[:].unsqueeze(1).broadcast_to([P, CT, D]), ALU.add))
            t = V.done(V.after(t).scalar_tensor_tensor(Y[:, ds(L.at, CT), :], L.tot[:], 0.1, L.Xc, ALU.mult, ALU.add))
            return t

        in_lanes("shared1", shared)

        ET = CAP // P
        HALF = CAP // 2
        eh = [in_zone(0, [4, CAP]), flat(w1[:])[:, 0:4 * CAP].rearrange("p (f s) -> p f s", f=4)]
        ex, exT, ey = ([in_zone(2560 + 1920 * k + 640 * i, sh) for k in range(2)]
                       for i, sh in enumerate(([ET, D], [CAP], [ET, D])))
        w2f = w2[:].rearrange("p e f d -> p (e f d)")
        ew1 = [w2f[:, 1536 * k:1536 * k + 512] for k in range(2)]
        ew2 = [w2f[:, 1536 * k + 512:1536 * k + 1024].rearrange("p (f d) -> p f d", f=4) for k in range(2)]
        eb2 = [w2f[:, 1536 * k + 1024:1536 * k + 1152] for k in range(2)]
        eb1 = [w2f[:, 1536 * k + 1152:1536 * k + 1156] for k in range(2)]
        turned_x, used_w1 = ([Track(f"{n}{k}", nc.scalar, sem(f"{n}{k}"), 1) for k in range(2)]
                             for n in ("turned_x", "used_w1"))
        for T in turned_x + used_w1:
            T.engine.sem_inc(T.sem, 1)
            tracks.append(T)

        def passed(T, t):
            T.after(t).sem_inc(T.sem, 1)
            T.count += 1

        def expert1(L, t):
            k = L.k
            e = ds(L.at, 1)
            XIN[k].plain(turned_x[k].here(), SCATTER.here())
            x_in = XIN[k].done(nc.scalar.dma_start(
                ex[k][:], slots_x[ds(L.at * CAP, CAP)].rearrange("(j p) d -> p j d", p=P)))
            W1IN[k].plain(used_w1[k].here())
            W1IN[k].done(nc.scalar.dma_start(ew1[k][:], args["L1_ffn_w1"][e].rearrange("e d f -> d (e f)")))
            w1_in = W1IN[k].done(nc.scalar.dma_start(eb1[k][:], args["L1_ffn_b1"][e].rearrange("e p f -> p (e f)")))
            W2IN[k].plain(L.finished.here())
            W2IN[k].done(nc.sync.dma_start(ew2[k][:], args["L1_ffn_w2"][e].rearrange("e (f p) d -> p (e f) d", p=P)))
            w2_in = W2IN[k].done(nc.sync.dma_start(eb2[k][:], args["L1_ffn_b2"][e].broadcast_to([P, D])))
            b, b4 = L.bank(), L.bank()
            PE.after(x_in)
            for j in range(ET):
                mm = nc.tensor.transpose(PS[:, b if j < 4 else b4, j % 4 * P:j % 4 * P + P], ex[k][:, j, :], ident[:])
            t = PE.done(mm)
            yield
            L.free[b] = A.done(A.after(t).copy(exT[k][:, 0:512], bank(b)))
            t = L.free[b4] = A.done(A.after(t).copy(exT[k][:, 512:CAP], PS[:, b4, 0:CAP - 512]))
            passed(turned_x[k], t)
            yield
            PE.after(t, w1_in)
            A.after(w1_in)
            for n in range(4):
                for h in range(2):
                    b = L.bank()
                    at = slice(h * HALF, (h + 1) * HALF)
                    t = PE.done(PE.after(L.free.get(b)).matmul(PS[:, b, 0:HALF], ew1[k][:, n * P:(n + 1) * P], exT[k][:, at],
                                                               start=True, stop=True))
                    t = L.free[b] = A.done(A.after(t).activation(eh[k][:, n, at], PS[:, b, 0:HALF], ACT.Silu,
                                                                 bias=eb1[k][:, n:n + 1]))
            passed(used_w1[k], t)
            yield
            b4 = L.bank()
            PE.after(t, w2_in, L.free.get(b4))
            V.after(w2_in, YOUT[k].here())
            for j in range(ET):
                for f in range(4):
                    mm = nc.tensor.matmul(PS[:, L.out if j < 4 else b4, j % 4 * D:j % 4 * D + D],
                                          eh[k][:, f, j * P:(j + 1) * P], ew2[k][:, f, :], start=(f == 0), stop=(f == 3))
                if j == 3:
                    t = PE.done(mm)
            t4 = PE.done(mm)
            yield
            t = V.done(V.after(t).tensor_tensor(ey[k][:, 0:4], chunk(L.out), eb2[k][:].unsqueeze(1).broadcast_to([P, 4, D]), ALU.add))
            t = V.done(V.after(t4).tensor_tensor(ey[k][:, 4], PS[:, b4, 0:D], eb2[k][:], ALU.add))
            YOUT[k].plain(t)
            YOUT[k].done(nc.sync.dma_start(slots_y[ds(L.at * CAP, CAP)].rearrange("(j p) d -> p j d", p=P), ey[k][:]))
            return t

        in_lanes("experts1", expert1, turns=E // 2, width=1, lag=0)

        join()
        found = in_zone(0, [2, NT, D])
        PO.after(YOUT[0].here(), YOUT[1].here())
        for j in range(NT):
            for c in range(2):
                GATHER.done(nc.gpsimd.indirect_dma_start(
                    found[:, c, j, :], None, slots_y, bass.IndirectOffsetOnAxis(ap=gather_from[:, c, j:j + 1], axis=0),
                    bounds_check=SLOTS - 1, oob_is_err=False))

        def combine(L, t):
            V.after(GATHER.here())
            for c in range(2):
                t = V.done(V.after(t).tensor_tensor(
                    (L.x1, L.sq)[c][:], found[:, c, ds(L.at, CT), :],
                    share[:, c, ds(L.at, CT)].unsqueeze(2).broadcast_to([P, CT, D]), ALU.mult))
            t = V.done(V.after(t).tensor_tensor(L.tot[:], L.x1[:], L.sq[:], ALU.add))
            t = V.done(V.after(t).tensor_tensor(L.tot[:], L.tot[:], Y[:, ds(L.at, CT), :], ALU.add))
            t = yield from layer_norm(L, L.tot, L.Xc, t)
            return t

        w2qkv = load(LD[4], "w2qkv", [P, 3 * D], args["L2_attn_W_qkv"])
        w2p = load(LD[4], "w2p", [P, D], args["L2_attn_W_proj"])
        b2q = load(LD[4], "b2q", [P, 2], args["L2_attn_b_qk"])
        b2v = load(LD[4], "b2v", [P, D], args["L2_attn_b_v"].unsqueeze(0).broadcast_to([P, D]))
        b2p = load(LD[4], "b2p", [P, D], args["L2_attn_b_proj"].unsqueeze(0).broadcast_to([P, D]))
        V.after(LD[4].here())
        t = V.done(nc.vector.tensor_tensor(b2q[:, 0:1], b2q[:, 0:1], qscale2[:], ALU.mult))
        PE.after(LD[4].here())
        A.after(t, LD[4].here())
        in_lanes("combine1", combine, attention_prep(w2qkv[:, 0:D], w2qkv[:, D:2 * D], w2qkv[:, 2 * D:], qscale2[:, 0:1],
                                                      b2q[:, 0:1], b2q[:, 1:2], b2v[:]))
        join()
        constant_rows(True)
        attention("a2", diag_kq=bf["alibi_kq"], diag_qk=bf["alibi_qk"], lin=True,
                  slope=lambda g, r: float(2.0 ** (-0.5 * (g * R + r + 1))))

        NJ = 8
        win = load(LD[5], "win", [P, NJ * P], args["L2_ffn_Win"])
        binr = load(LD[5], "binr", [P, NJ], args["L2_ffn_bin_"])
        cw1 = load(LD[5], "cw1", [P, NJ], args["L2_ffn_W1"])
        cb1 = load(LD[5], "cb1", [P, NJ], args["L2_ffn_b1"])
        cw2 = load(LD[5], "cw2", [P, NJ], args["L2_ffn_W2"])
        cb2 = load(LD[5], "cb2", [64, 1], args["L2_ffn_b2"])
        wout = load(LD[5], "wout", [P, NJ, D], args["L2_ffn_Wout_rep"])
        wout1 = load(LD[5], "wout1", [64, D], args["L2_ffn_Wout"])
        bout = load(LD[5], "bout", [P, D], args["L2_ffn_bout"].unsqueeze(0).broadcast_to([P, D]))
        h8 = [in_zone(4096 * k, [NJ, S]) for k in range(2)]
        cb2w = sb("cb2w", [64, P])
        V.after(LD[5].here())
        t = V.done(nc.vector.tensor_tensor(binr[:], binr[:], cw1[:], ALU.mult))
        t = V.done(V.after(t).tensor_tensor(cb1[:], cb1[:], binr[:], ALU.add))
        t = V.done(nc.vector.tensor_tensor(wout[:], wout[:], cw2[:].unsqueeze(2).broadcast_to([P, NJ, D]), ALU.mult))
        t = V.done(V.after(t).tensor_copy(cb2w[:], cb2[:].broadcast_to([64, P])))
        t = PE.done(PE.after(t, LD[5].here()).matmul(PS[:, 6, 0:D], cb2w[:], wout1[:], start=True, stop=True))
        t = V.done(V.after(t).tensor_tensor(bout[:], bout[:], PS[:, 6, 0:D], ALU.add))
        V.after(t)
        A.after(t, LD[5].here())

        def channels(L, t):
            h = h8[L.k]
            t = A.done(A.plain(t).copy(L.xn[:], L.Xc))
            t = yield from transposed(L, t)
            yield
            PE.after(t)
            for n in range(NJ):
                b, t = product(L, win[:, n * P:(n + 1) * P], L.xT[:])
                t = L.free[b] = A.done(A.after(t).activation(h[:, n, :], bank(b), ACT.Relu,
                                                             scale=cw1[:, n:n + 1], bias=cb1[:, n:n + 1]))
            yield
            t = token_major(L, (t,), lambda f, j: h[:, f, j * P:(j + 1) * P], lambda f: wout[:, f, :], NJ)
            yield
            t = V.done(V.after(t).tensor_tensor(L.tot[:], chunk(L.out), L.Xc, ALU.add))
            t = V.done(V.after(t).tensor_tensor(L.tot[:], L.tot[:], bout[:].unsqueeze(1).broadcast_to([P, CT, D]), ALU.add))
            t = yield from layer_norm(L, L.tot, L.Xc, t)
            return t

        w3qkv = load(LD[6], "w3qkv", [P, 3 * D], args["L3_attn_w_qkv"])
        w3o = load(LD[6], "w3o", [P, D], args["L3_attn_w_out"])
        b3o = load(LD[6], "b3o", [P, D], args["L3_attn_b_out"].unsqueeze(0).broadcast_to([P, D]))
        tr3 = load(LD[6], "tr3", [P, 2], args["L3_attn_trace_tf"])
        vk3 = load(LD[6], "vk3", [HD, G * R], args["L3_attn_void_k"])
        vvb = sb("vvb", [P, G, P])
        t = V.done(V.after(V.here()).memset(vvb[:], 0.0))
        LD[7].plain(t)
        for g in range(G):
            for r in range(R):
                LD[7].done(nc.sync.dma_start(vvb[32 * r:32 * r + 1, g, 32 * r:32 * r + HD], args["L3_attn_void_v"][g * R + r:g * R + r + 1]))
                LD[7].done(nc.sync.dma_start(vvb[32 * r:32 * r + 1, g, 32 * r + HD:32 * r + HD + 1], args["c_ident"][0:1, 0:1]))
        V.after(LD[6].here())
        q3 = sb("q3", [P, 1])
        t = V.done(nc.vector.tensor_scalar(q3[:], tr3[:, 0:1], -1.0, None, ALU.mult))
        t = V.done(V.after(t).tensor_tensor(q3[:], q3[:], tr3[:, 0:1], ALU.max))
        t = V.done(V.after(t).tensor_tensor(q3[:], q3[:], tr3[:, 1:2], ALU.mult))
        t = V.done(V.after(t).tensor_scalar(q3[:], q3[:], 1.0, 1.0, ALU.add, ALU.max))
        t = V.done(V.after(t).reciprocal(q3[:], q3[:]))
        t_q3 = V.done(V.after(t).tensor_scalar(q3[:], q3[:], D ** -0.5, None, ALU.mult))
        vkp = sb("vkp", [HD, 3, G * R], BF16)
        vkr = sb("vkr", [HD, G * R])
        t = V.done(nc.vector.tensor_copy(vkp[:, 0], vk3[:]))
        t = V.done(V.after(t).tensor_tensor(vkr[:], vk3[:], vkp[:, 0], ALU.subtract))
        t = V.done(V.after(t).tensor_copy(vkp[:, 1], vkr[:]))
        t = V.done(V.after(t).tensor_tensor(vkp[:, 2], vkr[:], vkp[:, 1], ALU.subtract))
        vko = sb("vko", [96, G, R, 32], BF16)
        vkc = sb("vkc", [96, G * R], BF16)
        t2 = V.done(nc.vector.memset(vko[:], 0.0))
        t2 = V.done(nc.vector.memset(vkc[:], 1.0))
        LD[8].plain(t, t2)
        for i in range(3):
            u = LD[8].done(nc.sync.dma_start(vkc[24 * i:24 * i + 24, :], vkp[:]))
        t = V.done(V.after(u).tensor_copy(vko[:, :, :, 0:1], vkc[:].rearrange("p (g r o) -> p g r o", g=G, o=1)))
        pvo = sb("pvo", [P, S])
        PE.after(LD[6].here(), LD[7].here(), t)
        A.after(t_q3)
        V.after(t)
        in_lanes("layer2", attention_out(w2p[:], b2p[:]), channels,
                 attention_prep(w3qkv[:, 0:D], w3qkv[:, D:2 * D], w3qkv[:, 2 * D:], q3[:, 0:1]))
        join()
        constant_rows(False)
        attention("a3", void=(vko, vvb))

        rw3 = load(LD[7], "rw3", [P, E], args["L3_ffn_router_w"])
        lng = load(LD[7], "lng", [P, 2], args["L3_ffn_ln"])
        gu3 = w1
        dn3 = w2[:].rearrange("p e f d -> p (e f d)")[:, 0:E * 2 * D].rearrange("p (e f d) -> p e f d", e=E, f=2)
        LD[7].plain(PE.here())
        LD[7].done(nc.sync.dma_start(gu3[:], args["L3_ffn_gate_up_w"].rearrange("e d f -> d e f")))
        for e in range(E):
            LD[7].done(nc.sync.dma_start(dn3[:, e], args["L3_ffn_down_w"][e].rearrange("(f p) d -> p f d", p=P)))
        selr = sb("selr", [3 * E, E, P])
        LD[7].done(nc.sync.dma_start(selr[:], args["c_select"]))
        sel16 = sb("sel16", [3 * E, E, P], BF16)
        weights3 = sb("weights3", [P, NT, 3, E], BF16)
        turned_x3 = keep[:, VT + 2048:VT + 4096]
        turned_w3 = keep[0:3 * E, 0:B * S // 2].bitcast(BF16)
        xeT = [in_zone(1024 * k, [2, S]) for k in range(2)]
        gate = [in_zone(2048 + 1024 * k, [2, S]) for k in range(2)]
        PE.after(LD[7].here())
        A.after(LD[7].here())
        V.after(LD[7].here())


        sel_ready = V.done(V.after(V.here()).tensor_copy(sel16[:], selr[:]))
        PE.after(sel_ready)

        def route3(L, t):
            t = yield from layer_norm(L, L.Xc, L.xn, t)
            t_x = yield from transposed(L, t, scale=lng[:, 0:1], bias=lng[:, 1:2])
            t_keep = PO.done(PO.plain(t_x).tensor_copy(turned_x3[:, ds(L.at * P, S)], L.xT[:]))
            yield
            t, logits = router_logits(L, t_x, rw3)
            yield
            t = V.done(V.after(t).tensor_scalar(LG[:, ds(L.at, CT), :], logits, -10000.0, 10000.0, ALU.max, ALU.min))
            V.after(t_keep)
            return t

        in_lanes("route3", attention_out(w3o[:], b3o[:]), route3, lag=0)
        join()
        t = softmax(V.here(), 1e-8)
        t = V.done(V.after(t).tensor_scalar(LG[:], LG[:], 1e-8, 1.0, ALU.max, ALU.min))
        t = top2(t)
        t = V.done(V.after(t).tensor_tensor(M1[:], M1[:], M2[:], ALU.add))
        t = V.done(V.after(t).tensor_tensor(LG[:], LG[:], M1[:], ALU.mult))
        t = V.done(V.after(t).tensor_copy(weights3[:, :, 0], LG[:]))
        t = V.done(V.after(t).tensor_tensor(G2[:], LG[:], weights3[:, :, 0], ALU.subtract))
        t = V.done(V.after(t).tensor_copy(weights3[:, :, 1], G2[:]))
        t = V.done(V.after(t).tensor_tensor(weights3[:, :, 2], G2[:], weights3[:, :, 1], ALU.subtract))
        PE.after(t)
        for h in range(2):
            turned = PS[0:3 * E, h, :].bitcast(BF16)
            for j in range(NT // 2):
                mm = nc.tensor.transpose(turned[:, j * P:(j + 1) * P],
                                         weights3[:, h * NT // 2 + j].rearrange("p i e -> p (i e)"), bf["ident"][:])
            t = PE.done(mm)
            t = A.done(A.after(t).copy(turned_w3[:, h * 2 * S:(h + 1) * 2 * S], turned))

        def experts3(L, t):
            t_m = t_dn = None
            PE.after(L.finished.here())
            for e in range(E):
                b = L.bank()
                PE.plain(L.free.get(b))
                u = PE.done(nc.tensor.matmul(bank(b), sel16[:, e, :], turned_w3[:, ds(L.at * P, S)], start=True, stop=True))
                x = xeT[L.k][:, e % 2, :]
                t = L.free[b] = V.done(V.after(u, t_m).tensor_tensor(
                    x, bank(b), turned_x3[:, ds(L.at * P, S)], ALU.mult))
                yield
                PE.after(t)
                t_g = {}
                for n in (0, 2, 1, 3):
                    b, u = product(L, gu3[:, e, n * P:(n + 1) * P], x)
                    if n < 2:
                        t_g[n] = L.free[b] = A.done(A.after(u, t_m).activation(gate[L.k][:, n, :], bank(b), ACT.Silu))
                    else:
                        t = L.free[b] = V.done(V.after(u, t_g[n - 2], t_dn).tensor_tensor(
                            L.hT[:, n - 2, :], bank(b), gate[L.k][:, n - 2, :], ALU.mult))
                t_m = t
                yield
                PE.after(t)
                for f in range(2):
                    for j in range(CT):
                        mm = nc.tensor.matmul(PS[:, L.out, j * D:(j + 1) * D], L.hT[:, f, j * P:(j + 1) * P], dn3[:, e, f, :],
                                              start=(e == 0 and f == 0 and j == 0), stop=True, skip_group_check=True)
                t_dn = PE.done(mm)
            yield
            t = V.done(V.after(t_dn).scalar_tensor_tensor(L.tot[:], L.Xc, 2.0, chunk(L.out), ALU.mult, ALU.add))
            t = yield from layer_norm(L, L.tot, L.Xc, t)
            OUT.plain(t)
            OUT.done(nc.sync.dma_start(out_tiles[:, ds(L.at, CT), :], L.Xc))
            return t

        out_tiles = out.rearrange("b (j p) d -> p (b j) d", p=P)
        in_lanes("experts3", experts3, lag=0)

        nc.sync.wait_ge(OUT.sem, OUT.here().value())


def layout(x):
    f = np.float32
    a = {k: np.ascontiguousarray(v) for k, v in x.items()}
    o = {"x": a["L0_attn_x"]}
    for n in ("L0_attn_in_proj_w", "L0_attn_out_proj_w", "L0_attn_fc_w", "L0_attn_proj_w", "L0_ffn_w_up", "L0_ffn_w_down"):
        o[n] = np.ascontiguousarray(a[n].T)
    for n in ("L0_attn_norm1_w", "L0_attn_norm2_w"):
        o[n] = a[n].reshape(D, 1)
    perm = np.arange(D).reshape(G, R, HD).transpose(0, 2, 1).reshape(-1)
    for n in ("q_heads", "k_heads"):
        o["L1_attn_" + n] = np.ascontiguousarray(a["L1_attn_" + n].T[:, perm])
    for n in ("v_heads", "output_proj"):
        o["L1_attn_" + n] = np.ascontiguousarray(a["L1_attn_" + n].T)
    for n in ("router_w", "w1", "w2", "b2", "sw1", "sw2", "sb2"):
        o["L1_ffn_" + n] = a["L1_ffn_" + n]
    o["L1_ffn_b1"] = np.ascontiguousarray(a["L1_ffn_b1"].reshape(E, 4, P).transpose(0, 2, 1))
    o["L1_ffn_sb1"] = np.ascontiguousarray(a["L1_ffn_sb1"].reshape(4, P).T)
    w, b = a["L2_attn_W_qkv"], a["L2_attn_b_qkv"]
    o["L2_attn_W_qkv"] = np.ascontiguousarray(np.concatenate([w[:, 0:D][:, perm], w[:, D:2 * D][:, perm], w[:, 2 * D:]], 1))
    o["L2_attn_b_qk"] = np.ascontiguousarray(np.stack([b[0:D][perm], b[D:2 * D][perm]], 1))
    o["L2_attn_b_v"] = np.ascontiguousarray(b[2 * D:])
    o["L2_attn_W_proj"], o["L2_attn_b_proj"] = a["L2_attn_W_proj"], a["L2_attn_b_proj"]
    per = lambda v: np.ascontiguousarray(v.reshape(8, P).T)
    o["L2_ffn_Win"] = np.repeat(a["L2_ffn_Win"], 16, axis=1)
    o["L2_ffn_bin_"] = per(np.repeat(a["L2_ffn_bin_"], 16))
    for n in ("W1", "b1", "W2"):
        o["L2_ffn_" + n] = per(a["L2_ffn_" + n])
    o["L2_ffn_b2"] = a["L2_ffn_b2"].reshape(64, 1)
    o["L2_ffn_Wout"] = a["L2_ffn_Wout"]
    o["L2_ffn_Wout_rep"] = np.ascontiguousarray(np.repeat(a["L2_ffn_Wout"], 16, axis=0).reshape(8, P, D).transpose(1, 0, 2))
    o["L2_ffn_bout"] = a["L2_ffn_bout"]
    w = a["L3_attn_w_qkv"]
    o["L3_attn_w_qkv"] = np.ascontiguousarray(np.concatenate([w[:, 0:D][:, perm], w[:, D:2 * D][:, perm], w[:, 2 * D:]], 1))
    o["L3_attn_w_out"], o["L3_attn_b_out"] = a["L3_attn_w_out"], a["L3_attn_b_out"]
    head = perm // HD
    o["L3_attn_trace_tf"] = np.ascontiguousarray(np.stack(
        [a["L3_attn_attention_trace"].reshape(H)[head], a["L3_attn_temperature_factor"].reshape(H)[head]], 1))
    o["L3_attn_void_k"] = np.ascontiguousarray(a["L3_attn_void_k"].reshape(H, HD).T)
    o["L3_attn_void_v"] = a["L3_attn_void_v"].reshape(H, HD)
    o["L3_ffn_router_w"] = np.ascontiguousarray(a["L3_ffn_router_w"].T)
    o["L3_ffn_ln"] = np.ascontiguousarray(np.stack([a["L3_ffn_ln_gamma"], a["L3_ffn_ln_beta"]], 1))
    o["L3_ffn_gate_up_w"] = np.ascontiguousarray(a["L3_ffn_gate_up_w"].transpose(0, 2, 1))
    o["L3_ffn_down_w"] = np.ascontiguousarray(a["L3_ffn_down_w"].transpose(0, 2, 1))
    i = np.arange(P)
    o["c_select"] = np.ascontiguousarray(np.repeat(np.tile(np.eye(E, dtype=f), (3, 1))[:, :, None], P, axis=2))
    k, q = i[:, None], i[None, :]
    o["c_ident"] = np.eye(P, dtype=f)
    o["c_causal_kq"] = np.where(k > q, NEG, 0).astype(f)
    o["c_causal_qk"] = np.ascontiguousarray(o["c_causal_kq"].T)
    o["c_alibi_kq"] = np.minimum(k - q, 0).astype(f)
    o["c_alibi_qk"] = np.ascontiguousarray(o["c_alibi_kq"].T)
    o["c_headmean"] = np.where(k // HD == q // HD, 1.0 / HD, 0).astype(f)
    o["c_tri"] = (k < q).astype(f)
    o["c_rank"] = np.tile(E - np.arange(E), (P, 1)).astype(f)
    slope = 2.0 ** (-0.5 * (np.arange(H) + 1))
    o["c_slopes"] = np.tile(slope, (P, 1)).astype(f)
    o["c_qscale2"] = (HD ** -0.5 / slope[perm // HD]).reshape(D, 1).astype(f)
    pos = np.arange(S)
    rk, rq = np.zeros((NLIN + 2, S), f), np.zeros((NLIN + 2, S), f)
    for s in range(3):
        own, behind = pos // P == s, pos // P > s
        rk[3 * s][own], rk[3 * s + 1][own], rk[3 * s + 2][own] = pos[own] % P, 1, 1
        rq[3 * s][behind], rq[3 * s + 1][behind] = 1, -(pos[behind] % P)
        rq[3 * s + 2][behind] = -P * (pos[behind] // P - s)
    rk[NLIN:] = 1
    o["c_rows_k"], o["c_rows_q"] = rk, rq
    return o


def kernel(**inputs):
    import concourse.bacc as bacc
    from concourse.bass_utils import run_bass_kernel_spmd

    nc = bacc.Bacc("TRN2", target_bir_lowering=False, num_devices=1)
    arrays, args = {}, {}
    for name, a in layout(inputs).items():
        arrays["in_" + name] = a
        args[name] = nc.dram_tensor("in_" + name, a.shape, mybir.dt.from_np(a.dtype), kind="ExternalInput").ap()
    out = nc.dram_tensor("out_0", (B, S, D), F32, kind="ExternalOutput").ap()
    build_program(nc, args, out)
    r = run_bass_kernel_spmd(nc, [arrays], core_ids=[0])
    return r.results[0]["out_0"]
```
